# Optimizing a Trainium2 kernel written in Bass

```python
import numpy as np
import jax
import jax.numpy as jnp

def _softmax(x, axis=-1):
    return jax.nn.softmax(x, axis=axis)

def _gelu(x):
    return jax.nn.gelu(x, approximate=True)

def _silu(x):
    return jax.nn.silu(x)

def _sigmoid(x):
    return jax.nn.sigmoid(x)

def _layernorm(x, axis=-1, eps=1e-05):
    m = jnp.mean(x, axis=axis, keepdims=True)
    v = jnp.var(x, axis=axis, keepdims=True)
    return (x - m) / jnp.sqrt(v + eps)

def _scatter_add(tgt, idx, src, axis=0):
    return tgt.at[idx].add(src)

def _segment_sum(src, seg, n):
    return jax.ops.segment_sum(src, seg, n)
kernel_name = 'mk_gnn_preln_d4_gnn_r32_b6d6f2'

def setup_inputs(seed: int=0):
    np.random.seed(seed)
    _w = jnp.asarray

    def _rec_inputs():
        import jax
        import jax.numpy as jnp
        _gk = jax.random.key(seed)
        x = -0.0003713 + 1 * jax.random.normal(jax.random.fold_in(_gk, 1), (3125, 128), jnp.float32)
        _s = jax.random.randint(jax.random.fold_in(_gk, 2), (25000,), 0, 3125, jnp.int32)
        _d = jax.random.randint(jax.random.fold_in(_gk, 3), (25000,), 0, 3125, jnp.int32)
        _loop = jnp.arange(3125, dtype=jnp.int32)
        src = jnp.concatenate([_s, _d, _loop])
        dst = jnp.concatenate([_d, _s, _loop])
        _o = jnp.argsort(dst, stable=True)
        src = src[_o]
        dst = dst[_o]
        edge_weight = jax.random.uniform(jax.random.fold_in(_gk, 13), (53125,), jnp.float32, 0.0, 1)
        return (x, src, dst, edge_weight)
    x, src, dst, edge_weight = _rec_inputs()

    def _L0_gnn_setup():
        import jax, jax.numpy as jnp
        import numpy as np
        N = 3125
        E = 50000
        IN_F = 128
        OUT_F = 128
        EPS = 1e-12
        key = jax.random.key(seed)
        k1, k2, k3, k4, k5, k6 = jax.random.split(key, 6)
        x = jax.random.normal(k1, (N, IN_F), dtype=jnp.float32)
        rows = jnp.sort(jax.random.randint(k2, (E,), 0, N, dtype=jnp.int32))
        cols = jax.random.randint(k3, (E,), 0, N, dtype=jnp.int32)
        vals = jax.random.uniform(k4, (E,), dtype=jnp.float32)
        bound = 1.0 / np.sqrt(2 * IN_F)
        W = jax.random.uniform(k5, (OUT_F, 2 * IN_F), dtype=jnp.float32, minval=-bound, maxval=bound)
        b = jax.random.uniform(k6, (OUT_F,), dtype=jnp.float32, minval=-bound, maxval=bound)
        return {'x': x, 'rows': rows, 'cols': cols, 'vals': vals, 'W': W, 'b': b}
    _L0_gnn_all = _L0_gnn_setup()
    _L0_gnn_in = {k: v for k, v in _L0_gnn_all.items() if k in ('W', 'b')}
    del _L0_gnn_all

    def _L1_gnn_setup():
        import jax, jax.numpy as jnp
        import numpy as np
        N = 3125
        E = 25000
        D = 128
        key = jax.random.key(seed)
        ks = jax.random.split(key, 12)
        s = lambda fan_in: 1.0 / np.sqrt(fan_in)
        return {'h': jax.random.normal(ks[0], (N, D), dtype=jnp.float32), 'w': jax.random.uniform(ks[1], (E,), dtype=jnp.float32), 'src': jax.random.randint(ks[2], (E,), 0, N, dtype=jnp.int32), 'dst': jax.random.randint(ks[3], (E,), 0, N, dtype=jnp.int32), 'W1': jax.random.uniform(ks[4], (2 * D + 1, D), jnp.float32, -s(2 * D + 1), s(2 * D + 1)), 'b1': jnp.zeros((D,), jnp.float32), 'W2': jax.random.uniform(ks[5], (D, D), jnp.float32, -s(D), s(D)), 'b2': jnp.zeros((D,), jnp.float32), 'U1': jax.random.uniform(ks[6], (2 * D, D), jnp.float32, -s(2 * D), s(2 * D)), 'c1': jnp.zeros((D,), jnp.float32), 'U2': jax.random.uniform(ks[7], (D, D), jnp.float32, -s(D), s(D)), 'c2': jnp.zeros((D,), jnp.float32)}
    _L1_gnn_all = _L1_gnn_setup()
    _L1_gnn_in = {k: v for k, v in _L1_gnn_all.items() if k in ('W1', 'b1', 'W2', 'b2', 'U1', 'c1', 'U2', 'c2')}
    del _L1_gnn_all

    def _L2_gnn_setup():
        import jax, jax.numpy as jnp
        import numpy as np
        N_NODES = 50000
        NEG_SLOPE = 0.2
        EPS = 1e-16

        def gat_conv(x, W, att_src, att_dst, bias, src, dst, heads, out_ch, n):
            xw = (x @ W).reshape(n, heads, out_ch)
            a_src = jnp.einsum('nhc,hc->nh', xw, att_src)
            a_dst = jnp.einsum('nhc,hc->nh', xw, att_dst)
            alpha = jax.nn.leaky_relu(a_src[src] + a_dst[dst], NEG_SLOPE)
            amax = jax.ops.segment_max(alpha, dst, num_segments=n)
            ex = jnp.exp(alpha - amax[dst])
            denom = jax.ops.segment_sum(ex, dst, num_segments=n)
            coef = ex / (denom[dst] + EPS)
            msg = coef[:, :, None] * xw[src]
            out = jax.ops.segment_sum(msg, dst, num_segments=n)
            return out.reshape(n, heads * out_ch) + bias
        key = jax.random.key(seed)
        ks = jax.random.split(key, 12)
        n, fin, hid, out_dim, heads = (N_NODES, 128, 128, 128, 2)
        E = 25000
        sc = lambda *s: 1.0 / np.sqrt(s[0])
        return {'x': jax.random.normal(ks[0], (n, fin), jnp.float32), 'edge_index': jax.random.randint(ks[1], (2, E), 0, n, jnp.int64), 'W_emb': jax.random.normal(ks[2], (fin, out_dim), jnp.float32) * sc(fin), 'b_emb': jnp.zeros((out_dim,), jnp.float32), 'W1': jax.random.normal(ks[3], (out_dim, heads * hid), jnp.float32) * sc(out_dim), 'att_src1': jax.random.normal(ks[4], (heads, hid), jnp.float32) * sc(hid), 'att_dst1': jax.random.normal(ks[5], (heads, hid), jnp.float32) * sc(hid), 'b1': jnp.zeros((heads * hid,), jnp.float32), 'W2': jax.random.normal(ks[6], (heads * hid, out_dim), jnp.float32) * sc(heads * hid), 'att_src2': jax.random.normal(ks[7], (1, out_dim), jnp.float32) * sc(out_dim), 'att_dst2': jax.random.normal(ks[8], (1, out_dim), jnp.float32) * sc(out_dim), 'b2': jnp.zeros((out_dim,), jnp.float32)}
    _L2_gnn_all = _L2_gnn_setup()
    _L2_gnn_in = {k: v for k, v in _L2_gnn_all.items() if k in ('W_emb', 'b_emb', 'W1', 'att_src1', 'att_dst1', 'b1', 'W2', 'att_src2', 'att_dst2', 'b2')}
    del _L2_gnn_all

    def _L3_gnn_setup():
        import jax, jax.numpy as jnp
        import numpy as np

        def _sage_conv(h, src, dst, n_nodes, Wl, bl, Wr):
            msg_sum = jax.ops.segment_sum(h[src], dst, num_segments=n_nodes)
            cnt = jax.ops.segment_sum(jnp.ones((src.shape[0], 1), h.dtype), dst, num_segments=n_nodes)
            agg = msg_sum / jnp.maximum(cnt, 1.0)
            return agg @ Wl + bl + h @ Wr
        key = jax.random.key(seed)
        ks = jax.random.split(key, 8)
        N, E, D, H = (50000, 25000, 128, 128)
        x = jax.random.normal(ks[0], (N, D), dtype=jnp.float32)
        edge_index = jax.random.randint(ks[1], (2, E), 0, N, dtype=jnp.int64)
        s = 0.1
        return {'x': x, 'edge_index': edge_index, 'Wl1': jax.random.normal(ks[2], (D, H), dtype=jnp.float32) * s, 'bl1': jnp.zeros((H,), dtype=jnp.float32), 'Wr1': jax.random.normal(ks[3], (D, H), dtype=jnp.float32) * s, 'Wl2': jax.random.normal(ks[4], (H, H), dtype=jnp.float32) * s, 'bl2': jnp.zeros((H,), dtype=jnp.float32), 'Wr2': jax.random.normal(ks[5], (H, H), dtype=jnp.float32) * s}
    _L3_gnn_all = _L3_gnn_setup()
    _L3_gnn_in = {k: v for k, v in _L3_gnn_all.items() if k in ('Wl1', 'bl1', 'Wr1', 'Wl2', 'bl2', 'Wr2')}
    del _L3_gnn_all
    return {'x': x, 'src': src, 'dst': dst, 'edge_weight': edge_weight, 'L0_gnn_W': _L0_gnn_in['W'], 'L0_gnn_b': _L0_gnn_in['b'], 'L1_gnn_W1': _L1_gnn_in['W1'], 'L1_gnn_b1': _L1_gnn_in['b1'], 'L1_gnn_W2': _L1_gnn_in['W2'], 'L1_gnn_b2': _L1_gnn_in['b2'], 'L1_gnn_U1': _L1_gnn_in['U1'], 'L1_gnn_c1': _L1_gnn_in['c1'], 'L1_gnn_U2': _L1_gnn_in['U2'], 'L1_gnn_c2': _L1_gnn_in['c2'], 'L2_gnn_W_emb': _L2_gnn_in['W_emb'], 'L2_gnn_b_emb': _L2_gnn_in['b_emb'], 'L2_gnn_W1': _L2_gnn_in['W1'], 'L2_gnn_att_src1': _L2_gnn_in['att_src1'], 'L2_gnn_att_dst1': _L2_gnn_in['att_dst1'], 'L2_gnn_b1': _L2_gnn_in['b1'], 'L2_gnn_W2': _L2_gnn_in['W2'], 'L2_gnn_att_src2': _L2_gnn_in['att_src2'], 'L2_gnn_att_dst2': _L2_gnn_in['att_dst2'], 'L2_gnn_b2': _L2_gnn_in['b2'], 'L3_gnn_Wl1': _L3_gnn_in['Wl1'], 'L3_gnn_bl1': _L3_gnn_in['bl1'], 'L3_gnn_Wr1': _L3_gnn_in['Wr1'], 'L3_gnn_Wl2': _L3_gnn_in['Wl2'], 'L3_gnn_bl2': _L3_gnn_in['bl2'], 'L3_gnn_Wr2': _L3_gnn_in['Wr2']}

def reference(x, src, dst, edge_weight, L0_gnn_W, L0_gnn_b, L1_gnn_W1, L1_gnn_b1, L1_gnn_W2, L1_gnn_b2, L1_gnn_U1, L1_gnn_c1, L1_gnn_U2, L1_gnn_c2, L2_gnn_W_emb, L2_gnn_b_emb, L2_gnn_W1, L2_gnn_att_src1, L2_gnn_att_dst1, L2_gnn_b1, L2_gnn_W2, L2_gnn_att_src2, L2_gnn_att_dst2, L2_gnn_b2, L3_gnn_Wl1, L3_gnn_bl1, L3_gnn_Wr1, L3_gnn_Wl2, L3_gnn_bl2, L3_gnn_Wr2):
    import jax
    import jax.numpy as jnp

    def _L0_gnn_ref(x, rows, cols, vals, W, b):
        import jax, jax.numpy as jnp
        import numpy as np
        N = 3125
        E = 50000
        IN_F = 128
        OUT_F = 128
        EPS = 1e-12
        gathered = vals[:, None] * x[cols]
        neighbor = jax.ops.segment_sum(gathered, rows, num_segments=N)
        combined = jnp.concatenate([x, neighbor], axis=1)
        out = combined @ W.T + b
        norm = jnp.sqrt(jnp.sum(out * out, axis=1, keepdims=True))
        return out / jnp.maximum(norm, EPS)

    def _L1_gnn_ref(h, w, src, dst, W1, b1, W2, b2, U1, c1, U2, c2):
        import jax, jax.numpy as jnp
        import numpy as np
        N = 3125
        E = 25000
        D = 128
        n = h.shape[0]
        msg_in = jnp.concatenate([h[src], h[dst], w[:, None]], axis=1)
        msg = jax.nn.relu(msg_in @ W1 + b1) @ W2 + b2
        agg = jax.ops.segment_max(msg, dst, num_segments=n)
        deg = jax.ops.segment_sum(jnp.ones((dst.shape[0],), jnp.int32), dst, num_segments=n)
        agg = jnp.where((deg > 0)[:, None], agg, jnp.zeros((), h.dtype))
        upd_in = jnp.concatenate([h, agg], axis=1)
        return jax.nn.relu(upd_in @ U1 + c1) @ U2 + c2

    def _L2_gnn_ref(x, edge_index, W_emb, b_emb, W1, att_src1, att_dst1, b1, W2, att_src2, att_dst2, b2):
        import jax, jax.numpy as jnp
        import numpy as np
        N_NODES = 50000
        NEG_SLOPE = 0.2
        EPS = 1e-16

        def gat_conv(x, W, att_src, att_dst, bias, src, dst, heads, out_ch, n):
            xw = (x @ W).reshape(n, heads, out_ch)
            a_src = jnp.einsum('nhc,hc->nh', xw, att_src)
            a_dst = jnp.einsum('nhc,hc->nh', xw, att_dst)
            alpha = jax.nn.leaky_relu(a_src[src] + a_dst[dst], NEG_SLOPE)
            amax = jax.ops.segment_max(alpha, dst, num_segments=n)
            ex = jnp.exp(alpha - amax[dst])
            denom = jax.ops.segment_sum(ex, dst, num_segments=n)
            coef = ex / (denom[dst] + EPS)
            msg = coef[:, :, None] * xw[src]
            out = jax.ops.segment_sum(msg, dst, num_segments=n)
            return out.reshape(n, heads * out_ch) + bias
        n = x.shape[0]
        loop = jnp.arange(n, dtype=edge_index.dtype)
        src = jnp.concatenate([edge_index[0], loop])
        dst = jnp.concatenate([edge_index[1], loop])
        h = x @ W_emb + b_emb
        h = gat_conv(h, W1, att_src1, att_dst1, b1, src, dst, heads=2, out_ch=128, n=n)
        h = jax.nn.elu(h)
        h = gat_conv(h, W2, att_src2, att_dst2, b2, src, dst, heads=1, out_ch=128, n=n)
        return h

    def _L3_gnn_ref(x, edge_index, Wl1, bl1, Wr1, Wl2, bl2, Wr2):
        import jax, jax.numpy as jnp
        import numpy as np

        def _sage_conv(h, src, dst, n_nodes, Wl, bl, Wr):
            msg_sum = jax.ops.segment_sum(h[src], dst, num_segments=n_nodes)
            cnt = jax.ops.segment_sum(jnp.ones((src.shape[0], 1), h.dtype), dst, num_segments=n_nodes)
            agg = msg_sum / jnp.maximum(cnt, 1.0)
            return agg @ Wl + bl + h @ Wr
        n_nodes = x.shape[0]
        src, dst = (edge_index[0], edge_index[1])
        h = jax.nn.relu(_sage_conv(x, src, dst, n_nodes, Wl1, bl1, Wr1))
        h = jax.nn.relu(_sage_conv(h, src, dst, n_nodes, Wl2, bl2, Wr2))
        return h
    edge_index = jnp.stack([src, dst])
    h = jnp.maximum(_layernorm(x, axis=-1), 0.0)
    x = x + _L0_gnn_ref(h, src, dst, edge_weight, L0_gnn_W, L0_gnn_b)
    h = jnp.maximum(_layernorm(x, axis=-1), 0.0)
    x = x + _L1_gnn_ref(h, edge_weight, src, dst, L1_gnn_W1, L1_gnn_b1, L1_gnn_W2, L1_gnn_b2, L1_gnn_U1, L1_gnn_c1, L1_gnn_U2, L1_gnn_c2)
    h = jnp.maximum(_layernorm(x, axis=-1), 0.0)
    x = x + _L2_gnn_ref(h, edge_index, L2_gnn_W_emb, L2_gnn_b_emb, L2_gnn_W1, L2_gnn_att_src1, L2_gnn_att_dst1, L2_gnn_b1, L2_gnn_W2, L2_gnn_att_src2, L2_gnn_att_dst2, L2_gnn_b2)
    h = jnp.maximum(_layernorm(x, axis=-1), 0.0)
    x = x + _L3_gnn_ref(h, edge_index, L3_gnn_Wl1, L3_gnn_bl1, L3_gnn_Wr1, L3_gnn_Wl2, L3_gnn_bl2, L3_gnn_Wr2)
    return x

_drawn_inputs = setup_inputs


def setup_inputs(seed=0):
    import zlib

    import numpy as np

    out = dict(_drawn_inputs(seed))
    spreads = {'L1_gnn_b1': (0.0, 0.8),
     'L1_gnn_b2': (0.0, 0.434),
     'L1_gnn_c1': (0.0, 0.1),
     'L1_gnn_c2': (0.0, 0.1),
     'L2_gnn_b_emb': (0.0, 0.1),
     'L2_gnn_b1': (0.0, 0.1),
     'L2_gnn_b2': (0.0, 0.1),
     'L3_gnn_bl1': (0.0, 0.1),
     'L3_gnn_bl2': (0.0, 0.1)}
    factors = {'edge_weight': 13.879,
     'L0_gnn_b': 200.0,
     'L1_gnn_W1': 3.373,
     'L2_gnn_att_dst1': 170.965,
     'L2_gnn_att_src2': 8.0,
     'L2_gnn_att_dst2': 111.62}
    for name, (base, spread) in spreads.items():
        noise = np.random.default_rng([zlib.crc32(name.encode()), seed]).standard_normal(out[name].shape)
        drawn = base * np.exp(spread * noise) if base else spread * noise
        out[name] = jnp.asarray(drawn.astype(out[name].dtype))
    for name, factor in factors.items():
        out[name] = (out[name] * factor).astype(out[name].dtype)
    return out
```

```python
from contextlib import ExitStack

import numpy as np
import concourse.bass as bass
from concourse import mybir

N, D, E = 3125, 128, 53125
P = 125
W = N // P
EDGES = 128
TILES = -(-E // EDGES)
STEPS = TILES + W - 1
SK, SJ = 110, 4
Q = 20
QW = -(-N // Q)
NP = QW * Q
CSTEPS = TILES + QW - 1
CK, CJ = 52, 11
GCN_ROUNDS, GCN_STEPS, CNT_PER_ROUND = 44, 10, 13
TABLES = 5
GE = TABLES * EDGES
MSG_ROUNDS, MSG_SLOTS, HALF = 55, 8, 4
SUM_BANKS = (1, 2, 3, 6)
GROUP = 5
GROUPS = W // GROUP
GC = GROUP * P
KEEP = 12
BIG = 3.0e38
SLOPE = 0.2
assert SK * SJ == STEPS == GCN_ROUNDS * GCN_STEPS == MSG_ROUNDS * MSG_SLOTS
assert CK * CJ == CSTEPS == GCN_ROUNDS * CNT_PER_ROUND and W * Q <= 512 and GCN_STEPS == 2 * TABLES

f32, i32, f16, bf16 = mybir.dt.float32, mybir.dt.int32, mybir.dt.float16, mybir.dt.bfloat16
ALU = mybir.AluOpType
ACT = mybir.ActivationFunctionType
AX = mybir.AxisListType
RMAX = bass.bass_isa.ReduceOp.max

STAGES = (("steps", SJ), ("counts", CJ),
          ("gcn_hT", GROUPS), ("gcn_aT", GROUPS), ("gcn_out", GROUPS),
          ("msg_hT", GROUPS), ("msg_P", GROUPS), ("msg_Q", GROUPS),
          ("msg_aT", GROUPS), ("msg_u", GROUPS), ("msg_out", GROUPS),
          ("gat_hT", GROUPS), ("gat_emb", GROUPS), ("gat_eT", GROUPS), ("gat_x0", GROUPS), ("gat_x1", GROUPS),
          ("rows0", 1), ("rows1", 1),
          ("gat_o0T", GROUPS), ("gat_o1T", GROUPS), ("gat_x2", GROUPS), ("rows2", 1),
          ("sage1_aT", GROUPS), ("sage1_hT", GROUPS), ("sage1_out", GROUPS),
          ("sage2_aT", GROUPS), ("sage2_hT", GROUPS), ("sage2_out", GROUPS))


def before(stage):
    n = 0
    for name, rounds in STAGES:
        if name == stage:
            return n
        n += rounds
    raise KeyError(stage)


def after(stage):
    return before(stage) + dict(STAGES)[stage]


def gnn(nc, a, out):
    ctx = ExitStack()
    with ctx:
        def sb(name, shape, dt=f32):
            return ctx.enter_context(nc.sbuf_tensor(name, shape, dt))

        sems = {}

        def sig(name):
            if name not in sems:
                sems[name] = ctx.enter_context(nc.semaphore(name))
            return sems[name]

        def dram(name, shape, dt=f32):
            return nc.dram_tensor(name, shape, dt).ap()

        win_d, cwin_d = dram("win_d", [STEPS], i32), dram("cwin_d", [CSTEPS], i32)
        dl_d, pen_d, w_d, src_d = (dram(n, [STEPS, EDGES]) for n in ("dl_d", "pen_d", "w_d", "src_d"))
        sum_d = [dram(f"sum{n}_d", [N + EDGES, D]) for n in range(TABLES)]
        x_d = dram("x_d", [N, D])
        h0_d, p_d = dram("h0_d", [N, D]), dram("p_d", [N, D])
        h3_d, g3_d = dram("h3_d", [N, D]), dram("g3_d", [N, D])
        xw_d = [dram(f"xw{n}_d", [N, D]) for n in range(2)]
        o_d = [dram(f"o{n}_d", [N, D]) for n in range(3)]
        rows_d = [dram(f"rows{n}_d", [2, N]) for n in range(3)]
        agg_d = [dram(f"agg{n}_d", [N, D]) for n in range(2)]
        k_d = dram("k_d", [P, (W - KEEP) * NP], f16)

        def nodes(ap):
            return ap.rearrange("(w p) d -> p w d", p=P)

        K = sb("K", [128, W, NP], f16)
        U = sb("U", [128, 11100])
        ident = sb("ident", [128, 128])
        ramp = sb("ramp", [128, 128])
        keys = sb("keys", [128, W * Q], f16)
        pidx = sb("pidx", [128, 1])
        wts = sb("wts", [128, 8, D])
        bias = sb("bias", [128, 9, D])
        bcol = sb("bcol", [128, 2])
        scal = sb("scal", [128, 16])
        carry = sb("carry", [128, 1])
        index = sb("index", [128, GCN_STEPS], i32)
        rowv_all = sb("rowv", [128, 4 * W])
        rowv = rowv_all[0:P].rearrange("p (a w) -> p a w", a=4)
        KA = K[:, KEEP:, :].rearrange("p b d -> p (b d)").bitcast(f32)

        def carve(arena, words):
            at = [0]

            def take(*shape, dt=f32):
                size = int(np.prod(shape))
                need = size if dt in (f32, i32) else -(-size // 2)
                assert at[0] + need <= words, (at[0], need, words)
                v = arena[:, at[0]:at[0] + need]
                at[0] += need
                if dt is not f32:
                    v = v.bitcast(dt)[:, 0:size]
                if len(shape) == 2:
                    v = v.rearrange("p (a b) -> p a b", a=shape[0])
                elif len(shape) == 3:
                    v = v.rearrange("p (a b c) -> p a b c", a=shape[0], b=shape[1])
                return v
            return take

        UWORDS, KWORDS = 11100, (W - KEEP) * NP // 2
        take = carve(U, UWORDS)
        SRC = take(STEPS, dt=i32)
        LAST = take(STEPS)
        IK, CIK = take(STEPS, dt=i32), take(CSTEPS, dt=i32)
        SRCF = take(STEPS)
        WT = take(STEPS)
        KEY, SLO = take(CSTEPS, dt=f16), take(CSTEPS, dt=f16)
        HN = take(W, D)
        dst_hot = [take(GE) for _ in range(2)]
        src_row = [take(GE) for _ in range(2)]
        rows = take(TABLES, D)
        khot, slohot = take(2, W * Q, dt=f16), take(2, 128, dt=f16)
        cnt = take(2, W * Q, dt=f16)
        take = carve(U, UWORDS)
        take(3 * STEPS + CSTEPS)
        macc = take(W, D + 1)
        MG = take(MSG_SLOTS, D)
        lasthot = take(MSG_SLOTS, P)
        Qc = take(MSG_SLOTS, D)
        take = carve(wts[:, :, :].rearrange("p a b -> p (a b)"), 8 * D)
        same = take(TABLES, EDGES)
        picked = take(2, D)
        earlier = take(EDGES)
        take = carve(rowv_all, 4 * W)
        take(2 * W)
        again, spare = take(TABLES), take(1)
        take = carve(KA, KWORDS)
        X, H, Y, T, HT, QU = (take(W * D) for _ in range(6))
        w3 = lambda v: v.rearrange("p (w d) -> p w d", w=W)
        mrhs = [Y[:, n * 512:(n + 1) * 512] for n in range(2)]
        dlb = [Y[:, (2 + n) * 512:(3 + n) * 512] for n in range(2)]
        penb = [Y[:, (4 + n) * 512:(5 + n) * 512] for n in range(2)]
        relu, scan = T[:, 0:512], T[:, 512:1024]
        back = T[:, 1024:1024 + HALF * (D + 1)].rearrange("p (s c) -> p s c", s=HALF)
        take = carve(KA, KWORDS)
        st_i = take(SJ, 4 * EDGES, dt=i32)
        st_w = take(SJ, EDGES)
        st_f = [take(SJ, EDGES) for _ in range(4)]
        ct_i = take(CJ, 2 * EDGES, dt=i32)
        ct_f = [take(CJ, EDGES) for _ in range(5)]
        ct_q = take(CJ, EDGES, dt=i32)
        tl_i = take(TILES, dt=i32)
        tl_f = [take(TILES) for _ in range(5)]
        tl_q = take(TILES, dt=i32)
        stp = take(SJ, 6)
        ctp = take(CJ, 6)
        stp_i, ctp_i = take(2, SJ, dt=i32), take(2, CJ, dt=i32)
        take = carve(U, UWORDS)
        xw = take(W, D + 1)
        cols = take(12, W)
        AB = [take(2, GC) for _ in range(2)]
        zs = take(GROUP, GC)
        r2 = take(GC)
        yg = take(GROUP, D)
        att = take(2, D)
        take = carve(U, UWORDS)
        take(W * (D + 1) + 12 * W + 4 * GC)
        ATT_T = take(W * D)
        macc_att = ATT_T[:, 0:N]
        take = carve(U, UWORDS)
        V1, V2, V3 = take(W * (D + 1)), take(W * D), take(N)
        hs1 = U[:, 0:W * (3 * D + 2) // 2].bitcast(bf16).rearrange("p (w c) -> p w c", w=W)
        hs2 = U[:, UWORDS - W * (3 * D + 2) // 2:UWORDS].bitcast(bf16).rearrange("p (w c) -> p w c", w=W)
        S1, S2 = U[:, 0:W * D], U[:, W * D:2 * W * D]
        S3 = U[:, 2 * W * D:2 * W * D + N]
        H3 = U[:, UWORDS - W * D:UWORDS]
        sg0 = U[:, 5000:5000 + GROUP * D].rearrange("p (w d) -> p w d", w=GROUP)
        sg1 = U[:, 0:GROUP * D].rearrange("p (w d) -> p w d", w=GROUP)
        PS = ctx.enter_context(nc.psum_tensor("PS", [128, 8, 512], f32))
        mm = PS[:, 0:2, :].rearrange("p b (j c) -> p (b j) c", c=128)

        KB = K[:, 0:KEEP, :].rearrange("p b d -> p (b d)").bitcast(f32)
        take = carve(KB, KEEP * NP // 2)
        X0, T0 = (take(W * D) for _ in range(2))
        H0 = HN[:, :, :].rearrange("p w d -> p (w d)")
        gathered = [sig(f"gathered{n}") for n in range(MSG_SLOTS)]
        tabled = [sig(f"tabled{n}") for n in range(TABLES)]
        block = ctx.enter_context(nc.Block())

        def wide(v):
            return v[0:P, 0:W * D].rearrange("p (w d) -> p w d", w=W)

        def over_features(v):
            return v.unsqueeze(2).to_broadcast([P, W, D])

        def over_windows(v):
            return v.unsqueeze(1).to_broadcast([P, W, D])

        @block.sync
        def _(sp):
            def loads(name, *pairs):
                for dst, src in pairs:
                    sp.dma_start(dst, src).then_inc(sig(name), 16)

            loads("x_in", (wide(X0), nodes(a["x"])))
            loads("sched_in", (tl_i[0:SK], a["last"].partition_broadcast(SK)),
                  (tl_f[3][0:SK], a["tiles"].partition_broadcast(SK)))
            loads("consts_in", (pidx[:, :], a["pidx"]), (ident[:, :], a["ident"]), (earlier, a["earlier"]),
                  (spare, a["spare"]), (keys[:, :], a["keys"]), (ramp[:, :], a["ramp"]))
            sp.wait_ge(sig("bias_zero"), 1)
            for t in range(TABLES):
                for w0 in range(0, W, 9):
                    w1 = min(w0 + 9, W)
                    loads("tables_zero", (sum_d[t][w0 * P:w1 * P].rearrange("(w p) d -> p w d", p=P), bias[0:P, 0:w1 - w0]))
            sp.wait_ge(sig("windows_made"), 2)
            loads("windows_out", (win_d.rearrange("(p j) -> p j", p=SK), stp_i[0:SK, 1, :]),
                  (cwin_d.rearrange("(p j) -> p j", p=CK), ctp_i[0:CK, 1, :]))
            sp.wait_ge(sig("windows_out"), 32)
            loads("windows_in", (IK[0:1], win_d.unsqueeze(0)), (CIK[0:1], cwin_d.unsqueeze(0)))
            sp.wait_ge(sig("h_made"), 1)
            loads("h0_out", (nodes(h0_d), wide(H0)))
            sp.wait_ge(sig("step_rows"), 1)
            by_step = lambda v: v.rearrange("(p j) e -> p j e", p=SK)
            loads("rows_out", (by_step(dl_d), st_f[0][0:SK]), (by_step(pen_d), st_f[2][0:SK]),
                  (by_step(w_d), st_w[0:SK]),
                  (by_step(src_d), st_f[3][0:SK]))

            def edge_rows(q, half):
                part = lambda v: v[bass.ds(q * TABLES, TABLES), :].rearrange("s e -> (s e)")
                sp.dma_start(dst_hot[half][0:P], part(dl_d).partition_broadcast(P)).then_inc(sig(f"edges_in{half}"), 16)
                sp.dma_start(src_row[half], part(src_d).partition_broadcast(128)).then_inc(sig(f"edges_in{half}"), 16)

            sp.wait_ge(sig("rows_out"), 64)
            for half in range(2):
                edge_rows(half, half)
            with sp.Fori(1, GCN_ROUNDS) as r:
                for half in range(2):
                    sp.wait_ge(sig("summed"), r * GCN_STEPS + half * TABLES)
                    sp.sem_inc(sig("half_seen"), 1)
                    sp.wait_ge(sig("index_ready"), r * 2 + half)
                    edge_rows(r * 2 + half, half)

            sp.wait_ge(sig("cnt_added"), CSTEPS + 2)
            loads("k_out", (k_d, K[0:P, KEEP:, :].rearrange("p b d -> p (b d)")))
            sp.wait_ge(sig("k_out"), 16)
            sp.wait_ge(sig("summed"), STEPS + TABLES)
            blocks = ["L0_a", "L0_b_w", "L1_src", "L1_dst", "L1_W2", "L1_U1a", "L1_U1b", "L1_U2"]
            loads("wts_in", *[(wts[:, n, :], a[b]) for n, b in enumerate(blocks)])
            vectors = ["L0_b", "L1_b2", "L1_c2", "L2_b_emb", "L2_b1a", "L2_b1b", "L2_b2", "L3_bl1", "L3_bl2"]
            loads("wts_in", *[(bias[0:P, n, :], a[b].partition_broadcast(P)) for n, b in enumerate(vectors)])
            loads("wts_in", (bcol[:, 0:1], a["L1_b1"]), (bcol[:, 1:2], a["L1_c1"]))

            loads("x_in", (wide(X), nodes(a["x"])))
            loads("h_in", (wide(H), nodes(h0_d)))
            for t in range(TABLES):
                sp.wait_ge(tabled[t], 16 * (STEPS // TABLES + 2))
            loads("nb0_in", (wide(Y), nodes(sum_d[0][0:N])))
            for t in range(1, TABLES):
                if t > 2:
                    sp.wait_ge(sig("nb_added"), t - 2)
                loads(f"nb{t}_in", (wide((T, HT)[t % 2]), nodes(sum_d[t][0:N])))
            sp.wait_ge(sig("h_in"), 16)
            loads("qrow_in", (QU[P:P + 1].rearrange("p (w d) -> p w d", w=W),
                              a["L1_wrow"].unsqueeze(1).to_broadcast([1, W, D])))
            sp.wait_ge(sig("dense_copied"), after("msg_P"))
            loads("p_out", (nodes(p_d), wide(Y)))

            def message_rows(q, half):
                part = lambda v: v[bass.ds(q * HALF, HALF), :].rearrange("s e -> (s e)")
                sem = sig(f"rows_in{half}")
                sp.dma_start(dlb[half][0:P], part(dl_d).partition_broadcast(P)).then_inc(sem, 16)
                sp.dma_start(penb[half], part(pen_d).partition_broadcast(128)).then_inc(sem, 16)
                sp.dma_start(mrhs[half][P:P + 1], part(w_d).unsqueeze(0)).then_inc(sem, 16)

            sp.wait_ge(sig("p_out"), 16)
            for half in range(2):
                message_rows(half, half)
            with sp.Fori(1, MSG_ROUNDS) as r:
                for half in range(2):
                    sp.wait_ge(sig("scan_ready"), r * 2 + half)
                    message_rows(r * 2 + half, half)

            sp.wait_ge(sig("msg_ready"), MSG_ROUNDS * 2 + 1)
            later = ["L2_emb", "L2_W1a", "L2_W1b", "L2_W2a", "L2_W2b"]
            loads("wts2_in", *[(wts[:, n, :], a[b]) for n, b in enumerate(later)])
            sp.wait_ge(sig("x2_made"), 1)
            loads("x_out", (nodes(x_d), wide(X)))
            for n in range(2):
                sp.wait_ge(sig("dense_copied"), after(f"gat_x{n}"))
                loads("xw_out", (nodes(xw_d[n]), wide((Y, H)[n])))
            sp.wait_ge(sig("x_out"), 16)
            sp.wait_ge(sig("xw_out"), 32)
            loads("k_in", (K[0:P, KEEP:, :].rearrange("p b d -> p (b d)"), k_d))
            loads("wts3_in", *[(wts[:, 5 + n, :], a[b]) for n, b in enumerate(("L3_Wl1", "L3_Wr1", "L3_Wl2"))])

            def store_out(sp, u, g):
                sp.wait_ge(sig("outs_free"), u * GROUPS + g + 1)
                loads("o_out", (o_d[u][g * GC:(g + 1) * GC, :].rearrange("(w p) d -> p w d", p=P), yg[0:P]))

            for u in range(3):
                if u < 2:
                    if u:
                        sp.wait_ge(sig("outs_ready"), GROUPS * u)
                    loads("xw_in", (xw[0:P, :, 0:D], nodes(xw_d[u])))
                    if u:
                        sp.wait_ge(sig("outs_free"), GROUPS * u)
                else:
                    sp.wait_ge(sig("outs_free"), GROUPS * u)
                loads("att_in", *[(att[0:P, n, :], a[b].partition_broadcast(P))
                                  for n, b in enumerate((f"L2_src{u}", f"L2_dst{u}"))])
                sp.wait_ge(sig("dense_copied"), after(f"rows{u}"))
                loads("rowsAB_out", (rows_d[u].rearrange("a (w p) -> (a w) p", p=P),
                                     yg[0:2 * W].rearrange("p a b -> p (a b)")[:, 0:P]))
                sp.wait_ge(sig("rowsAB_out"), 16 * (u + 1))
                for g in range(GROUPS):
                    if g > 1:
                        sp.wait_ge(sig("exp_ready"), (u * GROUPS + g - 1) * W)
                    loads(f"ab_in{g % 2}", (AB[g % 2][0:P], rows_d[u][:, g * GC:(g + 1) * GC].unsqueeze(0).to_broadcast([P, 2, GC])))
                    if g > 1:
                        store_out(sp, u, g - 2)
                store_out(sp, u, GROUPS - 2)
                store_out(sp, u, GROUPS - 1)
                if u == 1:
                    sp.wait_ge(sig("o_out"), 16 * 2 * GROUPS)
                    loads("o_in", (wide(V1), nodes(o_d[0])))
                    sp.wait_ge(sig("dense_copied"), after("gat_o0T"))
                    loads("o_in", (wide(V1), nodes(o_d[1])))
            sp.wait_ge(sig("dense_copied"), after("gat_x2"))
            loads("wts4_in", (wts[:, 0, :], a["L3_Wr2"]))
            sp.wait_ge(sig("o_out"), 16 * 3 * GROUPS)
            loads("x3_in", (wide(S1), nodes(x_d)), (wide(H3), nodes(o_d[2])))
            sp.wait_ge(sig("x3_made"), 1)
            loads("x3_out", (nodes(x_d), wide(S1)))
            sp.wait_ge(sig("h_made"), 4)
            loads("h3_out", (nodes(h3_d), wide(H3)))

            for v in range(2):
                for g in range(GROUPS):
                    sp.wait_ge(sig("sg_ready"), GROUP * (v * GROUPS + g + 2))
                    loads("agg_out", (agg_d[v][g * GC:(g + 1) * GC, :].rearrange("(w p) d -> p w d", p=P),
                                      (sg0, sg1)[v][0:P]))
                sp.wait_ge(sig("agg_out"), 16 * GROUPS * (v + 1) + 1)
                loads("s_in", (wide(S1), nodes(agg_d[v])))
                sp.wait_ge(sig("dense_copied"), after(f"sage{v + 1}_aT"))
                loads("s_in", (wide(S1), nodes((h3_d, g3_d)[v])))
                if v == 0:
                    sp.wait_ge(sig("g3_made"), 1)
                    loads("g3_out", (nodes(g3_d), wide(S1)))
            sp.wait_ge(sig("dense_copied"), after("sage2_out"))
            loads("x4_in", (wide(S2), nodes(x_d)))
            sp.wait_ge(sig("x4_made"), 1)
            loads("stored", (nodes(out), wide(S1)))
            sp.wait_ge(sig("stored"), 16)

        @block.gpsimd
        def _(pool):
            for name, free in (("msg_used", MSG_SLOTS), ("sums_added", HALF),
                               ("csum_ready", 2), ("cnt_copied", 2), ("cnt_added", 2), ("z_used", GROUP), ("sg_ready", GROUP),
                               ("picked_ready", 2), ("picked_copied", 2), ("summed", TABLES), ("rows_ready", 2), ("agg_out", 1),
                               ("relu_done", 1), ("msg_ready", 1), ("scan_ready", 1), ("back_ready", 1),
                               ("back_copied", 1), ("carried", 1), ("index_ready", 1), ("min_ready", 1), ("sums_ready", 1)):
                pool.sem_inc(sig(name), free)
            pool.wait_ge(sig("bias_zero"), 1)
            for t in range(TABLES):
                for half in range(2):
                    rows_ = slice(half * EDGES // 2, (half + 1) * EDGES // 2)
                    pool.dma_start(sum_d[t][N:][rows_], bias[rows_, 0, :]).then_inc(tabled[t], 16)

            def gather(dst, rows, index, sem):
                pool.indirect_dma_start(dst, None, rows, bass.IndirectOffsetOnAxis(ap=index, axis=0)).then_inc(sem, 16)

            pool.wait_ge(sig("windows_made"), 2)
            for j in range(SJ):
                gather(st_i[0:SK, j, :], a["edges"], stp_i[0:SK, 0, j:j + 1], sig("tiles_in"))
                gather(st_w[0:SK, j, :], a["weights"], stp_i[0:SK, 0, j:j + 1], sig("tiles_in"))
            for j in range(CJ):
                gather(ct_i[0:CK, j, :], a["ends"], ctp_i[0:CK, 0, j:j + 1], sig("ctiles_in"))
            pool.wait_ge(sig("h0_out"), 16)
            pool.memset(KB, 0.0).then_inc(sig("k_zero"), 1)

            pool.wait_ge(sig("tables_zero"), 16 * 3 * TABLES)
            with pool.Fori(0, GCN_ROUNDS) as r:
                for half in range(2):
                    for t in range(TABLES):
                        k = r * GCN_STEPS + (half * TABLES + t)
                        pool.wait_ge(sig("rows_ready"), k + 3)
                        pool.wait_ge(tabled[t], r * 32 + 16 * (half + 2))
                        pool.wait_ge(sig("index_ready"), r * 2 + (half + 2))
                        pool.sem_inc(sig("row_seen"), 1)
                        pool.indirect_dma_start(sum_d[t], bass.IndirectOffsetOnAxis(ap=index[:, half * TABLES + t:half * TABLES + (t + 1)], axis=0),
                                                rows[:, t, :], None, compute_op=ALU.add).then_inc(tabled[t], 16)

            pool.wait_ge(sig("p_out"), 16)
            with pool.Fori(0, MSG_ROUNDS) as r:
                for n in range(MSG_SLOTS):
                    k = r * MSG_SLOTS + n
                    pool.wait_ge(sig("msg_used"), k + 1)
                    pool.tensor_copy(index[:, n:n + 1], SRC[:, bass.ds(k, 1)]).then_inc(sig("index_copied"), 1)
                    pool.wait_ge(sig("index_copied"), k + 1)
                    pool.sem_inc(sig("index_seen"), 1)
                    gather(MG[:, n, :], p_d, index[:, n:n + 1], gathered[n])
            for u in range(3):
                pool.wait_ge(sig("range_in"), u + 1)
                pool.partition_all_reduce(scal[0:P, 2:4], scal[0:P, 0:2], P, RMAX).then_inc(sig("range_out"), 1)

        @block.scalar
        def _(act):
            def copy_round(n, pairs, func=ACT.Copy, **kw):
                act.wait_ge(sig("dense_ready"), n + 1)
                for i, (dst, src) in enumerate(pairs):
                    ins = nc.scalar.activation(dst, src, func, **kw)
                ins.then_inc(sig("dense_copied"), 1)

            def turned(stage, dst):
                for g in range(GROUPS):
                    copy_round(before(stage) + g,
                               [(dst[:, g * GC:(g + 1) * GC].rearrange("p (w n) -> p w n", w=GROUP), mm[:, 0:GROUP, 0:P])])

            def straight(stage, dst):
                for g in range(GROUPS):
                    copy_round(before(stage) + g, [(dst[0:P, g * GROUP:(g + 1) * GROUP, 0:D], mm[0:P, 0:GROUP, :])])

            def roots(n):
                act.wait_ge(sig("root_in"), n)
                nc.scalar.activation(rowv[:, 1, :], rowv[:, 1, :], ACT.Sqrt).then_inc(sig("root_out"), 1)

            roots(1)
            for j in range(SJ):
                copy_round(before("steps") + j, [(dst.rearrange("p (k j) -> p j k", j=SJ)[:, j, :], mm[:, i, 0:SK]) for i, dst in enumerate((SRC, SRCF, LAST, WT))])
            for j in range(CJ):
                copy_round(before("counts") + j, [(dst.rearrange("p (k j) -> p j k", j=CJ)[:, j, :], mm[:, i, 0:CK]) for i, dst in enumerate((KEY, SLO))])

            with act.Fori(0, GCN_ROUNDS) as r:
                def picked_copy(s):
                    k = r * GCN_STEPS + s
                    act.wait_ge(sig("picked_ready"), k + 3)
                    act.wait_ge(sig("summed"), k + (TABLES - 1))
                    nc.scalar.activation(picked[:, s % 2, :], PS[:, 2 + s % 2, 0:D], ACT.Copy)\
                        .then_inc(sig("picked_copied"), 1)

                def row_copy(s):
                    k = r * GCN_STEPS + s
                    act.wait_ge(sig("summed"), k + (TABLES + 1))
                    act.wait_ge(tabled[s % TABLES], r * 32 + 16 * (s // TABLES + 2))
                    nc.scalar.activation(rows[:, s % TABLES, :], PS[:, 6 + s % 2, 0:D], ACT.Copy)\
                        .then_inc(sig("rows_ready"), 1)

                for j in range(CNT_PER_ROUND):
                    if 1 <= j < 1 + GCN_STEPS:
                        picked_copy(j - 1)
                    if 2 <= j < 2 + GCN_STEPS:
                        row_copy(j - 2)
                    m = r * CNT_PER_ROUND + j
                    act.wait_ge(sig("csum_ready"), m + 3)
                    act.wait_ge(sig("cnt_added"), m + (1 if j else 2))
                    nc.scalar.activation(cnt[0:P, j % 2, :], PS[0:P, 4 + j % 2, 0:W * Q], ACT.Copy)\
                        .then_inc(sig("cnt_copied"), 1)

            turned("gcn_hT", HT)
            turned("gcn_aT", T)
            straight("gcn_out", wide(Y))
            roots(2)
            roots(3)
            turned("msg_hT", HT)
            straight("msg_P", wide(Y))
            straight("msg_Q", wide(QU))

            act.wait_ge(sig("qrow_in"), 16)
            act.wait_ge(sig("windows_in"), 32)
            act.wait_ge(sig("macc_zero"), 1)
            def windows_act(r):
                return nc.values_load_multi_w_load_instructions(
                    IK[0:1, bass.ds(r * MSG_SLOTS, MSG_SLOTS)], engines=[mybir.EngineType.Activation], min_val=0, max_val=W - 1,
                    skip_runtime_bounds_check_because="steps' windows lie in this range by their construction")[1]

            def projections(window, half):
                for s in range(HALF):
                    n = half * HALF + s
                    nc.scalar.activation(Qc[0:P + 1, n, :], QU[0:P + 1].rearrange("p (w d) -> p w d", w=W)
                                         [:, bass.ds(window[n], 1), :].rearrange("p a d -> p (a d)"), ACT.Copy)\
                        .then_inc(sig("q_copied"), 1)

            def relu_half(r, half):
                act.wait_ge(sig("pre_ready"), r * 2 + (half + 1))
                act.wait_ge(sig("msg_ready"), r * 2 + (half + 1))
                nc.scalar.activation(relu, PS[:, 4, :], ACT.Relu, bias=bcol[:, 0:1]).then_inc(sig("relu_done"), 1)

            def copy_back(r, half):
                act.wait_ge(sig("back_ready"), r * 2 + (half + 2))
                act.wait_ge(sig("sums_ready"), r * MSG_SLOTS + (half * HALF + 1))
                nc.scalar.activation(back[:, :, 0:D], PS[:, 0, :].rearrange("p (s d) -> p s d", s=HALF), ACT.Copy)\
                    .then_inc(sig("back_copied"), 1)

            window = windows_act(0)
            projections(window, 0)
            projections(window, 1)
            relu_half(0, 0)
            with act.Fori(0, MSG_ROUNDS - 1) as r:
                window = windows_act(r + 1)
                for half, after_ in ((0, (r, 1)), (1, (r + 1, 0))):
                    projections(window, half)
                    relu_half(*after_)
                    copy_back(r, half)
            relu_half(MSG_ROUNDS - 1, 1)
            copy_back(MSG_ROUNDS - 1, 0)
            copy_back(MSG_ROUNDS - 1, 1)

            turned("msg_aT", T)
            for g in range(GROUPS):
                copy_round(before("msg_u") + g,
                           [(QU[:, g * GC:(g + 1) * GC].rearrange("p (w n) -> p w n", w=GROUP), mm[:, 0:GROUP, 0:P])],
                           ACT.Relu, bias=bcol[:, 1:2])
            straight("msg_out", wide(Y))
            roots(4)
            turned("gat_hT", HT)
            straight("gat_emb", wide(Y))
            turned("gat_eT", T)
            straight("gat_x0", wide(Y))
            straight("gat_x1", wide(H))

            def scores_in(u, g):
                each = (GROUPS + 1 - g % 2) // 2
                return sig(f"ab_in{g % 2}"), 16 * (u * each + g // 2 + 1)

            for u in range(3):
                copy_round(before(f"rows{u}"), [(yg[0:2 * W].rearrange("p a b -> p (a b)")[:, 0:P], mm[0:2 * W, 0, 0:P])])
                def pair(g, q, c):
                    n = q * GROUP + (u * W * GROUPS + g * W + c)
                    b = q * GROUP + c
                    act.wait_ge(sig("z_used"), n + 1)
                    nc.scalar.activation(zs[0:P, c, :], AB[g % 2][0:P, 0, :], ACT.Relu, scale=-1.0,
                                         bias=cols[0:P, 9, bass.ds(b, 1)])
                    act.wait_ge(sig("min_ready"), n + 1)
                    nc.scalar.activation(r2[0:P], AB[g % 2][0:P, 1, :], ACT.Relu, scale=-1.0,
                                         bias=cols[0:P, 10, bass.ds(b, 1)]).then_inc(sig("pair_ready"), 1)

                def exponential(g, q, c):
                    act.wait_ge(sig("min_ready"), q * GROUP + (u * W * GROUPS + g * W + c + 2))
                    nc.scalar.activation(zs[0:P, c, :], zs[0:P, c, :], ACT.Exp, scale=-1.0).then_inc(sig("exp_ready"), 1)

                act.wait_ge(*scores_in(u, 0))
                pair(0, 0, 0)
                for g in range(GROUPS):
                    with act.Fori(0, GROUPS - 1) as q:
                        for c in range(GROUP):
                            pair(g, *((q, c + 1) if c < GROUP - 1 else (q + 1, 0)))
                            exponential(g, q, c)
                    for c in range(GROUP):
                        if c < GROUP - 1:
                            pair(g, GROUPS - 1, c + 1)
                        elif g < GROUPS - 1:
                            act.wait_ge(*scores_in(u, g + 1))
                            pair(g + 1, 0, 0)
                        exponential(g, GROUPS - 1, c)
                if u == 1:
                    for n, dst in enumerate((V3, V2)):
                        act.wait_ge(sig("elu_in"), n + 1)
                        nc.scalar.activation(V2[0:P], V2[0:P], ACT.Exp).then_inc(sig("elu_out"), 1)
                        turned(f"gat_o{n}T", dst)
                    straight("gat_x2", xw)
            roots(5)
            for v in range(2):
                with act.Fori(0, GROUPS) as g:
                    for w in range(GROUP):
                        i = g * GROUP + (v * W + w)
                        act.wait_ge(sig("sage_ready"), i + 1)
                        if w == 0:
                            act.wait_ge(sig("agg_out"), g * 16 + (v * GROUPS * 16 + 1))
                        nc.scalar.activation((sg0, sg1)[v][0:P, w, :], PS[0:P, 3 + w, 2 * D:3 * D], ACT.Copy)\
                            .then_inc(sig("third_copied"), 1)
                turned(f"sage{v + 1}_aT", S2)
                turned(f"sage{v + 1}_hT", S3)
                straight(f"sage{v + 1}_out", wide(S1))

        @block.vector
        def _(dve):
            v_ = nc.vector
            step = sig("dve_step")
            done = [0]

            def link(ins):
                done[0] += 1
                ins.then_inc(step, 1)
                dve.wait_ge(step, done[0])

            def root(n, out):
                dve.wait_ge(sig("root_out"), n)
                if out is not None:
                    link(v_.tensor_scalar_max(rowv[:, 1, :], rowv[:, 1, :], out))
                link(v_.reciprocal(rowv[:, 1, :], rowv[:, 1, :]))

            def normalise(x, h, t, n):
                link(v_.tensor_reduce(rowv[:, 0, :], x, AX.X, ALU.add))
                link(v_.tensor_scalar_mul(rowv[:, 0, :], rowv[:, 0, :], 1.0 / D))
                link(v_.tensor_tensor(h, x, over_features(rowv[:, 0, :]), ALU.subtract))
                link(v_.tensor_tensor(t, h, h, ALU.mult))
                link(v_.tensor_reduce(rowv[:, 1, :], t, AX.X, ALU.add))
                v_.tensor_scalar(rowv[:, 1, :], rowv[:, 1, :], 1.0 / D, 1e-5, ALU.mult, ALU.add)\
                    .then_inc(sig("root_in"), 1)
                root(n, None)
                link(v_.tensor_tensor(h, h, over_features(rowv[:, 1, :]), ALU.mult))
                v_.tensor_scalar_max(h, h, 0.0).then_inc(sig("h_made"), 1)

            v_.memset(bias[:, :, :], 0.0).then_inc(sig("bias_zero"), 1)
            dve.wait_ge(sig("x_in"), 16)
            normalise(wide(X0), wide(H0), wide(T0), 1)

            def quotient(q, v, by, r, qi):
                link(v_.tensor_scalar_mul(qi, v, 1.0 / by))
                link(v_.tensor_copy(q, qi))
                link(v_.scalar_tensor_tensor(r, q, -float(by), v, ALU.mult, ALU.add))
                link(v_.scalar_tensor_tensor(q, r, 0.0, q, ALU.is_ge, ALU.add))
                link(v_.scalar_tensor_tensor(q, r, float(by), q, ALU.is_ge, ALU.add))
                link(v_.tensor_scalar_add(q, q, -1.0))

            dve.wait_ge(sig("sched_in"), 32)
            dve.wait_ge(sig("consts_in"), 96)
            link(v_.tensor_copy(tl_f[0][0:SK], tl_i[0:SK]))
            for size, windows, sk, sj, sp_, spi in ((P, W, SK, SJ, stp, stp_i), (Q, QW, CK, CJ, ctp, ctp_i)):
                quotient(tl_f[1][0:sk], tl_f[0][0:sk], size, tl_f[2][0:sk], tl_q[0:sk])
                link(v_.scalar_tensor_tensor(tl_f[1][0:sk], tl_f[1][0:sk], float(windows - 1), tl_f[3][0:sk],
                                             ALU.min, ALU.add))
                for j in range(sj):
                    link(v_.tensor_scalar(sp_[0:sk, j, 0:1], pidx[0:sk], float(sj), float(j), ALU.mult, ALU.add))
                    link(v_.tensor_scalar(tl_f[4][0:sk], tl_f[1][0:sk], sp_[0:sk, j, 0:1], None, ALU.is_lt))
                    link(v_.tensor_reduce(sp_[0:sk, j, 1:2], tl_f[4][0:sk], AX.X, ALU.add))
                link(v_.tensor_tensor(sp_[0:sk, :, 2], sp_[0:sk, :, 0], sp_[0:sk, :, 1], ALU.subtract))
                link(v_.tensor_scalar_mul(sp_[0:sk, :, 3], sp_[0:sk, :, 2], -float(size)))
                link(v_.tensor_copy(spi[0:sk, 0, :], sp_[0:sk, :, 1]))
                v_.tensor_copy(spi[0:sk, 1, :], sp_[0:sk, :, 2]).then_inc(sig("windows_made"), 1)

            dve.wait_ge(sig("tiles_in"), 32 * SJ)
            part = lambda v, n: v[0:SK, :, n * EDGES:(n + 1) * EDGES]
            f = [v[0:SK] for v in st_f]
            link(v_.tensor_copy(f[0], part(st_i, 1)))
            link(v_.tensor_copy(f[3], part(st_i, 0)))
            link(v_.tensor_tensor(f[0], f[0], stp[0:SK, :, 3].unsqueeze(2).to_broadcast([SK, SJ, EDGES]), ALU.add))
            link(v_.tensor_tensor(f[1], part(st_i, 1), part(st_i, 3), ALU.not_equal))
            link(v_.scalar_tensor_tensor(f[1], f[0], 1.0, f[1], ALU.add, ALU.mult))
            link(v_.tensor_scalar_add(f[1], f[1], -1.0))
            link(v_.tensor_tensor(f[2], part(st_i, 1), part(st_i, 2), ALU.is_equal))
            v_.tensor_scalar(f[2], f[2], -1.0, BIG, ALU.add, ALU.mult).then_inc(sig("step_rows"), 1)

            dve.wait_ge(sig("ctiles_in"), 16 * CJ)
            f = [v[0:CK] for v in ct_f]
            link(v_.tensor_copy(f[0], ct_i[0:CK, :, EDGES:]))
            link(v_.tensor_copy(f[1], ct_i[0:CK, :, 0:EDGES]))
            link(v_.tensor_tensor(f[0], f[0], ctp[0:CK, :, 3].unsqueeze(2).to_broadcast([CK, CJ, EDGES]), ALU.add))
            quotient(f[2], f[1], P, f[4], ct_q[0:CK])
            link(v_.scalar_tensor_tensor(f[3], f[2], -float(P), f[1], ALU.mult, ALU.add))
            link(v_.scalar_tensor_tensor(f[1], f[2], float(Q), f[0], ALU.mult, ALU.add))
            link(v_.tensor_single_scalar(f[2], f[0], 0.0, ALU.is_ge))
            link(v_.scalar_tensor_tensor(f[2], f[0], float(Q), f[2], ALU.is_lt, ALU.mult))
            link(v_.scalar_tensor_tensor(f[1], f[1], 1.0, f[2], ALU.add, ALU.mult))
            v_.tensor_scalar_add(f[1], f[1], -1.0).then_inc(sig("cstep_rows"), 1)

            dve.wait_ge(sig("dense_copied"), after("counts"))
            dve.wait_ge(sig("rows_out"), 64)
            dve.wait_ge(sig("windows_out"), 32)
            v_.memset(KA, 0.0).then_inc(sig("zeros"), 1)
            dve.wait_ge(sig("zeros"), 1)
            dve.wait_ge(sig("k_zero"), 1)
            dve.wait_ge(sig("windows_in"), 32)

            def windows_of(row, at, n, last):
                return nc.values_load_multi_w_load_instructions(
                    row[0:1, bass.ds(at, n)], engines=[mybir.EngineType.DVE], min_val=0, max_val=last,
                    skip_runtime_bounds_check_because="steps' windows lie in this range by their construction")[1]

            with dve.Fori(0, GCN_ROUNDS) as r:
                dve.wait_ge(sig("tables_zero"), 16 * 3 * TABLES)
                cwindow = windows_of(CIK, r * CNT_PER_ROUND, CNT_PER_ROUND, QW - 1)

                def destinations(half):
                    dve.wait_ge(sig(f"edges_in{half}"), r * 32 + 32)
                    v_.tensor_scalar(dst_hot[half][0:P], dst_hot[half][0:P], pidx[0:P], None, ALU.is_equal)\
                        .then_inc(sig("dst_hot_ready"), 1)

                def sources(s):
                    k = r * GCN_STEPS + s
                    half, t = divmod(s, TABLES)
                    row = src_row[half][:, t * EDGES:(t + 1) * EDGES]
                    dve.wait_ge(sig("summed"), k + 1)
                    if t == 0:
                        dve.wait_ge(sig("index_ready"), r * 2 + (half + 1))
                    v_.tensor_scalar(same[:, t, :], row, SRCF[:, bass.ds(k, 1)], WT[:, bass.ds(k, 1)],
                                     ALU.is_equal, ALU.mult).then_inc(sig("same_ready"), 1)
                    v_.scalar_tensor_tensor(bias[:, 1 + t, :], row, SRCF[:, bass.ds(k, 1)], earlier, ALU.is_equal, ALU.mult,
                                            accum_out=again[:, t:t + 1]).then_inc(sig("again_made"), 1)

                def indices(half):
                    dve.wait_ge(sig("again_made"), r * GCN_STEPS + (half + 1) * TABLES)
                    v_.tensor_scalar(again, again, 0.0, spare, ALU.is_gt, ALU.mult).then_inc(sig("spare_made"), 1)
                    dve.wait_ge(sig("spare_made"), r * 2 + (half + 1))
                    for t in range(TABLES):
                        dve.wait_ge(tabled[t], r * 32 + 16 * (half + 1))
                    v_.tensor_tensor(index[:, half * TABLES:(half + 1) * TABLES], again, SRCF[:, bass.ds(r * GCN_STEPS + half * TABLES, TABLES)],
                                     ALU.max).then_inc(sig("index_ready"), 1)

                def count_hots(j):
                    m = r * CNT_PER_ROUND + j
                    dve.wait_ge(sig("csum_ready"), m + (1 if j else 2))
                    v_.tensor_scalar(khot[:, j % 2, :], keys[:, :], KEY[:, bass.ds(m, 1)], None, ALU.is_equal)
                    v_.tensor_scalar(slohot[:, j % 2, 0:P], keys[:, 0:P], SLO[:, bass.ds(m, 1)], None, ALU.is_equal)\
                        .then_inc(sig("chot_ready"), 1)

                def add_counts(j):
                    m = r * CNT_PER_ROUND + j
                    dve.wait_ge(sig("cnt_copied"), m + 3)
                    dve.wait_ge(sig("cnt_added"), m + 2)
                    part = K[0:P, :, bass.ds(cwindow[j] * Q, Q)]
                    v_.tensor_tensor(part, part, cnt[0:P, j % 2, :].rearrange("p (b d) -> p b d", b=W), ALU.add)\
                        .then_inc(sig("cnt_added"), 1)

                destinations(0)
                for j in range(CNT_PER_ROUND):
                    count_hots(j)
                    if j < GCN_STEPS:
                        sources(j)
                    if j % TABLES == TABLES - 1 and j < GCN_STEPS:
                        indices(j // TABLES)
                    if j == 4:
                        destinations(1)
                    if j:
                        add_counts(j - 1)
                add_counts(CNT_PER_ROUND - 1)

            X_, H_, Y_, T_ = wide(X), wide(H), wide(Y), wide(T)
            dve.wait_ge(sig("nb0_in"), 16)
            for t in range(1, TABLES):
                dve.wait_ge(sig(f"nb{t}_in"), 16)
                v_.tensor_tensor(Y_, Y_, wide((T, HT)[t % 2]), ALU.add).then_inc(sig("nb_added"), 1)
                dve.wait_ge(sig("nb_added"), t)
            dve.wait_ge(sig("x_in"), 32)
            dve.wait_ge(sig("dense_copied"), after("gcn_out"))
            dve.wait_ge(sig("wts_in"), 16 * 19)
            link(v_.tensor_tensor(Y_, Y_, over_windows(bias[0:P, 0, :]), ALU.add))
            link(v_.tensor_tensor(T_, Y_, Y_, ALU.mult))
            v_.tensor_reduce(rowv[:, 1, :], T_, AX.X, ALU.add).then_inc(sig("root_in"), 1)
            root(2, 1e-12)
            link(v_.tensor_tensor(Y_, Y_, over_features(rowv[:, 1, :]), ALU.mult))
            link(v_.tensor_tensor(X_, X_, Y_, ALU.add))
            normalise(X_, H_, T_, 3)

            dve.wait_ge(sig("dense_copied"), after("msg_Q"))
            v_.memset(macc[0:P], 0.0)
            v_.memset(carry[:, :], -BIG)
            v_.memset(back[:, :, D:D + 1], 1.0).then_inc(sig("macc_zero"), 1)

            def destination_hots(r, half):
                dve.wait_ge(sig(f"rows_in{half}"), r * 48 + 48)
                v_.tensor_scalar(mrhs[half][0:P], dlb[half][0:P], pidx[0:P], None, ALU.is_equal)\
                    .then_inc(sig("mrhs_ready"), 1)

            def last_hots(r, half):
                for s in range(HALF):
                    n = half * HALF + s
                    v_.tensor_scalar(lasthot[:, n, :], ramp[:, 0:P], LAST[:, bass.ds(r * MSG_SLOTS + n, 1)], None,
                                     ALU.is_equal).then_inc(sig("last_ready"), 1)

            def running_max(r, half):
                q = r * 2 + half
                dve.wait_ge(sig("msg_ready"), q + 2)
                dve.wait_ge(sig("back_ready"), q + 1)
                dve.wait_ge(sig("carried"), q + 1)
                v_.tensor_tensor_scan(scan, penb[half], PS[:, 5, :], carry[:, 0:1], ALU.add, ALU.max)\
                    .then_inc(sig("scan_ready"), 1)
                dve.wait_ge(sig("scan_ready"), q + 2)
                v_.tensor_copy(carry[:, :], scan[:, HALF * EDGES - 1:HALF * EDGES]).then_inc(sig("carried"), 1)

            def add_maxima(r, half, window):
                for s in range(HALF):
                    n = half * HALF + s
                    dve.wait_ge(sig("sums_ready"), r * MSG_SLOTS + (n + 2))
                    dve.wait_ge(sig("sums_added"), r * MSG_SLOTS + (n + HALF))
                    part = macc[0:P, bass.ds(window[n], 1), :].rearrange("p a d -> p (a d)")
                    v_.tensor_tensor(part, part, PS[0:P, SUM_BANKS[s], 0:D + 1], ALU.add).then_inc(sig("sums_added"), 1)

            destination_hots(0, 0)
            destination_hots(0, 1)
            last_hots(0, 0)
            running_max(0, 0)
            with dve.Fori(0, MSG_ROUNDS - 1) as r:
                window = windows_of(IK, r * MSG_SLOTS, MSG_SLOTS, W - 1)
                for half, after_ in ((0, (r, 1)), (1, (r + 1, 0))):
                    destination_hots(r + 1, half)
                    last_hots(*after_)
                    running_max(*after_)
                    add_maxima(r, half, window)
            r = MSG_ROUNDS - 1
            window = windows_of(IK, r * MSG_SLOTS, MSG_SLOTS, W - 1)
            last_hots(r, 1)
            running_max(r, 1)
            add_maxima(r, 0, window)
            add_maxima(r, 1, window)
            dve.wait_ge(sig("sums_added"), STEPS + HALF)
            link(v_.tensor_tensor(H_, over_features(macc[0:P, :, D]), over_windows(bias[0:P, 1, :]), ALU.mult))
            v_.tensor_tensor(H_, H_, macc[0:P, :, 0:D], ALU.add).then_inc(sig("agg_made"), 1)
            dve.wait_ge(sig("dense_copied"), after("msg_out"))
            link(v_.tensor_tensor(Y_, Y_, over_windows(bias[0:P, 2, :]), ALU.add))
            link(v_.tensor_tensor(X_, X_, Y_, ALU.add))
            v_.engine_nop().then_inc(sig("x2_made"), 1)
            normalise(X_, H_, T_, 4)
            dve.wait_ge(sig("dense_copied"), after("gat_emb"))
            v_.tensor_tensor(Y_, Y_, over_windows(bias[0:P, 3, :]), ALU.add).then_inc(sig("emb_made"), 1)

            c = lambda n: cols[0:P, n, :]
            for u in range(3):
                if u < 2:
                    dve.wait_ge(sig("xw_in"), 16 * (u + 1))
                else:
                    dve.wait_ge(sig("dense_copied"), after("gat_x2"))
                dve.wait_ge(sig("att_in"), 32 * (u + 1))
                v_.memset(xw[0:P, :, D:D + 1], 1.0)
                for n in range(2):
                    link(v_.tensor_tensor(wide(ATT_T), xw[0:P, :, 0:D], over_windows(att[0:P, n, :]), ALU.mult))
                    link(v_.tensor_reduce(c(n), wide(ATT_T), AX.X, ALU.add))
                link(v_.tensor_reduce(scal[0:P, 0:1], c(0), AX.X, ALU.max))
                link(v_.tensor_reduce(scal[0:P, 1:2], c(0), AX.X, ALU.min))
                v_.tensor_scalar_mul(scal[0:P, 1:2], scal[0:P, 1:2], -1.0).then_inc(sig("range_in"), 1)
                dve.wait_ge(sig("range_out"), u + 1)
                link(v_.tensor_tensor(scal[0:P, 4:5], scal[0:P, 2:3], scal[0:P, 3:4], ALU.add))
                link(v_.tensor_scalar_max(scal[0:P, 5:6], scal[0:P, 4:5], 1e-30))
                link(v_.reciprocal(scal[0:P, 5:6], scal[0:P, 5:6]))
                link(v_.tensor_scalar(c(2), c(0), scal[0:P, 3:4], scal[0:P, 5:6], ALU.add, ALU.mult))
                link(v_.tensor_scalar_min(c(2), c(2), 1.0))
                if u == 0:
                    dve.wait_ge(sig("k_in"), 16)
                    for b in range(W):
                        part = K[0:P, b, b * P:(b + 1) * P]
                        link(v_.tensor_tensor(part, part, ident[0:P, 0:P], ALU.add))
                v_.memset(macc_att[0:P], 0.0).then_inc(sig("max_step"), 1)
                with dve.Fori(0, W) as b:
                    dve.wait_ge(sig("max_step"), b + (u * (W + 1) + 1))
                    v_.scalar_tensor_tensor(macc_att[0:P], K[0:P, bass.ds(b, 1), 0:N].rearrange("p a d -> p (a d)"),
                                            cols[0:P, 2, bass.ds(b, 1)], macc_att[0:P], ALU.min, ALU.max)\
                        .then_inc(sig("max_step"), 1)
                for g in range(GROUPS):
                    dve.wait_ge(sig("max_turned"), u * GROUPS + g + 1)
                    v_.tensor_reduce(cols[0:P, 3, g * GROUP:(g + 1) * GROUP], mm[0:P, 0:GROUP, 0:P], AX.X, ALU.max)\
                        .then_inc(sig("max_reduced"), 1)
                dve.wait_ge(sig("max_reduced"), (u + 1) * GROUPS)
                link(v_.tensor_scalar(c(4), c(3), scal[0:P, 4:5], scal[0:P, 3:4], ALU.mult, ALU.subtract))
                link(v_.tensor_tensor(c(5), c(4), c(1), ALU.add))
                link(v_.scalar_tensor_tensor(c(6), c(5), SLOPE, c(5), ALU.mult, ALU.max))
                link(v_.tensor_tensor(c(7), c(1), c(6), ALU.subtract))
                link(v_.tensor_scalar_mul(c(9), c(0), -1.0))
                link(v_.tensor_scalar_mul(c(10), c(0), -SLOPE))
                v_.scalar_tensor_tensor(c(8), c(1), SLOPE, c(6), ALU.mult, ALU.subtract).then_inc(sig("ab_made"), 1)

                def minimum(g, q, i):
                    dve.wait_ge(sig("pair_ready"), q * GROUP + (u * W * GROUPS + g * W + i + 1))
                    v_.tensor_tensor(zs[0:P, i, :], zs[0:P, i, :], r2[0:P], ALU.min).then_inc(sig("min_ready"), 1)

                def counted(g, q, i):
                    dve.wait_ge(sig("exp_ready"), q * GROUP + (u * W * GROUPS + g * W + i + 1))
                    v_.tensor_tensor(zs[0:P, i, :], zs[0:P, i, :],
                                     K[0:P, bass.ds(q * GROUP + i, 1), g * GC:(g + 1) * GC].rearrange("p a d -> p (a d)"),
                                     ALU.mult).then_inc(sig("z_ready"), 1)

                minimum(0, 0, 0)
                for g in range(GROUPS):
                    with dve.Fori(0, GROUPS - 1) as q:
                        for i in range(GROUP):
                            minimum(g, *((q, i + 1) if i < GROUP - 1 else (q + 1, 0)))
                            counted(g, q, i)
                    for i in range(GROUP):
                        if i < GROUP - 1:
                            minimum(g, GROUPS - 1, i + 1)
                        elif g < GROUPS - 1:
                            minimum(g + 1, 0, 0)
                        counted(g, GROUPS - 1, i)
                    dve.wait_ge(sig("outs_ready"), u * GROUPS + g + 1)
                    dve.wait_ge(sig("rowsAB_out"), 16 * (u + 1))
                    dve.wait_ge(sig("o_out"), 16 * (u * GROUPS + g))
                    link(v_.tensor_scalar_add(scal[0:P, 8:13], PS[0:P, 3:8, D], 1e-16))
                    link(v_.reciprocal(scal[0:P, 8:13], scal[0:P, 8:13]))
                    for w in range(GROUP):
                        ins = v_.scalar_tensor_tensor(yg[0:P, w, :], PS[0:P, 3 + w, 0:D], scal[0:P, 8 + w:9 + w],
                                                      bias[0:P, 4 + u, :], ALU.mult, ALU.add)
                    ins.then_inc(sig("outs_free"), 1)
                if u == 1:
                    for n in range(2):
                        dve.wait_ge(sig("o_in"), 16 * (n + 1))
                        va, vb = V1[0:P, 0:W * D], V2[0:P]
                        v_.tensor_scalar_min(vb, va, 0.0).then_inc(sig("elu_in"), 1)
                        dve.wait_ge(sig("elu_in"), n + 1)
                        link(v_.tensor_scalar_max(va, va, 0.0))
                        dve.wait_ge(sig("elu_out"), n + 1)
                        v_.scalar_tensor_tensor(va, vb, -1.0, va, ALU.add, ALU.add).then_inc(sig("elu_made"), 1)

            for b in range(W):
                part = K[0:P, b, b * P:(b + 1) * P]
                link(v_.tensor_tensor(part, part, ident[0:P, 0:P], ALU.subtract))
            dve.wait_ge(sig("x3_in"), 32)
            v_.tensor_tensor(wide(S1), wide(S1), wide(H3), ALU.add).then_inc(sig("x3_made"), 1)
            dve.wait_ge(sig("x3_made"), 1)
            normalise(wide(S1), wide(H3), wide(S2), 5)
            dve.wait_ge(sig("x3_out"), 16)
            dve.wait_ge(sig("h3_out"), 16)

            def split(src, parts):
                link(v_.tensor_copy(parts[0:P, :, 0:D], src))
                for n in range(1, 3):
                    link(v_.tensor_tensor(src, src, parts[0:P, :, (n - 1) * D:n * D], ALU.subtract))
                    link(v_.tensor_copy(parts[0:P, :, n * D:(n + 1) * D], src))
                v_.memset(parts[0:P, :, 3 * D:3 * D + 2], 1.0).then_inc(sig("parts_made"), 1)

            split(wide(H3), hs1)
            for v in range(2):
                with dve.Fori(0, GROUPS) as g:
                    n = 0
                    base = done[0]
                    for w in range(GROUP):
                        i = g * GROUP + (v * W + w)
                        dst, bank = (sg0, sg1)[v][0:P, w, :], PS[0:P, 3 + w, :]

                        def chained(ins):
                            nonlocal n
                            n += 1
                            ins.then_inc(step, 1)
                            dve.wait_ge(step, g * (4 * GROUP) + (base + n))
                        dve.wait_ge(sig("third_copied"), i + 1)
                        chained(v_.tensor_scalar_max(scal[0:P, 13:14], bank[:, 3 * D:3 * D + 1], 1.0))
                        chained(v_.reciprocal(scal[0:P, 14:15], scal[0:P, 13:14]))
                        chained(v_.tensor_scalar(dst, dst, scal[0:P, 14:15], None, ALU.mult))
                        chained(v_.scalar_tensor_tensor(dst, bank[:, D:2 * D], scal[0:P, 14:15], dst, ALU.mult, ALU.add))
                        v_.scalar_tensor_tensor(dst, bank[:, 0:D], scal[0:P, 14:15], dst, ALU.mult, ALU.add)\
                            .then_inc(sig("sg_ready"), 1)
                        dve.wait_ge(sig("sg_ready"), i + (GROUP + 1))
                done[0] += 4 * GROUP * GROUPS
                dve.wait_ge(sig("dense_copied"), after(f"sage{v + 1}_out"))
                link(v_.tensor_tensor(wide(S1), wide(S1), over_windows(bias[0:P, 7 + v, :]), ALU.add))
                if v == 0:
                    v_.tensor_scalar_max(wide(S1), wide(S1), 0.0).then_inc(sig("g3_made"), 1)
                    dve.wait_ge(sig("g3_out"), 16)
                    split(wide(S1), hs2)
                else:
                    link(v_.tensor_scalar_max(wide(S1), wide(S1), 0.0))
                    dve.wait_ge(sig("x4_in"), 16)
                    v_.tensor_tensor(wide(S1), wide(S1), wide(S2), ALU.add).then_inc(sig("x4_made"), 1)

        @block.tensor
        def _(pe):
            mmul = nc.tensor.matmul

            def rounds(stage, ins, *ready):
                for name, value in ready:
                    pe.wait_ge(sig(name), value)
                for g in range(dict(STAGES)[stage]):
                    pe.wait_ge(sig("dense_copied"), before(stage) + g)
                    for last in ins(g):
                        pass
                    last.then_inc(sig("dense_ready"), 1)

            def turn(src):
                def ins(g):
                    for w in range(GROUP):
                        yield nc.tensor.transpose(mm[:, w, 0:P], src[0:P, g * GROUP + w, 0:D], ident[0:P, 0:P])
                return ins

            def project(*pairs):
                def ins(g):
                    for w in range(GROUP):
                        at = (g * GROUP + w) * P
                        for i, (nodes_T, block_) in enumerate(pairs):
                            yield mmul(mm[0:P, w, :], nodes_T[:, at:at + P], wts[:, block_, :],
                                       start=i == 0, stop=i == len(pairs) - 1)
                return ins

            def columns(views, size):
                def ins(j):
                    for i, v in enumerate(views):
                        yield nc.tensor.transpose(mm[:, i, 0:size], v[0:size, j, :], ident[0:size, 0:size])
                return ins

            pe.wait_ge(sig("consts_in"), 96)
            rounds("steps", columns((st_f[3], st_f[3], st_f[1], st_w), SK), ("step_rows", 1), ("tiles_in", 32 * SJ))
            rounds("counts", columns((ct_f[1], ct_f[3]), CK), ("cstep_rows", 1))

            pe.wait_ge(sig("h_made"), 1)
            pe.wait_ge(sig("windows_in"), 32)
            with pe.Fori(0, GCN_ROUNDS) as r:
                _, window = nc.values_load_multi_w_load_instructions(
                    IK[0:1, bass.ds(r * GCN_STEPS, GCN_STEPS)], engines=[mybir.EngineType.PE], min_val=0, max_val=W - 1,
                    skip_runtime_bounds_check_because="steps' windows lie in this range by their construction")

                def pick(s):
                    k = r * GCN_STEPS + s
                    half, t = divmod(s, TABLES)
                    pe.wait_ge(sig("dst_hot_ready"), r * 2 + (half + 1))
                    pe.wait_ge(sig("picked_copied"), k + 1)
                    mmul(PS[:, 2 + s % 2, 0:D], dst_hot[half][0:P, t * EDGES:(t + 1) * EDGES],
                         HN[0:P, bass.ds(window[s], 1), :].rearrange("p a d -> p (a d)"), start=True, stop=True)\
                        .then_inc(sig("picked_ready"), 1)

                def add_up(s):
                    k = r * GCN_STEPS + s
                    pe.wait_ge(sig("same_ready"), k + 1)
                    pe.wait_ge(sig("picked_copied"), k + 3)
                    pe.wait_ge(sig("rows_ready"), k + 1)
                    mmul(PS[:, 6 + s % 2, 0:D], same[:, s % TABLES, :], picked[:, s % 2, :],
                         start=True, stop=True).then_inc(sig("summed"), 1)

                for j in range(CNT_PER_ROUND):
                    m = r * CNT_PER_ROUND + j
                    pe.wait_ge(sig("chot_ready"), m + 1)
                    pe.wait_ge(sig("cnt_copied"), m + (1 if j else 2))
                    mmul(PS[0:P, 4 + j % 2, 0:W * Q], slohot[:, j % 2, 0:P], khot[:, j % 2, :], start=True, stop=True)\
                        .then_inc(sig("csum_ready"), 1)
                    if 1 <= j < 1 + GCN_STEPS:
                        pick(j - 1)
                    if 2 <= j < 2 + GCN_STEPS:
                        add_up(j - 2)

            rounds("gcn_hT", turn(wide(H)), ("h_in", 16), ("nb_added", TABLES - 1))
            rounds("gcn_aT", turn(wide(Y)))
            rounds("gcn_out", project((HT, 0), (T, 1)), ("wts_in", 16 * 19))
            rounds("msg_hT", turn(wide(H)), ("h_made", 2))
            rounds("msg_P", project((HT, 2)))
            rounds("msg_Q", project((HT, 3)), ("p_out", 16))

            def first_layer(r, half):
                q = r * 2 + half
                pe.wait_ge(sig("mrhs_ready"), q + 1)
                pe.wait_ge(sig("relu_done"), q + 1)
                for s in range(HALF):
                    n = half * HALF + s
                    part = PS[:, 4, s * EDGES:(s + 1) * EDGES]
                    pe.wait_ge(gathered[n], r * 16 + 16)
                    pe.wait_ge(sig("q_copied"), r * MSG_SLOTS + (n + 1))
                    mmul(part, MG[:, n, :], ident[:, :], start=True, stop=False).then_inc(sig("msg_used"), 1)
                    last = mmul(part, Qc[0:P + 1, n, :], mrhs[half][0:P + 1, s * EDGES:(s + 1) * EDGES],
                                start=False, stop=True)
                last.then_inc(sig("pre_ready"), 1)

            def second_layer(r, half):
                pe.wait_ge(sig("relu_done"), r * 2 + (half + 2))
                pe.wait_ge(sig("scan_ready"), r * 2 + (half + 1))
                mmul(PS[:, 5, :], wts[:, 4, :], relu, start=True, stop=True).then_inc(sig("msg_ready"), 1)

            def turn_back(r, half):
                pe.wait_ge(sig("scan_ready"), r * 2 + (half + 2))
                pe.wait_ge(sig("back_copied"), r * 2 + (half + 1))
                for s in range(HALF):
                    last = nc.tensor.transpose(PS[:, 0, s * EDGES:(s + 1) * EDGES], scan[:, s * EDGES:(s + 1) * EDGES],
                                               ident[:, :])
                last.then_inc(sig("back_ready"), 1)

            def pick_last(r, half):
                pe.wait_ge(sig("back_copied"), r * 2 + (half + 2))
                for s in range(HALF):
                    n = half * HALF + s
                    pe.wait_ge(sig("last_ready"), r * MSG_SLOTS + (n + 1))
                    pe.wait_ge(sig("sums_added"), r * MSG_SLOTS + (n + 1))
                    mmul(PS[0:P, SUM_BANKS[s], 0:D + 1], lasthot[:, n, :], back[:, s, :], start=True, stop=True)\
                        .then_inc(sig("sums_ready"), 1)

            first_layer(0, 0)
            second_layer(0, 0)
            with pe.Fori(0, MSG_ROUNDS - 1) as r:
                for half, after_ in ((0, (r, 1)), (1, (r + 1, 0))):
                    first_layer(*after_)
                    turn_back(r, half)
                    second_layer(*after_)
                    pick_last(r, half)
            r = MSG_ROUNDS - 1
            first_layer(r, 1)
            turn_back(r, 0)
            second_layer(r, 1)
            pick_last(r, 0)
            turn_back(r, 1)
            pick_last(r, 1)

            def hidden(g):
                for w in range(GROUP):
                    at = (g * GROUP + w) * P
                    mmul(mm[:, w, 0:P], wts[:, 5, :], HT[:, at:at + P], start=True, stop=False)
                    yield mmul(mm[:, w, 0:P], wts[:, 6, :], T[:, at:at + P], start=False, stop=True)

            rounds("msg_aT", turn(wide(H)), ("agg_made", 1))
            rounds("msg_u", hidden)
            rounds("msg_out", project((QU, 7)))
            rounds("gat_hT", turn(wide(H)), ("h_made", 3))
            rounds("gat_emb", project((HT, 0)), ("wts2_in", 16 * 5))
            rounds("gat_eT", turn(wide(Y)), ("emb_made", 1))
            rounds("gat_x0", project((T, 1)))
            rounds("gat_x1", project((T, 2)))

            for u in range(3):
                pe.wait_ge(sig("max_step"), (u + 1) * (W + 1))
                for g in range(GROUPS):
                    pe.wait_ge(sig("max_reduced"), u * GROUPS + g)
                    for w in range(GROUP):
                        at = (g * GROUP + w) * P
                        last = nc.tensor.transpose(mm[0:P, w, 0:P], macc_att[0:P, at:at + P], ident[0:P, 0:P])
                    last.then_inc(sig("max_turned"), 1)
                rounds(f"rows{u}", lambda g: [nc.tensor.transpose(
                    mm[0:2 * W, 0, 0:P], cols[0:P, 7:9, :].rearrange("p a w -> p (a w)"), ident[0:P, 0:P])],
                    ("ab_made", u + 1), ("max_reduced", (u + 1) * GROUPS))

                def chunk(n, b, i, first):
                    pe.wait_ge(sig("z_ready"), n + 1)
                    rows = xw[0:P, b, :] if isinstance(b, int) else xw[0:P, bass.ds(b, 1), :].rearrange("p a d -> p (a d)")
                    for w in range(GROUP):
                        last = mmul(PS[0:P, 3 + w, 0:D + 1], zs[0:P, i, w * P:(w + 1) * P], rows,
                                    start=first, stop=False, skip_group_check=True)
                    last.then_inc(sig("z_used"), 1)
                    return last

                for g in range(GROUPS):
                    at = u * W * GROUPS + g * W
                    pe.wait_ge(sig("outs_free"), u * GROUPS + g)
                    for i in range(GROUP):
                        chunk(at + i, i, i, i == 0)
                    with pe.Fori(1, GROUPS) as q:
                        for i in range(GROUP):
                            chunk(q * GROUP + (at + i), q * GROUP + i, i, False)
                    pe.wait_ge(sig("z_used"), at + W + GROUP)
                    pe.sem_inc(sig("outs_ready"), 1)
                if u == 1:
                    for n in range(2):
                        rounds(f"gat_o{n}T", turn(V1[:, 0:W * D].rearrange("p (w d) -> p w d", w=W)), ("elu_made", n + 1))
                    rounds("gat_x2", project((V3, 3), (V2, 4)))

            for v in range(2):
                pe.wait_ge(sig("parts_made"), v + 1)
                hs = (hs1, hs2)[v]
                with pe.Fori(0, GROUPS) as g:
                    for w in range(GROUP):
                        pe.wait_ge(sig("sg_ready"), g * GROUP + (v * W + w + 1))
                        for b in range(W):
                            last = mmul(PS[0:P, 3 + w, 0:3 * D + 1], K[0:P, b, bass.ds(g * GC + w * P, P)],
                                        hs[0:P, b, 0:3 * D + 1], start=b == 0, stop=b == W - 1)
                        last.then_inc(sig("sage_ready"), 1)
                name = f"sage{v + 1}"
                rounds(f"{name}_aT", turn(wide(S1)), ("s_in", 16 * (2 * v + 1)))
                rounds(f"{name}_hT", turn(wide(S1)), ("s_in", 16 * (2 * v + 2)))
                rounds(f"{name}_out", project((S2, 5 if v == 0 else 7), (S3, 6 if v == 0 else 0)),
                       ("wts3_in", 48), ("wts4_in", 16))


def kernel(**inputs):
    import concourse.bacc as bacc
    from concourse.bass_utils import run_bass_kernel_spmd

    g = {k: np.asarray(v) for k, v in inputs.items()}
    pad = TILES * EDGES - E
    src, dst, w = (g[k] for k in ("src", "dst", "edge_weight"))
    s_ = np.concatenate([src, np.zeros(pad, src.dtype)]).reshape(TILES, EDGES)
    d_ = np.concatenate([dst, np.full(pad, N, dst.dtype)])
    w_ = np.concatenate([w, np.zeros(pad, w.dtype)]).reshape(TILES, EDGES)
    prev = np.concatenate([np.full(1, N + 1, dst.dtype), d_[:-1]]).reshape(TILES, EDGES)
    next_ = np.concatenate([d_[1:], np.full(1, N + 1, dst.dtype)]).reshape(TILES, EDGES)
    d_ = d_.reshape(TILES, EDGES)
    block = lambda m, i, j: m[i * D:(i + 1) * D, j * D:(j + 1) * D]
    arrays = {
        "x": g["x"], "edges": np.concatenate([s_, d_, prev, next_], 1), "ends": np.concatenate([s_, d_], 1),
        "weights": w_, "last": d_[:, -1], "tiles": np.arange(TILES, dtype=np.float32),
        "pidx": np.arange(128, dtype=np.float32).reshape(128, 1), "ident": np.eye(128, dtype=np.float32),
        "earlier": np.tril(np.ones((EDGES, EDGES), np.float32), -1), "spare": N + np.arange(128, dtype=np.float32).reshape(128, 1),
        "ramp": np.tile(np.arange(128, dtype=np.float32), (128, 1)),
        "keys": np.tile(np.arange(W * Q, dtype=np.float16), (128, 1)),
        "L0_a": block(g["L0_gnn_W"], 0, 0).T, "L0_b_w": block(g["L0_gnn_W"], 0, 1).T, "L0_b": g["L0_gnn_b"],
        "L1_src": block(g["L1_gnn_W1"], 0, 0), "L1_dst": block(g["L1_gnn_W1"], 1, 0), "L1_wrow": g["L1_gnn_W1"][2 * D:],
        "L1_W2": g["L1_gnn_W2"], "L1_U1a": block(g["L1_gnn_U1"], 0, 0), "L1_U1b": block(g["L1_gnn_U1"], 1, 0),
        "L1_U2": g["L1_gnn_U2"], "L1_b1": g["L1_gnn_b1"].reshape(D, 1), "L1_c1": g["L1_gnn_c1"].reshape(D, 1),
        "L1_b2": g["L1_gnn_b2"], "L1_c2": g["L1_gnn_c2"],
        "L2_emb": g["L2_gnn_W_emb"], "L2_W1a": block(g["L2_gnn_W1"], 0, 0), "L2_W1b": block(g["L2_gnn_W1"], 0, 1),
        "L2_W2a": block(g["L2_gnn_W2"], 0, 0), "L2_W2b": block(g["L2_gnn_W2"], 1, 0), "L2_b_emb": g["L2_gnn_b_emb"],
        "L2_b1a": g["L2_gnn_b1"][:D], "L2_b1b": g["L2_gnn_b1"][D:], "L2_b2": g["L2_gnn_b2"],
        "L2_src0": g["L2_gnn_att_src1"][0], "L2_dst0": g["L2_gnn_att_dst1"][0],
        "L2_src1": g["L2_gnn_att_src1"][1], "L2_dst1": g["L2_gnn_att_dst1"][1],
        "L2_src2": g["L2_gnn_att_src2"][0], "L2_dst2": g["L2_gnn_att_dst2"][0],
        "L3_Wl1": g["L3_gnn_Wl1"], "L3_Wr1": g["L3_gnn_Wr1"], "L3_Wl2": g["L3_gnn_Wl2"], "L3_Wr2": g["L3_gnn_Wr2"],
        "L3_bl1": g["L3_gnn_bl1"], "L3_bl2": g["L3_gnn_bl2"],
    }
    arrays = {f"in_{k}": np.ascontiguousarray(v) for k, v in arrays.items()}
    nc = bacc.Bacc("TRN2", target_bir_lowering=False, num_devices=1)
    a = {k[3:]: nc.dram_tensor(k, v.shape, mybir.dt.from_np(v.dtype), kind="ExternalInput").ap() for k, v in arrays.items()}
    out = nc.dram_tensor("out", (N, D), f32, kind="ExternalOutput").ap()
    gnn(nc, a, out)
    r = run_bass_kernel_spmd(nc, [arrays], core_ids=[0])
    return r.results[0]["out"]
```

```python
from contextlib import ExitStack

import numpy as np
import concourse.bass as bass
from concourse import mybir

N, D, E = 3125, 128, 53125
P = 125
W = N // P
EDGES = 128
TILES = -(-E // EDGES)
STEPS = TILES + W - 1
SK, SJ = 110, 4
Q = 20
QW = -(-N // Q)
NP = QW * Q
CSTEPS = TILES + QW - 1
CK, CJ = 52, 11
GCN_ROUNDS, GCN_STEPS, CNT_PER_ROUND = 44, 10, 13
TABLES = 5
GE = TABLES * EDGES
MSG_ROUNDS, MSG_SLOTS, HALF = 55, 8, 4
SUM_BANKS = (1, 2, 3, 6)
POOL_SLOTS = (1,)
GROUP = 5
GROUPS = W // GROUP
GC = GROUP * P
KEEP = 12
BIG = 3.0e38
SLOPE = 0.2
assert SK * SJ == STEPS == GCN_ROUNDS * GCN_STEPS == MSG_ROUNDS * MSG_SLOTS
assert CK * CJ == CSTEPS == GCN_ROUNDS * CNT_PER_ROUND and W * Q <= 512 and GCN_STEPS == 2 * TABLES

f32, i32, f16, bf16 = mybir.dt.float32, mybir.dt.int32, mybir.dt.float16, mybir.dt.bfloat16
ALU = mybir.AluOpType
ACT = mybir.ActivationFunctionType
AX = mybir.AxisListType
RMAX = bass.bass_isa.ReduceOp.max

STAGES = (("steps", SJ), ("counts", CJ),
          ("gcn_hT", GROUPS), ("gcn_aT", GROUPS), ("gcn_out", GROUPS),
          ("msg_hT", GROUPS), ("msg_P", GROUPS), ("msg_Q", GROUPS),
          ("msg_aT", GROUPS), ("msg_u", GROUPS), ("msg_out", GROUPS),
          ("gat_hT", GROUPS), ("gat_emb", GROUPS), ("gat_eT", GROUPS), ("gat_x0", GROUPS), ("gat_x1", GROUPS),
          ("rows0", 1), ("rows1", 1),
          ("gat_o0T", GROUPS), ("gat_o1T", GROUPS), ("gat_x2", GROUPS), ("rows2", 1),
          ("sage1_aT", GROUPS), ("sage1_hT", GROUPS), ("sage1_out", GROUPS),
          ("sage2_aT", GROUPS), ("sage2_hT", GROUPS), ("sage2_out", GROUPS))


def before(stage):
    n = 0
    for name, rounds in STAGES:
        if name == stage:
            return n
        n += rounds
    raise KeyError(stage)


def after(stage):
    return before(stage) + dict(STAGES)[stage]


def gnn(nc, a, out):
    ctx = ExitStack()
    with ctx:
        def sb(name, shape, dt=f32):
            return ctx.enter_context(nc.sbuf_tensor(name, shape, dt))

        sems = {}

        def sig(name):
            if name not in sems:
                sems[name] = ctx.enter_context(nc.semaphore(name))
            return sems[name]

        def dram(name, shape, dt=f32):
            return nc.dram_tensor(name, shape, dt).ap()

        win_d, cwin_d = dram("win_d", [STEPS], i32), dram("cwin_d", [CSTEPS], i32)
        dl_d, pen_d, w_d, src_d = (dram(n, [STEPS, EDGES]) for n in ("dl_d", "pen_d", "w_d", "src_d"))
        sum_d = [dram(f"sum{n}_d", [N + EDGES, D]) for n in range(TABLES)]
        x_d = dram("x_d", [N, D])
        h0_d, p_d = dram("h0_d", [N, D]), dram("p_d", [N, D])
        h3_d, g3_d = dram("h3_d", [N, D]), dram("g3_d", [N, D])
        xw1_d = dram("xw1_d", [N, D])
        o_d = [dram(f"o{n}_d", [N, D]) for n in range(3)]
        rows_d = [dram(f"rows{n}_d", [2, N]) for n in range(3)]
        agg_d = [dram(f"agg{n}_d", [N, D]) for n in range(2)]
        k_d = dram("k_d", [P, (W - KEEP) * NP // 2])

        def nodes(ap):
            return ap.rearrange("(w p) d -> p w d", p=P)

        K = sb("K", [128, W, NP], f16)
        U = sb("U", [128, 11100])
        ident = sb("ident", [128, 128])
        ramp = sb("ramp", [128, 128])
        keys = sb("keys", [128, W * Q], f16)
        pidx = sb("pidx", [128, 1])
        wts = sb("wts", [128, 8, D])
        bias = sb("bias", [128, 9, D])
        bcol = sb("bcol", [128, 2])
        scal = sb("scal", [128, 16])
        carry = sb("carry", [128, 1])
        index = sb("index", [128, GCN_STEPS], i32)
        rowv_all = sb("rowv", [128, 4 * W])
        rowv = rowv_all[0:P].rearrange("p (a w) -> p a w", a=4)
        KA = K[:, KEEP:, :].rearrange("p b d -> p (b d)").bitcast(f32)

        def carve(arena, words):
            at = [0]

            def take(*shape, dt=f32):
                size = int(np.prod(shape))
                need = size if dt in (f32, i32) else -(-size // 2)
                assert at[0] + need <= words, (at[0], need, words)
                v = arena[:, at[0]:at[0] + need]
                at[0] += need
                if dt is not f32:
                    v = v.bitcast(dt)[:, 0:size]
                if len(shape) == 2:
                    v = v.rearrange("p (a b) -> p a b", a=shape[0])
                elif len(shape) == 3:
                    v = v.rearrange("p (a b c) -> p a b c", a=shape[0], b=shape[1])
                return v
            return take

        UWORDS, KWORDS = 11100, (W - KEEP) * NP // 2
        take = carve(U, UWORDS)
        SRC = take(STEPS, dt=i32)
        LAST = take(STEPS)
        IK, CIK = take(STEPS, dt=i32), take(CSTEPS, dt=i32)
        SRCF = take(STEPS)
        WT = take(STEPS)
        KEY, SLO = take(CSTEPS, dt=f16), take(CSTEPS, dt=f16)
        HN = take(W, D)
        dst_hot = [take(GE) for _ in range(2)]
        src_row = [take(GE) for _ in range(2)]
        rows = take(TABLES, D)
        slohot = take(2, 128, dt=f16)
        cnt = take(3, W * Q, dt=f16)
        take = carve(U, UWORDS)
        take(3 * STEPS + CSTEPS)
        macc = take(W, D + 1)
        MG = take(MSG_SLOTS, D)
        lasthot = take(MSG_SLOTS, P)
        Qc = take(MSG_SLOTS, D)
        take = carve(wts[:, :, :].rearrange("p a b -> p (a b)"), 8 * D)
        picked = take(2, D)
        earlier = take(EDGES)
        khot = take(2, W * Q, dt=f16)
        take = carve(rowv_all, 4 * W)
        take(2 * W)
        again, spare = take(TABLES), take(1)
        take = carve(KA, KWORDS)
        X, H, Y, T, HT, QU = (take(W * D) for _ in range(6))
        w3 = lambda v: v.rearrange("p (w d) -> p w d", w=W)
        mrhs = [Y[:, n * 512:(n + 1) * 512] for n in range(2)]
        dlb = [Y[:, (2 + n) * 512:(3 + n) * 512] for n in range(2)]
        penb = [Y[:, (4 + n) * 512:(5 + n) * 512] for n in range(2)]
        relu, scan = T[:, 0:512], T[:, 512:1024]
        back = T[:, 1024:1024 + HALF * (D + 1)].rearrange("p (s c) -> p s c", s=HALF)
        take = carve(KA, KWORDS)
        st_i = take(SJ, 4 * EDGES, dt=i32)
        st_w = take(SJ, EDGES)
        st_f = [take(SJ, EDGES) for _ in range(4)]
        ct_i = take(CJ, 2 * EDGES, dt=i32)
        ct_f = [take(CJ, EDGES) for _ in range(5)]
        ct_q = take(CJ, EDGES, dt=i32)
        tl_i = take(TILES, dt=i32)
        tl_f = [take(TILES) for _ in range(5)]
        tl_q = take(TILES, dt=i32)
        stp = take(SJ, 6)
        ctp = take(CJ, 6)
        stp_i, ctp_i = take(2, SJ, dt=i32), take(2, CJ, dt=i32)
        take = carve(U, UWORDS)
        xw = take(W, D + 1)
        cols = take(12, W)
        AB = [take(2, GC) for _ in range(2)]
        zs = take(GROUP, GC)
        yg = take(GROUP, D)
        att = take(2, D)
        take = carve(U, UWORDS)
        take(W * (D + 1) + 12 * W + 4 * GC)
        ATT_T = take(W * D)
        macc_att = ATT_T[:, 0:N]
        take = carve(U, UWORDS)
        V1, V2, V3 = take(W * (D + 1)), take(W * D), take(N)
        hs1 = U[:, 0:W * (3 * D + 2) // 2].bitcast(bf16).rearrange("p (w c) -> p w c", w=W)
        hs2 = U[:, UWORDS - W * (3 * D + 2) // 2:UWORDS].bitcast(bf16).rearrange("p (w c) -> p w c", w=W)
        S1, S2 = U[:, 0:W * D], U[:, W * D:2 * W * D]
        S3 = U[:, 2 * W * D:2 * W * D + N]
        H3 = U[:, UWORDS - W * D:UWORDS]
        sg0 = U[:, 5000:5000 + GROUP * D].rearrange("p (w d) -> p w d", w=GROUP)
        sg1 = U[:, 0:GROUP * D].rearrange("p (w d) -> p w d", w=GROUP)
        PS = ctx.enter_context(nc.psum_tensor("PS", [128, 8, 512], f32))
        pairs_of_banks = [PS[:, n:n + 2, :].rearrange("p b (j c) -> p (b j) c", c=128) for n in (0, 6)]

        def mm_of(n):
            return pairs_of_banks[n % 2]


        KB = K[:, 0:KEEP, :].rearrange("p b d -> p (b d)").bitcast(f32)
        take = carve(KB, KEEP * NP // 2)
        X0, T0 = (take(W * D) for _ in range(2))
        H0 = HN[:, :, :].rearrange("p w d -> p (w d)")
        gathered = [sig(f"gathered{n}") for n in range(MSG_SLOTS)]
        tabled = [sig(f"tabled{n}") for n in range(TABLES)]
        block = ctx.enter_context(nc.Block())

        def wide(v):
            return v[0:P, 0:W * D].rearrange("p (w d) -> p w d", w=W)

        def over_features(v):
            return v.unsqueeze(2).to_broadcast([P, W, D])

        def over_windows(v):
            return v.unsqueeze(1).to_broadcast([P, W, D])

        @block.sync
        def _(sp):
            def loads(name, *pairs):
                for dst, src in pairs:
                    sp.dma_start(dst, src).then_inc(sig(name), 16)

            loads("x_in", (wide(X0), nodes(a["x"])))
            loads("sched_in", (tl_i[0:SK], a["last"].partition_broadcast(SK)),
                  (tl_f[3][0:SK], a["tiles"].partition_broadcast(SK)))
            loads("consts_in", (pidx[:, :], a["pidx"]), (ident[:, :], a["ident"]), (earlier, a["earlier"]),
                  (spare, a["spare"]), (keys[:, :], a["keys"]), (ramp[:, :], a["ramp"]))
            sp.wait_ge(sig("bias_zero"), 1)
            for t in range(TABLES):
                for w0 in range(0, W, 9):
                    w1 = min(w0 + 9, W)
                    loads("tables_zero", (sum_d[t][w0 * P:w1 * P].rearrange("(w p) d -> p w d", p=P), bias[0:P, 0:w1 - w0]))
            sp.wait_ge(sig("windows_made"), 2)
            loads("windows_out", (win_d.rearrange("(p j) -> p j", p=SK), stp_i[0:SK, 1, :]),
                  (cwin_d.rearrange("(p j) -> p j", p=CK), ctp_i[0:CK, 1, :]))
            sp.wait_ge(sig("windows_out"), 32)
            loads("windows_in", (IK[0:1], win_d.unsqueeze(0)), (CIK[0:1], cwin_d.unsqueeze(0)))
            sp.wait_ge(sig("h_made"), 1)
            loads("h0_out", (nodes(h0_d), wide(H0)))
            sp.wait_ge(sig("step_rows"), 1)
            by_step = lambda v: v.rearrange("(p j) e -> p j e", p=SK)
            loads("rows_out", (by_step(dl_d), st_f[0][0:SK]), (by_step(pen_d), st_f[2][0:SK]),
                  (by_step(w_d), st_w[0:SK]),
                  (by_step(src_d), st_f[3][0:SK]))

            def edge_rows(q, half):
                part = lambda v: v[bass.ds(q * TABLES, TABLES), :].rearrange("s e -> (s e)")
                sp.dma_start(dst_hot[half][0:P], part(dl_d).partition_broadcast(P)).then_inc(sig(f"edges_in{half}"), 16)
                sp.dma_start(src_row[half], part(src_d).partition_broadcast(128)).then_inc(sig(f"edges_in{half}"), 16)

            sp.wait_ge(sig("rows_out"), 64)
            for half in range(2):
                edge_rows(half, half)
            with sp.Fori(1, GCN_ROUNDS) as r:
                for half in range(2):
                    sp.wait_ge(sig("summed"), r * GCN_STEPS + half * TABLES)
                    sp.sem_inc(sig("half_seen"), 1)
                    sp.wait_ge(sig("index_ready"), r * 2 + half)
                    edge_rows(r * 2 + half, half)

            def region(n):
                return slice(n * W * D, (n + 1) * W * D if n < 5 else KWORDS)

            sp.wait_ge(sig("cnt_added"), CSTEPS + 2)
            for n in (4, 2, 3, 1, 0, 5):
                loads(f"k_out{n}", (k_d[:, region(n)], KA[0:P, region(n)]))
            sp.wait_ge(sig("summed"), STEPS + TABLES)
            blocks = ["L0_a", "L0_b_w", "L1_src", "L1_dst", "L1_W2", "L1_U1a", "L1_U1b", "L1_U2"]
            loads("wts_in", *[(wts[:, n, :], a[b]) for n, b in enumerate(blocks)])
            vectors = ["L0_b", "L1_b2", "L1_c2", "L2_b_emb", "L2_b1a", "L2_b1b", "L2_b2", "L3_bl1", "L3_bl2"]
            loads("wts_in", *[(bias[0:P, n, :], a[b].partition_broadcast(P)) for n, b in enumerate(vectors)])
            loads("wts_in", (bcol[:, 0:1], a["L1_b1"]), (bcol[:, 1:2], a["L1_c1"]))

            for t in range(TABLES):
                sp.wait_ge(tabled[t], 16 * (STEPS // TABLES + 2))
            sp.wait_ge(sig("k_out2"), 16)
            loads("nb0_in", (wide(Y), nodes(sum_d[0][0:N])))
            for t in range(1, TABLES):
                if t > 2:
                    sp.wait_ge(sig("nb_added"), t - 2)
                else:
                    sp.wait_ge(sig(f"k_out{(3, 1)[t - 1]}"), 16)
                loads(f"nb{t}_in", (wide((H, T)[t % 2]), nodes(sum_d[t][0:N])))
            sp.wait_ge(sig("k_out0"), 16)
            loads("x_in", (wide(X), nodes(a["x"])))
            sp.wait_ge(sig("k_out5"), 16)
            loads("qrow_in", (QU[P:P + 1].rearrange("p (w d) -> p w d", w=W),
                              a["L1_wrow"].unsqueeze(1).to_broadcast([1, W, D])))
            sp.wait_ge(sig("dense_copied"), after("msg_P"))
            loads("p_out", (nodes(p_d), wide(Y)))

            def message_rows(q, half):
                part = lambda v: v[bass.ds(q * HALF, HALF), :].rearrange("s e -> (s e)")
                sp.dma_start(dlb[half][0:P], part(dl_d).partition_broadcast(P)).then_inc(sig(f"rows_in{half}"), 16)
                sp.dma_start(mrhs[half][P:P + 1], part(w_d).unsqueeze(0)).then_inc(sig(f"rows_in{half}"), 16)

            def segment_rows(q, half):
                sp.dma_start(penb[half], pen_d[bass.ds(q * HALF, HALF), :].rearrange("s e -> (s e)")
                             .partition_broadcast(128)).then_inc(sig(f"pen_in{half}"), 16)

            sp.wait_ge(sig("p_out"), 16)
            for half in range(2):
                message_rows(half, half)
                segment_rows(half, half)
            with sp.Fori(1, MSG_ROUNDS) as r:
                for half in range(2):
                    sp.wait_ge(sig("pre_ready"), r * 2 + (half - 1))
                    message_rows(r * 2 + half, half)
                    sp.wait_ge(sig("scan_ready"), r * 2 + half)
                    segment_rows(r * 2 + half, half)

            sp.wait_ge(sig("msg_ready"), MSG_ROUNDS * 2 + 1)
            later = ["L2_emb", "L2_W1a", "L2_W1b", "L2_W2a", "L2_W2b"]
            loads("wts2_in", *[(wts[:, n, :], a[b]) for n, b in enumerate(later)])
            sp.wait_ge(sig("x2_made"), 1)
            loads("x_out", (nodes(x_d), wide(X)))
            for n, stage in ((5, "msg_out"), (4, "gat_emb"), (2, "gat_eT"), (0, None), (3, "gat_x1")):
                if stage:
                    sp.wait_ge(sig("dense_copied"), after(stage))
                else:
                    sp.wait_ge(sig("x_out"), 16)
                loads("k_in", (KA[0:P, region(n)], k_d[:, region(n)]))
            loads("xw_out", (nodes(xw1_d), wide(H)))
            sp.wait_ge(sig("xw_out"), 16)
            loads("k_in", (KA[0:P, region(1)], k_d[:, region(1)]))
            loads("wts3_in", *[(wts[:, 5 + n, :], a[b]) for n, b in enumerate(("L3_Wl1", "L3_Wr1", "L3_Wl2"))])

            def store_out(sp, u, g):
                sp.wait_ge(sig("outs_free"), u * GROUPS + g + 1)
                loads("o_out", (o_d[u][g * GC:(g + 1) * GC, :].rearrange("(w p) d -> p w d", p=P), yg[0:P]))

            for u in range(3):
                if u == 1:
                    sp.wait_ge(sig("outs_ready"), GROUPS * u)
                    loads("xw_in", (xw[0:P, :, 0:D], nodes(xw1_d)))
                if u:
                    sp.wait_ge(sig("outs_free"), GROUPS * u)
                loads("att_in", *[(att[0:P, n, :], a[b].partition_broadcast(P))
                                  for n, b in enumerate((f"L2_src{u}", f"L2_dst{u}"))])
                sp.wait_ge(sig("dense_copied"), after(f"rows{u}"))
                loads("rowsAB_out", (rows_d[u].rearrange("a (w p) -> (a w) p", p=P),
                                     yg[0:2 * W].rearrange("p a b -> p (a b)")[:, 0:P]))
                sp.wait_ge(sig("rowsAB_out"), 16 * (u + 1))
                for g in range(GROUPS):
                    if g > 1:
                        sp.wait_ge(sig("min_ready"), (u * GROUPS + g - 1) * W)
                    loads(f"ab_in{g % 2}", (AB[g % 2][0:P], rows_d[u][:, g * GC:(g + 1) * GC].unsqueeze(0).to_broadcast([P, 2, GC])))
                    if g > 1:
                        store_out(sp, u, g - 2)
                store_out(sp, u, GROUPS - 2)
                store_out(sp, u, GROUPS - 1)
                if u == 1:
                    sp.wait_ge(sig("o_out"), 16 * 2 * GROUPS)
                    loads("o_in", (wide(V1), nodes(o_d[0])))
                    sp.wait_ge(sig("dense_copied"), after("gat_o0T"))
                    loads("o_in", (wide(V1), nodes(o_d[1])))
            sp.wait_ge(sig("dense_copied"), after("gat_x2"))
            loads("wts4_in", (wts[:, 0, :], a["L3_Wr2"]))
            sp.wait_ge(sig("o_out"), 16 * 3 * GROUPS)
            loads("x3_in", (wide(S1), nodes(x_d)), (wide(H3), nodes(o_d[2])))
            sp.wait_ge(sig("x3_made"), 1)
            loads("x3_out", (nodes(x_d), wide(S1)))
            sp.wait_ge(sig("h_made"), 4)
            loads("h3_out", (nodes(h3_d), wide(H3)))

            for v in range(2):
                for g in range(GROUPS):
                    sp.wait_ge(sig("sg_ready"), GROUP * (v * GROUPS + g + 2))
                    loads("agg_out", (agg_d[v][g * GC:(g + 1) * GC, :].rearrange("(w p) d -> p w d", p=P),
                                      (sg0, sg1)[v][0:P]))
                sp.wait_ge(sig("agg_out"), 16 * GROUPS * (v + 1) + 1)
                loads("s_in", (wide(S1), nodes(agg_d[v])))
                sp.wait_ge(sig("dense_copied"), after(f"sage{v + 1}_aT"))
                loads("s_in", (wide(S1), nodes((h3_d, g3_d)[v])))
                if v == 0:
                    sp.wait_ge(sig("g3_made"), 1)
                    loads("g3_out", (nodes(g3_d), wide(S1)))
            sp.wait_ge(sig("dense_copied"), after("sage2_out"))
            loads("x4_in", (wide(S2), nodes(x_d)))
            sp.wait_ge(sig("x4_made"), 1)
            loads("stored", (nodes(out), wide(S1)))
            sp.wait_ge(sig("stored"), 16)

        @block.gpsimd
        def _(pool):
            for name, free in (("msg_used", MSG_SLOTS), ("sums_added", HALF),
                               ("csum_ready", 2), ("cnt_copied", 2), ("cnt_added", 2), ("z_used", GROUP), ("sg_ready", GROUP),
                               ("picked_ready", 2), ("picked_copied", 2), ("summed", TABLES), ("rows_ready", 2), ("agg_out", 1),
                               ("relu_done", 1), ("msg_ready", 1), ("scan_ready", 1), ("back_ready", 1),
                               ("back_copied", 1), ("carried", 1), ("index_ready", 1), ("sums_ready", 1)):
                pool.sem_inc(sig(name), free)
            pool.wait_ge(sig("bias_zero"), 1)
            for t in range(TABLES):
                for half in range(2):
                    rows_ = slice(half * EDGES // 2, (half + 1) * EDGES // 2)
                    pool.dma_start(sum_d[t][N:][rows_], bias[rows_, 0, :]).then_inc(tabled[t], 16)

            def gather(dst, rows, index, sem):
                pool.indirect_dma_start(dst, None, rows, bass.IndirectOffsetOnAxis(ap=index, axis=0)).then_inc(sem, 16)

            pool.wait_ge(sig("windows_made"), 2)
            for j in range(SJ):
                gather(st_i[0:SK, j, :], a["edges"], stp_i[0:SK, 0, j:j + 1], sig("tiles_in"))
                gather(st_w[0:SK, j, :], a["weights"], stp_i[0:SK, 0, j:j + 1], sig("tiles_in"))
            for j in range(CJ):
                gather(ct_i[0:CK, j, :], a["ends"], ctp_i[0:CK, 0, j:j + 1], sig("ctiles_in"))
            pool.wait_ge(sig("h0_out"), 16)
            pool.memset(KB, 0.0).then_inc(sig("k_zero"), 1)

            pool.wait_ge(sig("tables_zero"), 16 * 3 * TABLES)
            with pool.Fori(0, GCN_ROUNDS) as r:
                for half in range(2):
                    for t in range(TABLES):
                        k = r * GCN_STEPS + (half * TABLES + t)
                        pool.wait_ge(sig("rows_ready"), k + 3)
                        pool.wait_ge(tabled[t], r * 32 + 16 * (half + 2))
                        pool.wait_ge(sig("index_ready"), r * 2 + (half + 2))
                        pool.sem_inc(sig("row_seen"), 1)
                        pool.indirect_dma_start(sum_d[t], bass.IndirectOffsetOnAxis(ap=index[:, half * TABLES + t:half * TABLES + (t + 1)], axis=0),
                                                rows[:, t, :], None, compute_op=ALU.add).then_inc(tabled[t], 16)

            pool.wait_ge(sig("p_out"), 16)
            with pool.Fori(0, MSG_ROUNDS) as r:
                for half in range(2):
                    k = r * MSG_SLOTS + half * HALF
                    pool.wait_ge(sig("msg_used"), k + HALF)
                    pool.tensor_copy(index[:, half * HALF:(half + 1) * HALF], SRC[:, bass.ds(k, HALF)])\
                        .then_inc(sig("index_copied"), 1)
                    pool.wait_ge(sig("index_copied"), r * 2 + (half + 1))
                    pool.sem_inc(sig("index_seen"), 1)
                    for n in range(half * HALF, (half + 1) * HALF):
                        gather(MG[:, n, :], p_d, index[:, n:n + 1], gathered[n])
            for u in range(3):
                pool.wait_ge(sig("range_in"), u + 1)
                pool.partition_all_reduce(scal[0:P, 2:4], scal[0:P, 0:2], P, RMAX).then_inc(sig("range_out"), 1)
                for g in range(GROUPS):
                    with pool.Fori(0, GROUPS) as q:
                        for i in POOL_SLOTS:
                            pool.wait_ge(sig("exp_ready"), q * GROUP + (u * W * GROUPS + g * W + i + 1))
                            nc.gpsimd.tensor_tensor(zs[0:P, i, :], zs[0:P, i, :],
                                                    K[0:P, bass.ds(q * GROUP + i, 1), g * GC:(g + 1) * GC]
                                                    .rearrange("p a d -> p (a d)"), ALU.mult).then_inc(sig("pool_z_ready"), 1)

        @block.scalar
        def _(act):
            def copy_round(n, pairs, func=ACT.Copy, **kw):
                act.wait_ge(sig("dense_ready"), n + 1)
                for dst, src in pairs:
                    ins = nc.scalar.activation(dst, src(mm_of(n)), func, **kw)
                ins.then_inc(sig("dense_copied"), 1)

            def turned(stage, dst):
                for g in range(GROUPS):
                    copy_round(before(stage) + g,
                               [(dst[:, g * GC:(g + 1) * GC].rearrange("p (w n) -> p w n", w=GROUP), lambda mm: mm[:, 0:GROUP, 0:P])])

            def straight(stage, dst):
                for g in range(GROUPS):
                    copy_round(before(stage) + g, [(dst[0:P, g * GROUP:(g + 1) * GROUP, 0:D], lambda mm: mm[0:P, 0:GROUP, :])])

            def roots(n):
                act.wait_ge(sig("root_in"), n)
                nc.scalar.activation(rowv[:, 1, :], rowv[:, 1, :], ACT.Sqrt).then_inc(sig("root_out"), 1)

            roots(1)
            for j in range(SJ):
                copy_round(before("steps") + j, [(dst.rearrange("p (k j) -> p j k", j=SJ)[:, j, :], lambda mm, i=i: mm[:, i, 0:SK])
                                                 for i, dst in enumerate((SRC, SRCF, LAST, WT))])
            for j in range(CJ):
                copy_round(before("counts") + j, [(dst.rearrange("p (k j) -> p j k", j=CJ)[:, j, :], lambda mm, i=i: mm[:, i, 0:CK])
                                                  for i, dst in enumerate((KEY, SLO))])

            with act.Fori(0, GCN_ROUNDS) as r:
                def picked_copy(s):
                    k = r * GCN_STEPS + s
                    act.wait_ge(sig("picked_ready"), k + 3)
                    act.wait_ge(sig("summed"), k + (TABLES - 1))
                    nc.scalar.activation(picked[:, s % 2, :], PS[:, 2 + s % 2, 0:D], ACT.Copy,
                                         scale=WT[:, bass.ds(k, 1)])\
                        .then_inc(sig("picked_copied"), 1)

                def row_copy(s):
                    k = r * GCN_STEPS + s
                    act.wait_ge(sig("summed"), k + (TABLES + 1))
                    act.wait_ge(tabled[s % TABLES], r * 32 + 16 * (s // TABLES + 2))
                    nc.scalar.activation(rows[:, s % TABLES, :], PS[:, 6 + s % 2, 0:D], ACT.Copy)\
                        .then_inc(sig("rows_ready"), 1)

                for j in range(CNT_PER_ROUND):
                    m = r * CNT_PER_ROUND + j
                    act.wait_ge(sig("csum_ready"), m + 3)
                    act.wait_ge(sig("cnt_added"), m + (0 if j else 2))
                    nc.scalar.activation(cnt[0:P, j % 3, :], PS[0:P, 4 + j % 2, 0:W * Q], ACT.Copy)\
                        .then_inc(sig("cnt_copied"), 1)
                    if 2 <= j < 2 + GCN_STEPS:
                        picked_copy(j - 2)
                    if 3 <= j < 3 + GCN_STEPS:
                        row_copy(j - 3)

            act.wait_ge(sig("k_out4"), 16)
            turned("gcn_hT", HT)
            turned("gcn_aT", T)
            straight("gcn_out", wide(Y))
            roots(2)
            roots(3)
            turned("msg_hT", HT)
            straight("msg_P", wide(Y))
            act.wait_ge(sig("k_out5"), 16)
            straight("msg_Q", wide(QU))

            act.wait_ge(sig("qrow_in"), 16)
            act.wait_ge(sig("windows_in"), 32)
            act.wait_ge(sig("macc_zero"), 1)
            def windows_act(r):
                return nc.values_load_multi_w_load_instructions(
                    IK[0:1, bass.ds(r * MSG_SLOTS, MSG_SLOTS)], engines=[mybir.EngineType.Activation], min_val=0, max_val=W - 1,
                    skip_runtime_bounds_check_because="steps' windows lie in this range by their construction")[1]

            def projections(window, half):
                for s in range(HALF):
                    n = half * HALF + s
                    nc.scalar.activation(Qc[0:P + 1, n, :], QU[0:P + 1].rearrange("p (w d) -> p w d", w=W)
                                         [:, bass.ds(window[n], 1), :].rearrange("p a d -> p (a d)"), ACT.Copy)\
                        .then_inc(sig("q_copied"), 1)

            def relu_half(r, half):
                act.wait_ge(sig("pre_ready"), r * 2 + (half + 1))
                act.wait_ge(sig("msg_ready"), r * 2 + (half + 1))
                nc.scalar.activation(relu, PS[:, 4, :], ACT.Relu, bias=bcol[:, 0:1]).then_inc(sig("relu_done"), 1)

            def copy_back(r, half):
                act.wait_ge(sig("back_ready"), r * 2 + (half + 2))
                act.wait_ge(sig("sums_ready"), r * MSG_SLOTS + (half * HALF + 1))
                nc.scalar.activation(back[:, :, 0:D], PS[:, 0, :].rearrange("p (s d) -> p s d", s=HALF), ACT.Copy)\
                    .then_inc(sig("back_copied"), 1)

            window = windows_act(0)
            projections(window, 0)
            projections(window, 1)
            relu_half(0, 0)
            with act.Fori(0, MSG_ROUNDS - 1) as r:
                window = windows_act(r + 1)
                for half, after_ in ((0, (r, 1)), (1, (r + 1, 0))):
                    projections(window, half)
                    relu_half(*after_)
                    copy_back(r, half)
            relu_half(MSG_ROUNDS - 1, 1)
            copy_back(MSG_ROUNDS - 1, 0)
            copy_back(MSG_ROUNDS - 1, 1)

            turned("msg_aT", T)
            for g in range(GROUPS):
                copy_round(before("msg_u") + g,
                           [(QU[:, g * GC:(g + 1) * GC].rearrange("p (w n) -> p w n", w=GROUP), lambda mm: mm[:, 0:GROUP, 0:P])],
                           ACT.Relu, bias=bcol[:, 1:2])
            straight("msg_out", wide(Y))
            roots(4)
            turned("gat_hT", HT)
            straight("gat_emb", wide(Y))
            turned("gat_eT", T)
            straight("gat_x0", xw)
            straight("gat_x1", wide(H))

            for u in range(3):
                copy_round(before(f"rows{u}"), [(yg[0:2 * W].rearrange("p a b -> p (a b)")[:, 0:P],
                                                 lambda mm: mm[0:2 * W, 0, 0:P])])
                def exponential(g, q, c):
                    b = q * GROUP + c
                    act.wait_ge(sig("min_ready"), q * GROUP + (u * W * GROUPS + g * W + c + 1))
                    nc.scalar.activation(zs[0:P, c, :], zs[0:P, c, :], ACT.Relu, bias=cols[0:P, 10, bass.ds(b, 1)])\
                        .then_inc(sig("held"), 1)
                    act.wait_ge(sig("held"), q * GROUP + (u * W * GROUPS + g * W + c + 1))
                    nc.scalar.activation(zs[0:P, c, :], zs[0:P, c, :], ACT.Exp, scale=-1.0).then_inc(sig("exp_ready"), 1)

                for g in range(GROUPS):
                    with act.Fori(0, GROUPS) as q:
                        for c in range(GROUP):
                            exponential(g, q, c)
                if u == 1:
                    for n, dst in enumerate((V3, V2)):
                        act.wait_ge(sig("elu_in"), n + 1)
                        nc.scalar.activation(V2[0:P], V2[0:P], ACT.Exp).then_inc(sig("elu_out"), 1)
                        turned(f"gat_o{n}T", dst)
                    straight("gat_x2", xw)
            roots(5)
            for v in range(2):
                with act.Fori(0, GROUPS) as g:
                    for w in range(GROUP):
                        i = g * GROUP + (v * W + w)
                        act.wait_ge(sig("sage_ready"), i + 1)
                        if w == 0:
                            act.wait_ge(sig("agg_out"), g * 16 + (v * GROUPS * 16 + 1))
                        nc.scalar.activation((sg0, sg1)[v][0:P, w, :], PS[0:P, 3 + w, 2 * D:3 * D], ACT.Copy)\
                            .then_inc(sig("third_copied"), 1)
                turned(f"sage{v + 1}_aT", S2)
                turned(f"sage{v + 1}_hT", S3)
                straight(f"sage{v + 1}_out", wide(S1))

        @block.vector
        def _(dve):
            v_ = nc.vector
            step = sig("dve_step")
            done = [0]

            def link(ins):
                done[0] += 1
                ins.then_inc(step, 1)
                dve.wait_ge(step, done[0])

            def root(n, out):
                dve.wait_ge(sig("root_out"), n)
                if out is not None:
                    link(v_.tensor_scalar_max(rowv[:, 1, :], rowv[:, 1, :], out))
                link(v_.reciprocal(rowv[:, 1, :], rowv[:, 1, :]))

            def normalise(x, h, t, n):
                link(v_.tensor_reduce(rowv[:, 0, :], x, AX.X, ALU.add))
                link(v_.tensor_scalar_mul(rowv[:, 0, :], rowv[:, 0, :], 1.0 / D))
                link(v_.tensor_tensor(h, x, over_features(rowv[:, 0, :]), ALU.subtract))
                link(v_.tensor_tensor(t, h, h, ALU.mult))
                link(v_.tensor_reduce(rowv[:, 1, :], t, AX.X, ALU.add))
                v_.tensor_scalar(rowv[:, 1, :], rowv[:, 1, :], 1.0 / D, 1e-5, ALU.mult, ALU.add)\
                    .then_inc(sig("root_in"), 1)
                root(n, None)
                link(v_.tensor_tensor(h, h, over_features(rowv[:, 1, :]), ALU.mult))
                v_.tensor_scalar_max(h, h, 0.0).then_inc(sig("h_made"), 1)

            v_.memset(bias[:, :, :], 0.0).then_inc(sig("bias_zero"), 1)
            dve.wait_ge(sig("x_in"), 16)
            normalise(wide(X0), wide(H0), wide(T0), 1)

            def quotient(q, v, by, r, qi):
                link(v_.tensor_scalar_mul(qi, v, 1.0 / by))
                link(v_.tensor_copy(q, qi))
                link(v_.scalar_tensor_tensor(r, q, -float(by), v, ALU.mult, ALU.add))
                link(v_.scalar_tensor_tensor(q, r, 0.0, q, ALU.is_ge, ALU.add))
                link(v_.scalar_tensor_tensor(q, r, float(by), q, ALU.is_ge, ALU.add))
                link(v_.tensor_scalar_add(q, q, -1.0))

            dve.wait_ge(sig("sched_in"), 32)
            dve.wait_ge(sig("consts_in"), 96)
            link(v_.tensor_copy(tl_f[0][0:SK], tl_i[0:SK]))
            for size, windows, sk, sj, sp_, spi in ((P, W, SK, SJ, stp, stp_i), (Q, QW, CK, CJ, ctp, ctp_i)):
                quotient(tl_f[1][0:sk], tl_f[0][0:sk], size, tl_f[2][0:sk], tl_q[0:sk])
                link(v_.scalar_tensor_tensor(tl_f[1][0:sk], tl_f[1][0:sk], float(windows - 1), tl_f[3][0:sk],
                                             ALU.min, ALU.add))
                for j in range(sj):
                    link(v_.tensor_scalar(sp_[0:sk, j, 0:1], pidx[0:sk], float(sj), float(j), ALU.mult, ALU.add))
                    link(v_.tensor_scalar(tl_f[4][0:sk], tl_f[1][0:sk], sp_[0:sk, j, 0:1], None, ALU.is_lt))
                    link(v_.tensor_reduce(sp_[0:sk, j, 1:2], tl_f[4][0:sk], AX.X, ALU.add))
                link(v_.tensor_tensor(sp_[0:sk, :, 2], sp_[0:sk, :, 0], sp_[0:sk, :, 1], ALU.subtract))
                link(v_.tensor_scalar_mul(sp_[0:sk, :, 3], sp_[0:sk, :, 2], -float(size)))
                link(v_.tensor_copy(spi[0:sk, 0, :], sp_[0:sk, :, 1]))
                v_.tensor_copy(spi[0:sk, 1, :], sp_[0:sk, :, 2]).then_inc(sig("windows_made"), 1)

            dve.wait_ge(sig("tiles_in"), 32 * SJ)
            part = lambda v, n: v[0:SK, :, n * EDGES:(n + 1) * EDGES]
            f = [v[0:SK] for v in st_f]
            link(v_.tensor_copy(f[0], part(st_i, 1)))
            link(v_.tensor_copy(f[3], part(st_i, 0)))
            link(v_.tensor_tensor(f[0], f[0], stp[0:SK, :, 3].unsqueeze(2).to_broadcast([SK, SJ, EDGES]), ALU.add))
            link(v_.tensor_tensor(f[1], part(st_i, 1), part(st_i, 3), ALU.not_equal))
            link(v_.scalar_tensor_tensor(f[1], f[0], 1.0, f[1], ALU.add, ALU.mult))
            link(v_.tensor_scalar_add(f[1], f[1], -1.0))
            link(v_.tensor_tensor(f[2], part(st_i, 1), part(st_i, 2), ALU.is_equal))
            v_.tensor_scalar(f[2], f[2], -1.0, BIG, ALU.add, ALU.mult).then_inc(sig("step_rows"), 1)

            dve.wait_ge(sig("ctiles_in"), 16 * CJ)
            f = [v[0:CK] for v in ct_f]
            link(v_.tensor_copy(f[0], ct_i[0:CK, :, EDGES:]))
            link(v_.tensor_copy(f[1], ct_i[0:CK, :, 0:EDGES]))
            link(v_.tensor_tensor(f[0], f[0], ctp[0:CK, :, 3].unsqueeze(2).to_broadcast([CK, CJ, EDGES]), ALU.add))
            quotient(f[2], f[1], P, f[4], ct_q[0:CK])
            link(v_.scalar_tensor_tensor(f[3], f[2], -float(P), f[1], ALU.mult, ALU.add))
            link(v_.scalar_tensor_tensor(f[1], f[2], float(Q), f[0], ALU.mult, ALU.add))
            link(v_.tensor_single_scalar(f[2], f[0], 0.0, ALU.is_ge))
            link(v_.scalar_tensor_tensor(f[2], f[0], float(Q), f[2], ALU.is_lt, ALU.mult))
            link(v_.scalar_tensor_tensor(f[1], f[1], 1.0, f[2], ALU.add, ALU.mult))
            v_.tensor_scalar_add(f[1], f[1], -1.0).then_inc(sig("cstep_rows"), 1)

            dve.wait_ge(sig("dense_copied"), after("counts"))
            dve.wait_ge(sig("rows_out"), 64)
            dve.wait_ge(sig("windows_out"), 32)
            v_.memset(KA, 0.0).then_inc(sig("zeros"), 1)
            dve.wait_ge(sig("zeros"), 1)
            dve.wait_ge(sig("k_zero"), 1)
            dve.wait_ge(sig("windows_in"), 32)

            def windows_of(row, at, n, last):
                return nc.values_load_multi_w_load_instructions(
                    row[0:1, bass.ds(at, n)], engines=[mybir.EngineType.DVE], min_val=0, max_val=last,
                    skip_runtime_bounds_check_because="steps' windows lie in this range by their construction")[1]

            with dve.Fori(0, GCN_ROUNDS) as r:
                dve.wait_ge(sig("tables_zero"), 16 * 3 * TABLES)
                cwindow = windows_of(CIK, r * CNT_PER_ROUND, CNT_PER_ROUND, QW - 1)

                def destinations(half):
                    dve.wait_ge(sig(f"edges_in{half}"), r * 32 + 32)
                    v_.tensor_scalar(dst_hot[half][0:P], dst_hot[half][0:P], pidx[0:P], None, ALU.is_equal)\
                        .then_inc(sig("dst_hot_ready"), 1)

                def sources(half):
                    same = src_row[half].rearrange("p (t e) -> p t e", t=TABLES)
                    v_.tensor_tensor(same, same, SRCF[:, bass.ds(r * GCN_STEPS + half * TABLES, TABLES)].unsqueeze(2)
                                     .to_broadcast([128, TABLES, EDGES]), ALU.is_equal).then_inc(sig("same_ready"), 1)
                    dve.wait_ge(sig("same_ready"), r * 2 + (half + 1))

                def earlier_ones(s):
                    half, t = divmod(s, TABLES)
                    if t == 0:
                        dve.wait_ge(sig("index_ready"), r * 2 + (half + 1))
                    v_.scalar_tensor_tensor(bias[:, 1 + t, :], src_row[half][:, t * EDGES:(t + 1) * EDGES], 1.0, earlier,
                                            ALU.mult, ALU.mult, accum_out=again[:, t:t + 1]).then_inc(sig("again_made"), 1)

                def indices(half):
                    dve.wait_ge(sig("again_made"), r * GCN_STEPS + (half + 1) * TABLES)
                    v_.tensor_scalar(again, again, 0.0, spare, ALU.is_gt, ALU.mult).then_inc(sig("spare_made"), 1)
                    dve.wait_ge(sig("spare_made"), r * 2 + (half + 1))
                    for t in range(TABLES):
                        dve.wait_ge(tabled[t], r * 32 + 16 * (half + 1))
                    v_.tensor_tensor(index[:, half * TABLES:(half + 1) * TABLES], again, SRCF[:, bass.ds(r * GCN_STEPS + half * TABLES, TABLES)],
                                     ALU.max).then_inc(sig("index_ready"), 1)

                def count_hots(j):
                    m = r * CNT_PER_ROUND + j
                    dve.wait_ge(sig("csum_ready"), m + (1 if j else 2))
                    v_.tensor_scalar(khot[:, j % 2, :], keys[:, :], KEY[:, bass.ds(m, 1)], None, ALU.is_equal)
                    v_.tensor_scalar(slohot[:, j % 2, 0:P], keys[:, 0:P], SLO[:, bass.ds(m, 1)], None, ALU.is_equal)\
                        .then_inc(sig("chot_ready"), 1)

                def add_counts(j):
                    m = r * CNT_PER_ROUND + j
                    dve.wait_ge(sig("cnt_copied"), m + 3)
                    dve.wait_ge(sig("cnt_added"), m + 2)
                    part = K[0:P, :, bass.ds(cwindow[j] * Q, Q)]
                    v_.tensor_tensor(part, part, cnt[0:P, j % 3, :].rearrange("p (b d) -> p b d", b=W), ALU.add)\
                        .then_inc(sig("cnt_added"), 1)

                for j in range(CNT_PER_ROUND):
                    count_hots(j)
                    half, i = divmod(j, TABLES)
                    if half < 2 and i == 0:
                        destinations(half)
                        sources(half)
                    if half < 2 and i < 3:
                        for t in range(2 * i, min(2 * i + 2, TABLES)):
                            earlier_ones(half * TABLES + t)
                    if half < 2 and i == 2:
                        indices(half)
                    if j > 1:
                        add_counts(j - 2)
                add_counts(CNT_PER_ROUND - 2)
                add_counts(CNT_PER_ROUND - 1)

            X_, H_, Y_, T_ = wide(X), wide(H), wide(Y), wide(T)
            dve.wait_ge(sig("nb0_in"), 16)
            for t in range(1, TABLES):
                dve.wait_ge(sig(f"nb{t}_in"), 16)
                v_.tensor_tensor(Y_, Y_, wide((H, T)[t % 2]), ALU.add).then_inc(sig("nb_added"), 1)
                dve.wait_ge(sig("nb_added"), t)
            dve.wait_ge(sig("x_in"), 32)
            dve.wait_ge(sig("dense_copied"), after("gcn_out"))
            dve.wait_ge(sig("wts_in"), 16 * 19)
            link(v_.tensor_tensor(Y_, Y_, over_windows(bias[0:P, 0, :]), ALU.add))
            link(v_.tensor_tensor(T_, Y_, Y_, ALU.mult))
            v_.tensor_reduce(rowv[:, 1, :], T_, AX.X, ALU.add).then_inc(sig("root_in"), 1)
            root(2, 1e-12)
            link(v_.tensor_tensor(Y_, Y_, over_features(rowv[:, 1, :]), ALU.mult))
            link(v_.tensor_tensor(X_, X_, Y_, ALU.add))
            normalise(X_, H_, T_, 3)

            dve.wait_ge(sig("dense_copied"), after("msg_Q"))
            v_.memset(macc[0:P], 0.0)
            v_.memset(carry[:, :], -BIG)
            v_.memset(back[:, :, D:D + 1], 1.0).then_inc(sig("macc_zero"), 1)

            def destination_hots(r, half):
                dve.wait_ge(sig(f"rows_in{half}"), r * 32 + 32)
                v_.tensor_scalar(mrhs[half][0:P], dlb[half][0:P], pidx[0:P], None, ALU.is_equal)\
                    .then_inc(sig("mrhs_ready"), 1)

            def last_hots(r, half):
                for s in range(HALF):
                    n = half * HALF + s
                    v_.tensor_scalar(lasthot[:, n, :], ramp[:, 0:P], LAST[:, bass.ds(r * MSG_SLOTS + n, 1)], None,
                                     ALU.is_equal).then_inc(sig("last_ready"), 1)

            def running_max(r, half):
                q = r * 2 + half
                dve.wait_ge(sig(f"pen_in{half}"), r * 16 + 16)
                dve.wait_ge(sig("msg_ready"), q + 2)
                dve.wait_ge(sig("back_ready"), q + 1)
                dve.wait_ge(sig("carried"), q + 1)
                v_.tensor_tensor_scan(scan, penb[half], PS[:, 5, :], carry[:, 0:1], ALU.add, ALU.max)\
                    .then_inc(sig("scan_ready"), 1)
                dve.wait_ge(sig("scan_ready"), q + 2)
                v_.tensor_copy(carry[:, :], scan[:, HALF * EDGES - 1:HALF * EDGES]).then_inc(sig("carried"), 1)

            def add_maxima(r, half, window):
                for s in range(HALF):
                    n = half * HALF + s
                    dve.wait_ge(sig("sums_ready"), r * MSG_SLOTS + (n + 2))
                    dve.wait_ge(sig("sums_added"), r * MSG_SLOTS + (n + HALF))
                    part = macc[0:P, bass.ds(window[n], 1), :].rearrange("p a d -> p (a d)")
                    v_.tensor_tensor(part, part, PS[0:P, SUM_BANKS[s], 0:D + 1], ALU.add).then_inc(sig("sums_added"), 1)

            destination_hots(0, 0)
            destination_hots(0, 1)
            last_hots(0, 0)
            running_max(0, 0)
            with dve.Fori(0, MSG_ROUNDS - 1) as r:
                window = windows_of(IK, r * MSG_SLOTS, MSG_SLOTS, W - 1)
                for half, after_ in ((0, (r, 1)), (1, (r + 1, 0))):
                    destination_hots(r + 1, half)
                    last_hots(*after_)
                    running_max(*after_)
                    add_maxima(r, half, window)
            r = MSG_ROUNDS - 1
            window = windows_of(IK, r * MSG_SLOTS, MSG_SLOTS, W - 1)
            last_hots(r, 1)
            running_max(r, 1)
            add_maxima(r, 0, window)
            add_maxima(r, 1, window)
            dve.wait_ge(sig("sums_added"), STEPS + HALF)
            link(v_.tensor_tensor(H_, over_features(macc[0:P, :, D]), over_windows(bias[0:P, 1, :]), ALU.mult))
            v_.tensor_tensor(H_, H_, macc[0:P, :, 0:D], ALU.add).then_inc(sig("agg_made"), 1)
            dve.wait_ge(sig("dense_copied"), after("msg_out"))
            link(v_.tensor_tensor(Y_, Y_, over_windows(bias[0:P, 2, :]), ALU.add))
            link(v_.tensor_tensor(X_, X_, Y_, ALU.add))
            v_.engine_nop().then_inc(sig("x2_made"), 1)
            normalise(X_, H_, T_, 4)
            dve.wait_ge(sig("dense_copied"), after("gat_emb"))
            v_.tensor_tensor(Y_, Y_, over_windows(bias[0:P, 3, :]), ALU.add).then_inc(sig("emb_made"), 1)

            c = lambda n: cols[0:P, n, :]

            def scores_in(u, g):
                each = (GROUPS + 1 - g % 2) // 2
                return sig(f"ab_in{g % 2}"), 16 * (u * each + g // 2 + 1)

            for u in range(3):
                if u == 1:
                    dve.wait_ge(sig("xw_in"), 16)
                else:
                    dve.wait_ge(sig("dense_copied"), after(("gat_x0", None, "gat_x2")[u]))
                dve.wait_ge(sig("att_in"), 32 * (u + 1))
                v_.memset(xw[0:P, :, D:D + 1], 1.0)
                for n in range(2):
                    link(v_.tensor_tensor(wide(ATT_T), xw[0:P, :, 0:D], over_windows(att[0:P, n, :]), ALU.mult))
                    link(v_.tensor_reduce(c(n), wide(ATT_T), AX.X, ALU.add))
                link(v_.tensor_reduce(scal[0:P, 0:1], c(0), AX.X, ALU.max))
                link(v_.tensor_reduce(scal[0:P, 1:2], c(0), AX.X, ALU.min))
                v_.tensor_scalar_mul(scal[0:P, 1:2], scal[0:P, 1:2], -1.0).then_inc(sig("range_in"), 1)
                dve.wait_ge(sig("range_out"), u + 1)
                link(v_.tensor_tensor(scal[0:P, 4:5], scal[0:P, 2:3], scal[0:P, 3:4], ALU.add))
                link(v_.tensor_scalar_max(scal[0:P, 5:6], scal[0:P, 4:5], 1e-30))
                link(v_.reciprocal(scal[0:P, 5:6], scal[0:P, 5:6]))
                link(v_.tensor_scalar(c(2), c(0), scal[0:P, 3:4], scal[0:P, 5:6], ALU.add, ALU.mult))
                link(v_.tensor_scalar_min(c(2), c(2), 1.0))
                if u == 0:
                    dve.wait_ge(sig("k_in"), 16 * 6)
                    for b in range(W):
                        part = K[0:P, b, b * P:(b + 1) * P]
                        ins = v_.tensor_tensor(part, part, ident[0:P, 0:P], ALU.add)
                    link(ins)
                v_.memset(macc_att[0:P], 0.0).then_inc(sig("max_step"), 1)
                with dve.Fori(0, W) as b:
                    dve.wait_ge(sig("max_step"), b + (u * (W + 1) + 1))
                    v_.scalar_tensor_tensor(macc_att[0:P], K[0:P, bass.ds(b, 1), 0:N].rearrange("p a d -> p (a d)"),
                                            cols[0:P, 2, bass.ds(b, 1)], macc_att[0:P], ALU.min, ALU.max)\
                        .then_inc(sig("max_step"), 1)
                for g in range(GROUPS):
                    dve.wait_ge(sig("max_turned"), u * GROUPS + g + 1)
                    v_.tensor_reduce(cols[0:P, 3, g * GROUP:(g + 1) * GROUP], pairs_of_banks[0][0:P, 0:GROUP, 0:P],
                                     AX.X, ALU.max)\
                        .then_inc(sig("max_reduced"), 1)
                dve.wait_ge(sig("max_reduced"), (u + 1) * GROUPS)
                link(v_.tensor_scalar(c(4), c(3), scal[0:P, 4:5], scal[0:P, 3:4], ALU.mult, ALU.subtract))
                link(v_.tensor_tensor(c(5), c(4), c(1), ALU.add))
                link(v_.scalar_tensor_tensor(c(6), c(5), SLOPE, c(5), ALU.mult, ALU.max))
                v_.tensor_tensor(c(7), c(6), c(1), ALU.subtract)
                v_.tensor_scalar_mul(c(9), c(0), SLOPE - 1.0)
                link(v_.tensor_scalar_mul(c(10), c(0), -SLOPE))
                v_.scalar_tensor_tensor(c(8), c(1), -SLOPE, c(6), ALU.mult, ALU.add).then_inc(sig("ab_made"), 1)

                def minimum(g, q, i):
                    dve.wait_ge(sig("z_used"), q * GROUP + (u * W * GROUPS + g * W + i + 1))
                    v_.scalar_tensor_tensor(zs[0:P, i, :], AB[g % 2][0:P, 0, :], cols[0:P, 9, bass.ds(q * GROUP + i, 1)],
                                            AB[g % 2][0:P, 1, :], ALU.add, ALU.min).then_inc(sig("min_ready"), 1)

                def counted(g, q, i):
                    if i not in POOL_SLOTS:
                        dve.wait_ge(sig("exp_ready"), q * GROUP + (u * W * GROUPS + g * W + i + 1))
                        v_.tensor_tensor(zs[0:P, i, :], zs[0:P, i, :],
                                         K[0:P, bass.ds(q * GROUP + i, 1), g * GC:(g + 1) * GC].rearrange("p a d -> p (a d)"),
                                         ALU.mult).then_inc(sig("z_ready"), 1)

                dve.wait_ge(*scores_in(u, 0))
                minimum(0, 0, 0)
                minimum(0, 0, 1)
                for g in range(GROUPS):
                    with dve.Fori(0, GROUPS - 1) as q:
                        for i in range(GROUP):
                            minimum(g, *((q, i + 2) if i < GROUP - 2 else (q + 1, i + 2 - GROUP)))
                            counted(g, q, i)
                    for i in range(GROUP):
                        if i < GROUP - 2:
                            minimum(g, GROUPS - 1, i + 2)
                        elif g < GROUPS - 1:
                            if i == GROUP - 2:
                                dve.wait_ge(*scores_in(u, g + 1))
                            minimum(g + 1, 0, i + 2 - GROUP)
                        counted(g, GROUPS - 1, i)
                    dve.wait_ge(sig("outs_ready"), u * GROUPS + g + 1)
                    dve.wait_ge(sig("rowsAB_out"), 16 * (u + 1))
                    dve.wait_ge(sig("o_out"), 16 * (u * GROUPS + g))
                    link(v_.tensor_scalar_add(scal[0:P, 8:13], PS[0:P, 3:8, D], 1e-16))
                    link(v_.reciprocal(scal[0:P, 8:13], scal[0:P, 8:13]))
                    for w in range(GROUP):
                        ins = v_.scalar_tensor_tensor(yg[0:P, w, :], PS[0:P, 3 + w, 0:D], scal[0:P, 8 + w:9 + w],
                                                      bias[0:P, 4 + u, :], ALU.mult, ALU.add)
                    ins.then_inc(sig("outs_free"), 1)
                if u == 1:
                    for n in range(2):
                        dve.wait_ge(sig("o_in"), 16 * (n + 1))
                        va, vb = V1[0:P, 0:W * D], V2[0:P]
                        v_.tensor_scalar_min(vb, va, 0.0).then_inc(sig("elu_in"), 1)
                        dve.wait_ge(sig("elu_in"), n + 1)
                        link(v_.tensor_scalar_max(va, va, 0.0))
                        dve.wait_ge(sig("elu_out"), n + 1)
                        v_.scalar_tensor_tensor(va, vb, -1.0, va, ALU.add, ALU.add).then_inc(sig("elu_made"), 1)

            for b in range(W):
                part = K[0:P, b, b * P:(b + 1) * P]
                ins = v_.tensor_tensor(part, part, ident[0:P, 0:P], ALU.subtract)
            link(ins)
            dve.wait_ge(sig("x3_in"), 32)
            v_.tensor_tensor(wide(S1), wide(S1), wide(H3), ALU.add).then_inc(sig("x3_made"), 1)
            dve.wait_ge(sig("x3_made"), 1)
            normalise(wide(S1), wide(H3), wide(S2), 5)
            dve.wait_ge(sig("x3_out"), 16)
            dve.wait_ge(sig("h3_out"), 16)

            def split(src, parts):
                link(v_.tensor_copy(parts[0:P, :, 0:D], src))
                for n in range(1, 3):
                    link(v_.tensor_tensor(src, src, parts[0:P, :, (n - 1) * D:n * D], ALU.subtract))
                    link(v_.tensor_copy(parts[0:P, :, n * D:(n + 1) * D], src))
                v_.memset(parts[0:P, :, 3 * D:3 * D + 2], 1.0).then_inc(sig("parts_made"), 1)

            split(wide(H3), hs1)
            for v in range(2):
                with dve.Fori(0, GROUPS) as g:
                    n = 0
                    base = done[0]
                    for w in range(GROUP):
                        i = g * GROUP + (v * W + w)
                        dst, bank = (sg0, sg1)[v][0:P, w, :], PS[0:P, 3 + w, :]

                        def chained(ins):
                            nonlocal n
                            n += 1
                            ins.then_inc(step, 1)
                            dve.wait_ge(step, g * (4 * GROUP) + (base + n))
                        dve.wait_ge(sig("third_copied"), i + 1)
                        chained(v_.tensor_scalar_max(scal[0:P, 13:14], bank[:, 3 * D:3 * D + 1], 1.0))
                        chained(v_.reciprocal(scal[0:P, 14:15], scal[0:P, 13:14]))
                        chained(v_.tensor_scalar(dst, dst, scal[0:P, 14:15], None, ALU.mult))
                        chained(v_.scalar_tensor_tensor(dst, bank[:, D:2 * D], scal[0:P, 14:15], dst, ALU.mult, ALU.add))
                        v_.scalar_tensor_tensor(dst, bank[:, 0:D], scal[0:P, 14:15], dst, ALU.mult, ALU.add)\
                            .then_inc(sig("sg_ready"), 1)
                        dve.wait_ge(sig("sg_ready"), i + (GROUP + 1))
                done[0] += 4 * GROUP * GROUPS
                dve.wait_ge(sig("dense_copied"), after(f"sage{v + 1}_out"))
                link(v_.tensor_tensor(wide(S1), wide(S1), over_windows(bias[0:P, 7 + v, :]), ALU.add))
                if v == 0:
                    v_.tensor_scalar_max(wide(S1), wide(S1), 0.0).then_inc(sig("g3_made"), 1)
                    dve.wait_ge(sig("g3_out"), 16)
                    split(wide(S1), hs2)
                else:
                    link(v_.tensor_scalar_max(wide(S1), wide(S1), 0.0))
                    dve.wait_ge(sig("x4_in"), 16)
                    v_.tensor_tensor(wide(S1), wide(S1), wide(S2), ALU.add).then_inc(sig("x4_made"), 1)

        @block.tensor
        def _(pe):
            mmul = nc.tensor.matmul

            def rounds(stage, ins, *ready):
                for name, value in ready:
                    pe.wait_ge(sig(name), value)
                if before(stage):
                    pe.wait_ge(sig("dense_copied"), before(stage))
                for g in range(dict(STAGES)[stage]):
                    n = before(stage) + g
                    if n > 1:
                        pe.wait_ge(sig("dense_copied"), n - 1)
                    for last in ins(g, mm_of(n)):
                        pass
                    last.then_inc(sig("dense_ready"), 1)

            def turn(src):
                def ins(g, mm):
                    for w in range(GROUP):
                        yield nc.tensor.transpose(mm[:, w, 0:P], src[0:P, g * GROUP + w, 0:D], ident[0:P, 0:P])
                return ins

            def project(*pairs):
                def ins(g, mm):
                    for w in range(GROUP):
                        at = (g * GROUP + w) * P
                        for i, (nodes_T, block_) in enumerate(pairs):
                            yield mmul(mm[0:P, w, :], nodes_T[:, at:at + P], wts[:, block_, :],
                                       start=i == 0, stop=i == len(pairs) - 1)
                return ins

            def columns(views, size):
                def ins(j, mm):
                    for i, v in enumerate(views):
                        yield nc.tensor.transpose(mm[:, i, 0:size], v[0:size, j, :], ident[0:size, 0:size])
                return ins

            pe.wait_ge(sig("consts_in"), 96)
            rounds("steps", columns((st_f[3], st_f[3], st_f[1], st_w), SK), ("step_rows", 1), ("tiles_in", 32 * SJ))
            rounds("counts", columns((ct_f[1], ct_f[3]), CK), ("cstep_rows", 1))

            pe.wait_ge(sig("h_made"), 1)
            pe.wait_ge(sig("windows_in"), 32)
            with pe.Fori(0, GCN_ROUNDS) as r:
                _, window = nc.values_load_multi_w_load_instructions(
                    IK[0:1, bass.ds(r * GCN_STEPS, GCN_STEPS)], engines=[mybir.EngineType.PE], min_val=0, max_val=W - 1,
                    skip_runtime_bounds_check_because="steps' windows lie in this range by their construction")

                def pick(s):
                    k = r * GCN_STEPS + s
                    half, t = divmod(s, TABLES)
                    pe.wait_ge(sig("dst_hot_ready"), r * 2 + (half + 1))
                    pe.wait_ge(sig("picked_copied"), k + 1)
                    mmul(PS[:, 2 + s % 2, 0:D], dst_hot[half][0:P, t * EDGES:(t + 1) * EDGES],
                         HN[0:P, bass.ds(window[s], 1), :].rearrange("p a d -> p (a d)"), start=True, stop=True)\
                        .then_inc(sig("picked_ready"), 1)

                def add_up(s):
                    k = r * GCN_STEPS + s
                    half, t = divmod(s, TABLES)
                    pe.wait_ge(sig("same_ready"), r * 2 + (half + 1))
                    pe.wait_ge(sig("picked_copied"), k + 3)
                    pe.wait_ge(sig("rows_ready"), k + 1)
                    mmul(PS[:, 6 + s % 2, 0:D], src_row[half][:, t * EDGES:(t + 1) * EDGES], picked[:, s % 2, :],
                         start=True, stop=True).then_inc(sig("summed"), 1)

                for j in range(CNT_PER_ROUND):
                    m = r * CNT_PER_ROUND + j
                    pe.wait_ge(sig("chot_ready"), m + 1)
                    pe.wait_ge(sig("cnt_copied"), m + (1 if j else 2))
                    mmul(PS[0:P, 4 + j % 2, 0:W * Q], slohot[:, j % 2, 0:P], khot[:, j % 2, :], start=True, stop=True)\
                        .then_inc(sig("csum_ready"), 1)
                    if 2 <= j < 2 + GCN_STEPS:
                        pick(j - 2)
                    if 3 <= j < 3 + GCN_STEPS:
                        add_up(j - 3)

            rounds("gcn_hT", turn(wide(H0)), ("rows_ready", STEPS + 2), ("k_out4", 16))
            rounds("gcn_aT", turn(wide(Y)), ("nb_added", TABLES - 1))
            rounds("gcn_out", project((HT, 0), (T, 1)), ("wts_in", 16 * 19))
            rounds("msg_hT", turn(wide(H)), ("h_made", 2))
            rounds("msg_P", project((HT, 2)))
            rounds("msg_Q", project((HT, 3)), ("p_out", 16))

            def first_layer(r, half):
                q = r * 2 + half
                pe.wait_ge(sig("mrhs_ready"), q + 1)
                pe.wait_ge(sig("relu_done"), q + 1)
                for s in range(HALF):
                    n = half * HALF + s
                    part = PS[:, 4, s * EDGES:(s + 1) * EDGES]
                    pe.wait_ge(gathered[n], r * 16 + 16)
                    pe.wait_ge(sig("q_copied"), r * MSG_SLOTS + (n + 1))
                    mmul(part, MG[:, n, :], ident[:, :], start=True, stop=False).then_inc(sig("msg_used"), 1)
                    last = mmul(part, Qc[0:P + 1, n, :], mrhs[half][0:P + 1, s * EDGES:(s + 1) * EDGES],
                                start=False, stop=True)
                last.then_inc(sig("pre_ready"), 1)

            def second_layer(r, half):
                pe.wait_ge(sig("relu_done"), r * 2 + (half + 2))
                pe.wait_ge(sig("scan_ready"), r * 2 + (half + 1))
                mmul(PS[:, 5, :], wts[:, 4, :], relu, start=True, stop=True).then_inc(sig("msg_ready"), 1)

            def turn_back(r, half):
                pe.wait_ge(sig("scan_ready"), r * 2 + (half + 2))
                pe.wait_ge(sig("back_copied"), r * 2 + (half + 1))
                for s in range(HALF):
                    last = nc.tensor.transpose(PS[:, 0, s * EDGES:(s + 1) * EDGES], scan[:, s * EDGES:(s + 1) * EDGES],
                                               ident[:, :])
                last.then_inc(sig("back_ready"), 1)

            def pick_last(r, half):
                pe.wait_ge(sig("back_copied"), r * 2 + (half + 2))
                for s in range(HALF):
                    n = half * HALF + s
                    pe.wait_ge(sig("last_ready"), r * MSG_SLOTS + (n + 1))
                    pe.wait_ge(sig("sums_added"), r * MSG_SLOTS + (n + 1))
                    mmul(PS[0:P, SUM_BANKS[s], 0:D + 1], lasthot[:, n, :], back[:, s, :], start=True, stop=True)\
                        .then_inc(sig("sums_ready"), 1)

            first_layer(0, 0)
            second_layer(0, 0)
            with pe.Fori(0, MSG_ROUNDS - 1) as r:
                for half, after_ in ((0, (r, 1)), (1, (r + 1, 0))):
                    first_layer(*after_)
                    turn_back(r, half)
                    second_layer(*after_)
                    pick_last(r, half)
            r = MSG_ROUNDS - 1
            first_layer(r, 1)
            turn_back(r, 0)
            second_layer(r, 1)
            pick_last(r, 0)
            turn_back(r, 1)
            pick_last(r, 1)

            def hidden(g, mm):
                for w in range(GROUP):
                    at = (g * GROUP + w) * P
                    mmul(mm[:, w, 0:P], wts[:, 5, :], HT[:, at:at + P], start=True, stop=False)
                    yield mmul(mm[:, w, 0:P], wts[:, 6, :], T[:, at:at + P], start=False, stop=True)

            rounds("msg_aT", turn(wide(H)), ("agg_made", 1))
            rounds("msg_u", hidden)
            rounds("msg_out", project((QU, 7)))
            rounds("gat_hT", turn(wide(H)), ("h_made", 3))
            rounds("gat_emb", project((HT, 0)), ("wts2_in", 16 * 5))
            rounds("gat_eT", turn(wide(Y)), ("emb_made", 1))
            rounds("gat_x0", project((T, 1)))
            rounds("gat_x1", project((T, 2)))

            for u in range(3):
                pe.wait_ge(sig("max_step"), (u + 1) * (W + 1))
                for g in range(GROUPS):
                    pe.wait_ge(sig("max_reduced"), u * GROUPS + g)
                    for w in range(GROUP):
                        at = (g * GROUP + w) * P
                        last = nc.tensor.transpose(pairs_of_banks[0][0:P, w, 0:P], macc_att[0:P, at:at + P], ident[0:P, 0:P])
                    last.then_inc(sig("max_turned"), 1)
                rounds(f"rows{u}", lambda g, mm: [nc.tensor.transpose(
                    mm[0:2 * W, 0, 0:P], cols[0:P, 7:9, :].rearrange("p a w -> p (a w)"), ident[0:P, 0:P])],
                    ("ab_made", u + 1), ("max_reduced", (u + 1) * GROUPS))

                def chunk(g, b, i, first, b_round=0):
                    by_pool = i in POOL_SLOTS
                    slots = [x for x in range(GROUP) if (x in POOL_SLOTS) == by_pool]
                    q = 0 if isinstance(b, int) else b_round
                    pe.wait_ge(sig("pool_z_ready" if by_pool else "z_ready"),
                               q * len(slots) + ((u * GROUPS + g) * GROUPS * len(slots) + slots.index(i) + 1))
                    rows = xw[0:P, b, :] if isinstance(b, int) else xw[0:P, bass.ds(b, 1), :].rearrange("p a d -> p (a d)")
                    for w in range(GROUP):
                        last = mmul(PS[0:P, 3 + w, 0:D + 1], zs[0:P, i, w * P:(w + 1) * P], rows,
                                    start=first, stop=False, skip_group_check=True)
                    last.then_inc(sig("z_used"), 1)
                    return last

                for g in range(GROUPS):
                    at = u * W * GROUPS + g * W
                    pe.wait_ge(sig("outs_free"), u * GROUPS + g)
                    for i in range(GROUP):
                        chunk(g, i, i, i == 0)
                    with pe.Fori(1, GROUPS) as q:
                        for i in range(GROUP):
                            chunk(g, q * GROUP + i, i, False, q)
                    pe.wait_ge(sig("z_used"), at + W + GROUP)
                    pe.sem_inc(sig("outs_ready"), 1)
                if u == 1:
                    for n in range(2):
                        rounds(f"gat_o{n}T", turn(V1[:, 0:W * D].rearrange("p (w d) -> p w d", w=W)), ("elu_made", n + 1))
                    rounds("gat_x2", project((V3, 3), (V2, 4)))

            for v in range(2):
                pe.wait_ge(sig("parts_made"), v + 1)
                hs = (hs1, hs2)[v]
                with pe.Fori(0, GROUPS) as g:
                    for w in range(GROUP):
                        pe.wait_ge(sig("sg_ready"), g * GROUP + (v * W + w + 1))
                        for b in range(W):
                            last = mmul(PS[0:P, 3 + w, 0:3 * D + 1], K[0:P, b, bass.ds(g * GC + w * P, P)],
                                        hs[0:P, b, 0:3 * D + 1], start=b == 0, stop=b == W - 1)
                        last.then_inc(sig("sage_ready"), 1)
                name = f"sage{v + 1}"
                rounds(f"{name}_aT", turn(wide(S1)), ("s_in", 16 * (2 * v + 1)))
                rounds(f"{name}_hT", turn(wide(S1)), ("s_in", 16 * (2 * v + 2)))
                rounds(f"{name}_out", project((S2, 5 if v == 0 else 7), (S3, 6 if v == 0 else 0)),
                       ("wts3_in", 48), ("wts4_in", 16))


def kernel(**inputs):
    import concourse.bacc as bacc
    from concourse.bass_utils import run_bass_kernel_spmd

    g = {k: np.asarray(v) for k, v in inputs.items()}
    pad = TILES * EDGES - E
    src, dst, w = (g[k] for k in ("src", "dst", "edge_weight"))
    s_ = np.concatenate([src, np.zeros(pad, src.dtype)]).reshape(TILES, EDGES)
    d_ = np.concatenate([dst, np.full(pad, N, dst.dtype)])
    w_ = np.concatenate([w, np.zeros(pad, w.dtype)]).reshape(TILES, EDGES)
    prev = np.concatenate([np.full(1, N + 1, dst.dtype), d_[:-1]]).reshape(TILES, EDGES)
    next_ = np.concatenate([d_[1:], np.full(1, N + 1, dst.dtype)]).reshape(TILES, EDGES)
    d_ = d_.reshape(TILES, EDGES)
    block = lambda m, i, j: m[i * D:(i + 1) * D, j * D:(j + 1) * D]
    arrays = {
        "x": g["x"], "edges": np.concatenate([s_, d_, prev, next_], 1), "ends": np.concatenate([s_, d_], 1),
        "weights": w_, "last": d_[:, -1], "tiles": np.arange(TILES, dtype=np.float32),
        "pidx": np.arange(128, dtype=np.float32).reshape(128, 1), "ident": np.eye(128, dtype=np.float32),
        "earlier": np.tril(np.ones((EDGES, EDGES), np.float32), -1), "spare": N + np.arange(128, dtype=np.float32).reshape(128, 1),
        "ramp": np.tile(np.arange(128, dtype=np.float32), (128, 1)),
        "keys": np.tile(np.arange(W * Q, dtype=np.float16), (128, 1)),
        "L0_a": block(g["L0_gnn_W"], 0, 0).T, "L0_b_w": block(g["L0_gnn_W"], 0, 1).T, "L0_b": g["L0_gnn_b"],
        "L1_src": block(g["L1_gnn_W1"], 0, 0), "L1_dst": block(g["L1_gnn_W1"], 1, 0), "L1_wrow": g["L1_gnn_W1"][2 * D:],
        "L1_W2": g["L1_gnn_W2"], "L1_U1a": block(g["L1_gnn_U1"], 0, 0), "L1_U1b": block(g["L1_gnn_U1"], 1, 0),
        "L1_U2": g["L1_gnn_U2"], "L1_b1": g["L1_gnn_b1"].reshape(D, 1), "L1_c1": g["L1_gnn_c1"].reshape(D, 1),
        "L1_b2": g["L1_gnn_b2"], "L1_c2": g["L1_gnn_c2"],
        "L2_emb": g["L2_gnn_W_emb"], "L2_W1a": block(g["L2_gnn_W1"], 0, 0), "L2_W1b": block(g["L2_gnn_W1"], 0, 1),
        "L2_W2a": block(g["L2_gnn_W2"], 0, 0), "L2_W2b": block(g["L2_gnn_W2"], 1, 0), "L2_b_emb": g["L2_gnn_b_emb"],
        "L2_b1a": g["L2_gnn_b1"][:D], "L2_b1b": g["L2_gnn_b1"][D:], "L2_b2": g["L2_gnn_b2"],
        "L2_src0": g["L2_gnn_att_src1"][0], "L2_dst0": g["L2_gnn_att_dst1"][0],
        "L2_src1": g["L2_gnn_att_src1"][1], "L2_dst1": g["L2_gnn_att_dst1"][1],
        "L2_src2": g["L2_gnn_att_src2"][0], "L2_dst2": g["L2_gnn_att_dst2"][0],
        "L3_Wl1": g["L3_gnn_Wl1"], "L3_Wr1": g["L3_gnn_Wr1"], "L3_Wl2": g["L3_gnn_Wl2"], "L3_Wr2": g["L3_gnn_Wr2"],
        "L3_bl1": g["L3_gnn_bl1"], "L3_bl2": g["L3_gnn_bl2"],
    }
    arrays = {f"in_{k}": np.ascontiguousarray(v) for k, v in arrays.items()}
    nc = bacc.Bacc("TRN2", target_bir_lowering=False, num_devices=1)
    a = {k[3:]: nc.dram_tensor(k, v.shape, mybir.dt.from_np(v.dtype), kind="ExternalInput").ap() for k, v in arrays.items()}
    out = nc.dram_tensor("out", (N, D), f32, kind="ExternalOutput").ap()
    gnn(nc, a, out)
    r = run_bass_kernel_spmd(nc, [arrays], core_ids=[0])
    return r.results[0]["out"]
```

```python
from contextlib import ExitStack

import numpy as np
import concourse.bass as bass
from concourse import mybir

N, D, E = 3125, 128, 53125
P = 125
W = N // P
EDGES = 128
TILES = -(-E // EDGES)
STEPS = TILES + W - 1
SK, SJ = 110, 4
Q = 20
QW = -(-N // Q)
NP = QW * Q
CSTEPS = TILES + QW - 1
CK, CJ = 52, 11
GCN_ROUNDS, GCN_STEPS, CNT_PER_ROUND = 44, 10, 13
TABLES = 5
GE = TABLES * EDGES
MSG_ROUNDS, MSG_SLOTS, HALF = 55, 8, 4
SUM_BANKS = (1, 2, 3, 6)
MAX_PARTS = ((0, 1600), (1600, N))
POOL_SLOTS = (0,)
GROUP = 5
GROUPS = W // GROUP
GC = GROUP * P
KEEP = 12
BIG = 3.0e38
SLOPE = 0.2
FIXED = 4096.0
PARTS = (2, 3)
assert FIXED * D**0.5 < 65504 and W <= 2 * 13
assert SK * SJ == STEPS == GCN_ROUNDS * GCN_STEPS == MSG_ROUNDS * MSG_SLOTS
assert CK * CJ == CSTEPS == GCN_ROUNDS * CNT_PER_ROUND and W * Q <= 512 and GCN_STEPS == 2 * TABLES

f32, i32, f16, bf16 = mybir.dt.float32, mybir.dt.int32, mybir.dt.float16, mybir.dt.bfloat16
ALU = mybir.AluOpType
ACT = mybir.ActivationFunctionType
AX = mybir.AxisListType
RMAX = bass.bass_isa.ReduceOp.max

STAGES = (("steps", SJ), ("counts", CJ),
          ("gcn_hT", GROUPS), ("gcn_aT", GROUPS), ("gcn_out", GROUPS),
          ("msg_hT", GROUPS), ("msg_P", GROUPS), ("msg_Q", GROUPS),
          ("msg_aT", GROUPS), ("msg_u", GROUPS), ("msg_out", GROUPS),
          ("gat_hT", GROUPS), ("gat_emb", GROUPS), ("gat_eT", GROUPS), ("gat_x0", GROUPS), ("gat_x1", GROUPS),
          ("rows0", 1), ("rows1", 1),
          ("gat_o0T", GROUPS), ("gat_o1T", GROUPS), ("gat_x2", GROUPS), ("rows2", 1),
          ("sage1_aT", GROUPS), ("sage1_hT", GROUPS), ("sage1_out", GROUPS),
          ("sage2_aT", GROUPS), ("sage2_hT", GROUPS), ("sage2_out", GROUPS))


def before(stage):
    n = 0
    for name, rounds in STAGES:
        if name == stage:
            return n
        n += rounds
    raise KeyError(stage)


def after(stage):
    return before(stage) + dict(STAGES)[stage]


def gnn(nc, a, out):
    ctx = ExitStack()
    with ctx:
        def sb(name, shape, dt=f32):
            return ctx.enter_context(nc.sbuf_tensor(name, shape, dt))

        sems = {}

        def sig(name):
            if name not in sems:
                sems[name] = ctx.enter_context(nc.semaphore(name))
            return sems[name]

        def dram(name, shape, dt=f32):
            return nc.dram_tensor(name, shape, dt).ap()

        win_d, cwin_d = dram("win_d", [STEPS], i32), dram("cwin_d", [CSTEPS], i32)
        dl_d, pen_d, w_d, src_d = (dram(n, [STEPS, EDGES]) for n in ("dl_d", "pen_d", "w_d", "src_d"))
        sum_d = [dram(f"sum{n}_d", [N + EDGES, D]) for n in range(TABLES)]
        x_d = dram("x_d", [N, D])
        h0_d, p_d = dram("h0_d", [N, D]), dram("p_d", [N, D])
        xw1_d = dram("xw1_d", [N, D])
        o_d = [dram(f"o{n}_d", [N, D]) for n in range(3)]
        rows_d = [dram(f"rows{n}_d", [2, N]) for n in range(3)]
        k_d = dram("k_d", [P, (W - KEEP) * NP // 2])

        def nodes(ap):
            return ap.rearrange("(w p) d -> p w d", p=P)

        K = sb("K", [128, W, NP], f16)
        U = sb("U", [128, 11100])
        ident = sb("ident", [128, 128])
        ramp = sb("ramp", [128, 128])
        keys = sb("keys", [128, W * Q], f16)
        pidx = sb("pidx", [128, 1])
        wts = sb("wts", [128, 8, D])
        bias = sb("bias", [128, 9, D])
        bcol = sb("bcol", [128, 2])
        scal = sb("scal", [128, 16])
        carry = sb("carry", [128, 1])
        index = sb("index", [128, GCN_STEPS], i32)
        rowv_all = sb("rowv", [128, 4 * W])
        rowv = rowv_all[0:P].rearrange("p (a w) -> p a w", a=4)
        KA = K[:, KEEP:, :].rearrange("p b d -> p (b d)").bitcast(f32)

        def carve(arena, words):
            at = [0]

            def take(*shape, dt=f32):
                size = int(np.prod(shape))
                need = size if dt in (f32, i32) else -(-size // 2)
                assert at[0] + need <= words, (at[0], need, words)
                v = arena[:, at[0]:at[0] + need]
                at[0] += need
                if dt is not f32:
                    v = v.bitcast(dt)[:, 0:size]
                if len(shape) == 2:
                    v = v.rearrange("p (a b) -> p a b", a=shape[0])
                elif len(shape) == 3:
                    v = v.rearrange("p (a b c) -> p a b c", a=shape[0], b=shape[1])
                return v
            return take

        UWORDS, KWORDS = 11100, (W - KEEP) * NP // 2
        take = carve(U, UWORDS)
        SRC = take(STEPS, dt=i32)
        LAST = take(STEPS)
        IK, CIK = take(STEPS, dt=i32), take(CSTEPS, dt=i32)
        SRCF = take(STEPS)
        WT = take(STEPS)
        KEY = take(CSTEPS, dt=f16)
        SLO = take(CSTEPS, dt=f16)
        HN = take(W, D)
        dst_hot = [take(GE) for _ in range(2)]
        src_row = [take(GE) for _ in range(2)]
        rows = take(TABLES, D)
        slohot = take(2, 128, dt=f16)
        cnt = take(3, W * Q, dt=f16)
        take = carve(U, UWORDS)
        take(3 * STEPS + CSTEPS)
        macc = take(W, D + 1)
        MG = take(MSG_SLOTS, D)
        lasthot = take(MSG_SLOTS, P)
        Qc = take(MSG_SLOTS, D)
        take = carve(wts[:, :, :].rearrange("p a b -> p (a b)"), 8 * D)
        picked = take(2, D)
        earlier = take(EDGES)
        khot = take(2, W * Q, dt=f16)
        take = carve(rowv_all, 4 * W)
        take(2 * W)
        again, spare = take(TABLES), take(1)
        take = carve(KA, KWORDS)
        X, H, Y, T, HT, QU = (take(W * D) for _ in range(6))
        w3 = lambda v: v.rearrange("p (w d) -> p w d", w=W)
        mrhs = [Y[:, n * 512:(n + 1) * 512] for n in range(2)]
        dlb = [Y[:, (2 + n) * 512:(3 + n) * 512] for n in range(2)]
        penb = [Y[:, (4 + n) * 512:(5 + n) * 512] for n in range(2)]
        relu, scan = T[:, 0:512], T[:, 512:1024]
        back = T[:, 1024:1024 + HALF * (D + 1)].rearrange("p (s c) -> p s c", s=HALF)
        take = carve(KA, KWORDS)
        st_i = take(SJ, 4 * EDGES, dt=i32)
        st_w = take(SJ, EDGES)
        st_f = [take(SJ, EDGES) for _ in range(4)]
        ct_i = take(CJ, 2 * EDGES, dt=i32)
        ct_f = [take(CJ, EDGES) for _ in range(5)]
        ct_q = take(CJ, EDGES, dt=i32)
        tl_i = take(TILES, dt=i32)
        tl_f = [take(TILES) for _ in range(5)]
        tl_q = take(TILES, dt=i32)
        stp = take(SJ, 6)
        ctp = take(CJ, 6)
        stp_i, ctp_i = take(2, SJ, dt=i32), take(2, CJ, dt=i32)
        take = carve(U, UWORDS)
        xw = take(W, D + 1)
        cols = take(14, W)
        AB = [take(2, GC) for _ in range(2)]
        zs = take(GROUP, GC)
        yg = take(GROUP, D)
        atts = [take(2, D) for _ in range(2)]
        take = carve(U, UWORDS)
        take(W * (D + 1) + 14 * W + 4 * GC)
        ATT_T = take(W * D)
        macc_att = ATT_T[:, 0:N]
        take = carve(U, UWORDS)
        V1, V2, V3 = take(W * (D + 1)), take(W * D), take(W * D)
        elus = ((V2, V3), (V1, V2))
        hs1 = U[:, 0:W * (2 * D + 2) // 2].bitcast(f16).rearrange("p (w c) -> p w c", w=W)
        hs2 = U[:, 0:W * (3 * D + 2) // 2].bitcast(bf16).rearrange("p (w c) -> p w c", w=W)
        S1, S2, H3 = U[:, 0:W * D], U[:, W * (D + 1):W * (2 * D + 1)], U[:, UWORDS - W * D:]
        agg1 = S2.rearrange("p (w d) -> p w d", w=W)
        agg2 = U[:, W * (3 * D + 2) // 2:][:, 0:(GROUP - 1) * GROUPS * D].rearrange("p (w d) -> p w d", d=D)
        rest = U[:, W * (3 * D + 2) // 2:][:, 0:13 * D].rearrange("p (w d) -> p w d", d=D)

        def mean_of(v, g, w):
            if v == 0:
                where = agg1, g * GROUP + w
            elif w < GROUP - 1:
                where = agg2, g * (GROUP - 1) + w
            else:
                where = bias, g
            return where[0][0:P, bass.ds(where[1], 1), :].rearrange("p a d -> p (a d)")

        PS = ctx.enter_context(nc.psum_tensor("PS", [128, 8, 512], f32))
        pairs_of_banks = [PS[:, n:n + 2, :].rearrange("p b (j c) -> p (b j) c", c=128) for n in (0, 6)]

        def mm_of(n):
            return pairs_of_banks[n % 2]


        KB = K[:, 0:KEEP, :].rearrange("p b d -> p (b d)").bitcast(f32)
        take = carve(KB, KEEP * NP // 2)
        X0, T0 = (take(W * D) for _ in range(2))
        H0 = HN[:, :, :].rearrange("p w d -> p (w d)")
        gathered = [sig(f"gathered{n}") for n in range(MSG_SLOTS)]
        tabled = [sig(f"tabled{n}") for n in range(TABLES)]
        block = ctx.enter_context(nc.Block())

        def wide(v):
            return v[0:P, 0:W * D].rearrange("p (w d) -> p w d", w=W)

        def over_features(v):
            return v.unsqueeze(2).to_broadcast([P, W, D])

        def over_windows(v):
            return v.unsqueeze(1).to_broadcast([P, W, D])

        @block.sync
        def _(sp):
            def loads(name, *pairs):
                for dst, src in pairs:
                    sp.dma_start(dst, src).then_inc(sig(name), 16)

            loads("x_in", (wide(X0), nodes(a["x"])))
            loads("sched_in", (tl_i[0:SK], a["last"].partition_broadcast(SK)),
                  (tl_f[3][0:SK], a["tiles"].partition_broadcast(SK)))
            loads("consts_in", (pidx[:, :], a["pidx"]), (ident[:, :], a["ident"]), (earlier, a["earlier"]),
                  (spare, a["spare"]), (keys[:, :], a["keys"]), (ramp[:, :], a["ramp"]))
            sp.wait_ge(sig("bias_zero"), 1)
            for t in range(TABLES):
                for w0 in range(0, W, 9):
                    w1 = min(w0 + 9, W)
                    loads("tables_zero", (sum_d[t][w0 * P:w1 * P].rearrange("(w p) d -> p w d", p=P), bias[0:P, 0:w1 - w0]))
            sp.wait_ge(sig("windows_made"), 2)
            loads("windows_out", (win_d.rearrange("(p j) -> p j", p=SK), stp_i[0:SK, 1, :]),
                  (cwin_d.rearrange("(p j) -> p j", p=CK), ctp_i[0:CK, 1, :]))
            sp.wait_ge(sig("windows_out"), 32)
            loads("windows_in", (IK[0:1], win_d.unsqueeze(0)), (CIK[0:1], cwin_d.unsqueeze(0)))
            sp.wait_ge(sig("h_made"), 1)
            loads("h0_out", (nodes(h0_d), wide(H0)))
            sp.wait_ge(sig("step_rows"), 1)
            by_step = lambda v: v.rearrange("(p j) e -> p j e", p=SK)
            loads("rows_out", (by_step(dl_d), st_f[0][0:SK]), (by_step(pen_d), st_f[2][0:SK]),
                  (by_step(w_d), st_w[0:SK]),
                  (by_step(src_d), st_f[3][0:SK]))

            def edge_rows(q, half):
                part = lambda v: v[bass.ds(q * TABLES, TABLES), :].rearrange("s e -> (s e)")
                sp.dma_start(dst_hot[half][0:P], part(dl_d).partition_broadcast(P)).then_inc(sig(f"edges_in{half}"), 16)
                sp.dma_start(src_row[half], part(src_d).partition_broadcast(128)).then_inc(sig(f"edges_in{half}"), 16)

            sp.wait_ge(sig("rows_out"), 64)
            for half in range(2):
                edge_rows(half, half)
            with sp.Fori(1, GCN_ROUNDS) as r:
                for half in range(2):
                    sp.wait_ge(sig("summed"), r * GCN_STEPS + half * TABLES)
                    sp.sem_inc(sig("half_seen"), 1)
                    sp.wait_ge(sig("index_ready"), r * 2 + half)
                    edge_rows(r * 2 + half, half)

            def region(n):
                return slice(n * W * D, (n + 1) * W * D if n < 5 else KWORDS)

            sp.wait_ge(sig("cnt_added"), CSTEPS + 2)
            def step_aside(*regions):
                for n in regions:
                    loads(f"k_out{n}", (k_d[:, region(n)], KA[0:P, region(n)]))

            step_aside(2, 3, 1, 4)
            for t in range(TABLES):
                sp.wait_ge(tabled[t], 16 * (STEPS // TABLES + 2))
            sp.wait_ge(sig("k_out2"), 16)
            loads("nb0_in", (wide(Y), nodes(sum_d[0][0:N])))
            for t in range(1, TABLES):
                if t > 2:
                    sp.wait_ge(sig("nb_added"), t - 2)
                else:
                    sp.wait_ge(sig(f"k_out{(3, 1)[t - 1]}"), 16)
                loads(f"nb{t}_in", (wide((H, T)[t % 2]), nodes(sum_d[t][0:N])))
            sp.wait_ge(sig("summed"), STEPS + TABLES)
            blocks = ["L0_a", "L0_b_w", "L1_src", "L1_dst", "L1_W2", "L1_U1a", "L1_U1b", "L1_U2"]
            loads("wts_in", *[(wts[:, n, :], a[b]) for n, b in enumerate(blocks)])
            vectors = ["L0_b", "L1_b2", "L1_c2", "L2_b_emb", "L2_b1a", "L2_b1b", "L2_b2", "L3_bl1", "L3_bl2"]
            loads("wts_in", *[(bias[0:P, n, :], a[b].partition_broadcast(P)) for n, b in enumerate(vectors)])
            loads("wts_in", (bcol[:, 0:1], a["L1_b1"]), (bcol[:, 1:2], a["L1_c1"]))
            step_aside(0, 5)
            sp.wait_ge(sig("k_out0"), 16)
            loads("x_in", (wide(X), nodes(a["x"])))
            sp.wait_ge(sig("k_out5"), 16)
            loads("qrow_in", (QU[P:P + 1].rearrange("p (w d) -> p w d", w=W),
                              a["L1_wrow"].unsqueeze(1).to_broadcast([1, W, D])))
            sp.wait_ge(sig("dense_copied"), after("msg_P"))
            loads("p_out", (nodes(p_d), wide(Y)))

            def message_rows(q, half):
                part = lambda v: v[bass.ds(q * HALF, HALF), :].rearrange("s e -> (s e)")
                sp.dma_start(dlb[half][0:P], part(dl_d).partition_broadcast(P)).then_inc(sig(f"rows_in{half}"), 16)
                sp.dma_start(mrhs[half][P:P + 1], part(w_d).unsqueeze(0)).then_inc(sig(f"rows_in{half}"), 16)

            def segment_rows(q, half):
                sp.dma_start(penb[half], pen_d[bass.ds(q * HALF, HALF), :].rearrange("s e -> (s e)")
                             .partition_broadcast(128)).then_inc(sig(f"pen_in{half}"), 16)

            sp.wait_ge(sig("p_out"), 16)
            for half in range(2):
                message_rows(half, half)
                segment_rows(half, half)
            with sp.Fori(1, MSG_ROUNDS) as r:
                for half in range(2):
                    sp.wait_ge(sig("pre_ready"), r * 2 + (half - 1))
                    message_rows(r * 2 + half, half)
                    sp.wait_ge(sig("scan_ready"), r * 2 + half)
                    segment_rows(r * 2 + half, half)

            sp.wait_ge(sig("msg_ready"), MSG_ROUNDS * 2 + 1)
            later = ["L2_emb", "L2_W1a", "L2_W1b", "L2_W2a", "L2_W2b"]
            loads("wts2_in", *[(wts[:, n, :], a[b]) for n, b in enumerate(later)])

            def attention_vectors(u):
                loads(f"att{u}_in", *[(atts[u % 2][0:P, n, :], a[b].partition_broadcast(P))
                                      for n, b in enumerate((f"L2_src{u}", f"L2_dst{u}"))])

            attention_vectors(0)
            attention_vectors(1)
            sp.wait_ge(sig("x2_made"), 1)
            loads("x_out", (nodes(x_d), wide(X)))
            for n, stage in ((5, "msg_out"), (4, "gat_emb"), (2, "gat_eT"), (0, None), (3, "gat_x1")):
                if stage:
                    sp.wait_ge(sig("dense_copied"), after(stage))
                else:
                    sp.wait_ge(sig("x_out"), 16)
                loads("k_in", (KA[0:P, region(n)], k_d[:, region(n)]))
            loads("xw_out", (nodes(xw1_d), wide(H)))
            sp.wait_ge(sig("xw_out"), 16)
            sp.wait_ge(sig("second_scored"), 1)
            loads("k_in", (KA[0:P, region(1)], k_d[:, region(1)]))
            loads("wts3_in", *[(wts[:, 5 + n, :], a[b]) for n, b in enumerate(("L3_Wl1", "L3_Wr1", "L3_Wl2"))])

            def store_out(sp, u, g):
                sp.wait_ge(sig("outs_free"), u * GROUPS + g + 1)
                loads("o_out", (o_d[u][g * GC:(g + 1) * GC, :].rearrange("(w p) d -> p w d", p=P), yg[0:P]))

            for u in range(3):
                if u == 1:
                    sp.wait_ge(sig("outs_ready"), GROUPS * u)
                    loads("xw_in", (xw[0:P, :, 0:D], nodes(xw1_d)))
                if u == 2:
                    sp.wait_ge(sig("outs_free"), GROUPS * u)
                    attention_vectors(u)
                sp.wait_ge(sig("dense_copied"), after(f"rows{u}"))
                loads("rowsAB_out", (rows_d[u].rearrange("a (w p) -> (a w) p", p=P),
                                     yg[0:2 * W].rearrange("p a b -> p (a b)")[:, 0:P]))
                sp.wait_ge(sig("rowsAB_out"), 16 * (u + 1))
                for g in range(GROUPS):
                    if g > 1:
                        sp.wait_ge(sig("min_ready"), (u * GROUPS + g - 1) * W)
                    loads(f"ab_in{g % 2}", (AB[g % 2][0:P], rows_d[u][:, g * GC:(g + 1) * GC].unsqueeze(0).to_broadcast([P, 2, GC])))
                    if g > 1:
                        store_out(sp, u, g - 2)
                store_out(sp, u, GROUPS - 2)
                store_out(sp, u, GROUPS - 1)
                if u == 1:
                    sp.wait_ge(sig("o_out"), 16 * 2 * GROUPS)
                    for n in range(2):
                        loads(f"o{n}_in", (wide(elus[n][0]), nodes(o_d[n])))
            sp.wait_ge(sig("dense_copied"), after("gat_x2"))
            loads("wts4_in", (wts[:, 0, :], a["L3_Wr2"]))
            sp.wait_ge(sig("o_out"), 16 * 3 * GROUPS)
            loads("x3_in", (wide(S1), nodes(x_d)), (wide(H3), nodes(o_d[2])))
            sp.wait_ge(sig("x3_made"), 1)
            loads("x3_out", (nodes(x_d), wide(S1)))
            sp.wait_ge(sig("sg_ready"), 2 * W + GROUP)
            loads("x4_in", (wide(X), nodes(x_d)))
            for g in range(GROUPS):
                sp.wait_ge(sig("x4_made"), g + 1)
                loads("stored", (out[g * GC:(g + 1) * GC, :].rearrange("(w p) d -> p w d", p=P),
                                 wide(H3)[:, g * GROUP:(g + 1) * GROUP]))
            sp.wait_ge(sig("stored"), 16 * GROUPS)

        @block.gpsimd
        def _(pool):
            for name, free in (("msg_used", MSG_SLOTS), ("sums_added", HALF),
                               ("csum_ready", 2), ("cnt_copied", 2), ("cnt_added", 2), ("z_used", GROUP), ("sg_ready", GROUP),
                               ("picked_ready", 2), ("picked_copied", 2), ("summed", TABLES), ("rows_ready", 2),
                               ("relu_done", 1), ("msg_ready", 1), ("scan_ready", 1), ("back_ready", 1),
                               ("back_copied", 1), ("carried", 1), ("index_ready", 1), ("sums_ready", 1)):
                pool.sem_inc(sig(name), free)
            pool.wait_ge(sig("bias_zero"), 1)
            for t in range(TABLES):
                for half in range(2):
                    rows_ = slice(half * EDGES // 2, (half + 1) * EDGES // 2)
                    pool.dma_start(sum_d[t][N:][rows_], bias[rows_, 0, :]).then_inc(tabled[t], 16)

            def gather(dst, rows, index, sem):
                pool.indirect_dma_start(dst, None, rows, bass.IndirectOffsetOnAxis(ap=index, axis=0)).then_inc(sem, 16)

            pool.wait_ge(sig("windows_made"), 2)
            for j in range(SJ):
                gather(st_i[0:SK, j, :], a["edges"], stp_i[0:SK, 0, j:j + 1], sig("tiles_in"))
                gather(st_w[0:SK, j, :], a["weights"], stp_i[0:SK, 0, j:j + 1], sig("tiles_in"))
            for j in range(CJ):
                gather(ct_i[0:CK, j, :], a["ends"], ctp_i[0:CK, 0, j:j + 1], sig("ctiles_in"))
            pool.wait_ge(sig("h0_out"), 16)
            pool.memset(KB, 0.0).then_inc(sig("k_zero"), 1)

            pool.wait_ge(sig("tables_zero"), 16 * 3 * TABLES)
            with pool.Fori(0, GCN_ROUNDS) as r:
                for half in range(2):
                    for t in range(TABLES):
                        k = r * GCN_STEPS + (half * TABLES + t)
                        pool.wait_ge(sig("rows_ready"), k + 3)
                        pool.wait_ge(tabled[t], r * 32 + 16 * (half + 2))
                        pool.wait_ge(sig("index_ready"), r * 2 + (half + 2))
                        pool.sem_inc(sig("row_seen"), 1)
                        n = half * TABLES + t
                        pool.indirect_dma_start(sum_d[t], bass.IndirectOffsetOnAxis(ap=index[:, n:n + 1], axis=0),
                                                rows[:, t, :], None, compute_op=ALU.add).then_inc(tabled[t], 16)

            pool.wait_ge(sig("p_out"), 16)
            with pool.Fori(0, MSG_ROUNDS) as r:
                for half in range(2):
                    k = r * MSG_SLOTS + half * HALF
                    pool.wait_ge(sig("msg_used"), k + HALF)
                    pool.tensor_copy(index[:, half * HALF:(half + 1) * HALF], SRC[:, bass.ds(k, HALF)])\
                        .then_inc(sig("index_copied"), 1)
                    pool.wait_ge(sig("index_copied"), r * 2 + (half + 1))
                    pool.sem_inc(sig("index_seen"), 1)
                    for n in range(half * HALF, (half + 1) * HALF):
                        gather(MG[:, n, :], p_d, index[:, n:n + 1], gathered[n])
            for u in range(3):
                pool.wait_ge(sig("range_in"), u + 1)
                pool.partition_all_reduce(scal[0:P, 2:4], scal[0:P, 0:2], P, RMAX).then_inc(sig("range_out"), 1)
                for g in range(GROUPS):
                    with pool.Fori(0, GROUPS) as q:
                        for i in POOL_SLOTS:
                            pool.wait_ge(sig("exp_ready"), q * GROUP + (u * W * GROUPS + g * W + i + 1))
                            nc.gpsimd.tensor_tensor(zs[0:P, i, :], zs[0:P, i, :],
                                                    K[0:P, bass.ds(q * GROUP + i, 1), g * GC:(g + 1) * GC]
                                                    .rearrange("p a d -> p (a d)"), ALU.mult).then_inc(sig("pool_z_ready"), 1)

        @block.scalar
        def _(act):
            def copy_round(n, pairs, func=ACT.Copy, **kw):
                act.wait_ge(sig("dense_ready"), n + 1)
                for dst, src in pairs:
                    ins = nc.scalar.activation(dst, src(mm_of(n)), func, **kw)
                ins.then_inc(sig("dense_copied"), 1)

            def turned(stage, dst):
                for g in range(GROUPS):
                    copy_round(before(stage) + g,
                               [(dst[:, g * GC:(g + 1) * GC].rearrange("p (w n) -> p w n", w=GROUP), lambda mm: mm[:, 0:GROUP, 0:P])])

            def straight(stage, dst):
                for g in range(GROUPS):
                    copy_round(before(stage) + g, [(dst[0:P, g * GROUP:(g + 1) * GROUP, 0:D], lambda mm: mm[0:P, 0:GROUP, :])])

            def roots(n):
                act.wait_ge(sig("root_in"), n)
                nc.scalar.activation(rowv[:, 1, :], rowv[:, 1, :], ACT.Sqrt).then_inc(sig("root_out"), 1)

            roots(1)
            for j in range(SJ):
                copy_round(before("steps") + j, [(dst.rearrange("p (k j) -> p j k", j=SJ)[:, j, :], lambda mm, i=i: mm[:, i, 0:SK])
                                                 for i, dst in enumerate((SRC, SRCF, LAST, WT))])
            for j in range(CJ):
                copy_round(before("counts") + j, [(dst.rearrange("p (k j) -> p j k", j=CJ)[:, j, :], lambda mm, i=i: mm[:, i, 0:CK])
                                                  for i, dst in enumerate((KEY, SLO))])

            with act.Fori(0, GCN_ROUNDS) as r:
                def picked_copy(s):
                    k = r * GCN_STEPS + s
                    act.wait_ge(sig("picked_ready"), k + 3)
                    act.wait_ge(sig("summed"), k + (TABLES - 1))
                    nc.scalar.activation(picked[:, s % 2, :], PS[:, 2 + s % 2, 0:D], ACT.Copy,
                                         scale=WT[:, bass.ds(k, 1)])\
                        .then_inc(sig("picked_copied"), 1)

                def row_copy(s):
                    k = r * GCN_STEPS + s
                    act.wait_ge(sig("summed"), k + (TABLES + 1))
                    act.wait_ge(tabled[s % TABLES], r * 32 + 16 * (s // TABLES + 2))
                    nc.scalar.activation(rows[:, s % TABLES, :], PS[:, 6 + s % 2, 0:D], ACT.Copy)\
                        .then_inc(sig("rows_ready"), 1)

                for j in range(CNT_PER_ROUND):
                    m = r * CNT_PER_ROUND + j
                    act.wait_ge(sig("csum_ready"), m + 3)
                    act.wait_ge(sig("cnt_added"), m + (0 if j else 2))
                    nc.scalar.activation(cnt[0:P, j % 3, :], PS[0:P, 4 + j % 2, 0:W * Q], ACT.Copy)\
                        .then_inc(sig("cnt_copied"), 1)
                    if 2 <= j < 2 + GCN_STEPS:
                        picked_copy(j - 2)
                    if 3 <= j < 3 + GCN_STEPS:
                        row_copy(j - 3)

            act.wait_ge(sig("k_out4"), 16)
            turned("gcn_hT", HT)
            turned("gcn_aT", T)
            straight("gcn_out", wide(Y))
            roots(2)
            roots(3)
            turned("msg_hT", HT)
            straight("msg_P", wide(Y))
            act.wait_ge(sig("k_out5"), 16)
            straight("msg_Q", wide(QU))

            act.wait_ge(sig("qrow_in"), 16)
            act.wait_ge(sig("windows_in"), 32)
            act.wait_ge(sig("macc_zero"), 1)
            def windows_act(r):
                return nc.values_load_multi_w_load_instructions(
                    IK[0:1, bass.ds(r * MSG_SLOTS, MSG_SLOTS)], engines=[mybir.EngineType.Activation], min_val=0, max_val=W - 1,
                    skip_runtime_bounds_check_because="steps' windows lie in this range by their construction")[1]

            def projections(window, half):
                for s in range(HALF):
                    n = half * HALF + s
                    nc.scalar.activation(Qc[0:P + 1, n, :], QU[0:P + 1].rearrange("p (w d) -> p w d", w=W)
                                         [:, bass.ds(window[n], 1), :].rearrange("p a d -> p (a d)"), ACT.Copy)\
                        .then_inc(sig("q_copied"), 1)

            def relu_half(r, half):
                act.wait_ge(sig("pre_ready"), r * 2 + (half + 1))
                act.wait_ge(sig("msg_ready"), r * 2 + (half + 1))
                nc.scalar.activation(relu, PS[:, 4, :], ACT.Relu, bias=bcol[:, 0:1]).then_inc(sig("relu_done"), 1)

            def copy_back(r, half):
                act.wait_ge(sig("back_ready"), r * 2 + (half + 2))
                act.wait_ge(sig("sums_ready"), r * MSG_SLOTS + (half * HALF + 1))
                nc.scalar.activation(back[:, :, 0:D], PS[:, 0, :].rearrange("p (s d) -> p s d", s=HALF), ACT.Copy)\
                    .then_inc(sig("back_copied"), 1)

            window = windows_act(0)
            projections(window, 0)
            projections(window, 1)
            relu_half(0, 0)
            with act.Fori(0, MSG_ROUNDS - 1) as r:
                window = windows_act(r + 1)
                for half, after_ in ((0, (r, 1)), (1, (r + 1, 0))):
                    projections(window, half)
                    relu_half(*after_)
                    copy_back(r, half)
            relu_half(MSG_ROUNDS - 1, 1)
            copy_back(MSG_ROUNDS - 1, 0)
            copy_back(MSG_ROUNDS - 1, 1)

            turned("msg_aT", T)
            for g in range(GROUPS):
                copy_round(before("msg_u") + g,
                           [(QU[:, g * GC:(g + 1) * GC].rearrange("p (w n) -> p w n", w=GROUP), lambda mm: mm[:, 0:GROUP, 0:P])],
                           ACT.Relu, bias=bcol[:, 1:2])
            straight("msg_out", wide(Y))
            roots(4)
            turned("gat_hT", HT)
            straight("gat_emb", wide(Y))
            turned("gat_eT", T)
            straight("gat_x0", xw)
            straight("gat_x1", wide(H))

            for u in range(3):
                if u:
                    act.wait_ge(sig("o_out"), 16 * u * GROUPS)
                copy_round(before(f"rows{u}"), [(yg[0:2 * W].rearrange("p a b -> p (a b)")[:, 0:P],
                                                 lambda mm: mm[0:2 * W, 0, 0:P])])
                def exponential(g, q, c):
                    b = q * GROUP + c
                    act.wait_ge(sig("min_ready"), q * GROUP + (u * W * GROUPS + g * W + c + 1))
                    nc.scalar.activation(zs[0:P, c, :], zs[0:P, c, :], ACT.Relu, bias=cols[0:P, 10, bass.ds(b, 1)])\
                        .then_inc(sig("held"), 1)
                    act.wait_ge(sig("held"), q * GROUP + (u * W * GROUPS + g * W + c + 1))
                    nc.scalar.activation(zs[0:P, c, :], zs[0:P, c, :], ACT.Exp, scale=-1.0).then_inc(sig("exp_ready"), 1)

                for g in range(GROUPS):
                    with act.Fori(0, GROUPS) as q:
                        for c in range(GROUP):
                            exponential(g, q, c)
                if u == 1:
                    for n, (_, other) in enumerate(elus):
                        act.wait_ge(sig("elu_in"), n + 1)
                        nc.scalar.activation(other[0:P], other[0:P], ACT.Exp).then_inc(sig("elu_out"), 1)
                        turned(f"gat_o{n}T", other)
                    straight("gat_x2", xw)
            roots(5)
            for v in range(2):
                with act.Fori(0, GROUPS) as g:
                    for w in range(GROUP):
                        i = g * GROUP + (v * W + w)
                        act.wait_ge(sig("sage_ready"), i + 1)
                        nc.scalar.activation(mean_of(v, g, w), PS[0:P, 3 + w, (PARTS[v] - 1) * D:PARTS[v] * D], ACT.Copy)\
                            .then_inc(sig("last_copied"), 1)
                turned(f"sage{v + 1}_aT", S1)
                turned(f"sage{v + 1}_hT", S2)
                straight(f"sage{v + 1}_out", wide(H3))

        @block.vector
        def _(dve):
            v_ = nc.vector
            step = sig("dve_step")
            done = [0]

            def link(ins):
                done[0] += 1
                ins.then_inc(step, 1)
                dve.wait_ge(step, done[0])

            def root(n, out):
                dve.wait_ge(sig("root_out"), n)
                if out is not None:
                    link(v_.tensor_scalar_max(rowv[:, 1, :], rowv[:, 1, :], out))
                link(v_.reciprocal(rowv[:, 1, :], rowv[:, 1, :]))

            def normalise(x, h, t, n):
                link(v_.tensor_reduce(rowv[:, 0, :], x, AX.X, ALU.add))
                link(v_.tensor_scalar_mul(rowv[:, 0, :], rowv[:, 0, :], 1.0 / D))
                link(v_.tensor_tensor(h, x, over_features(rowv[:, 0, :]), ALU.subtract))
                link(v_.tensor_tensor(t, h, h, ALU.mult))
                link(v_.tensor_reduce(rowv[:, 1, :], t, AX.X, ALU.add))
                v_.tensor_scalar(rowv[:, 1, :], rowv[:, 1, :], 1.0 / D, 1e-5, ALU.mult, ALU.add)\
                    .then_inc(sig("root_in"), 1)
                root(n, None)
                v_.scalar_tensor_tensor(h, h, 0.0, over_features(rowv[:, 1, :]), ALU.max, ALU.mult).then_inc(sig("h_made"), 1)

            v_.memset(bias[:, :, :], 0.0).then_inc(sig("bias_zero"), 1)
            dve.wait_ge(sig("x_in"), 16)
            normalise(wide(X0), wide(H0), wide(T0), 1)

            def quotient(q, v, by, r, qi):
                link(v_.tensor_scalar_mul(qi, v, 1.0 / by))
                link(v_.tensor_copy(q, qi))
                link(v_.scalar_tensor_tensor(r, q, -float(by), v, ALU.mult, ALU.add))
                link(v_.scalar_tensor_tensor(q, r, 0.0, q, ALU.is_ge, ALU.add))
                link(v_.scalar_tensor_tensor(q, r, float(by), q, ALU.is_ge, ALU.add))
                link(v_.tensor_scalar_add(q, q, -1.0))

            dve.wait_ge(sig("sched_in"), 32)
            dve.wait_ge(sig("consts_in"), 96)
            link(v_.tensor_copy(tl_f[0][0:SK], tl_i[0:SK]))
            for size, windows, sk, sj, sp_, spi in ((P, W, SK, SJ, stp, stp_i), (Q, QW, CK, CJ, ctp, ctp_i)):
                quotient(tl_f[1][0:sk], tl_f[0][0:sk], size, tl_f[2][0:sk], tl_q[0:sk])
                link(v_.scalar_tensor_tensor(tl_f[1][0:sk], tl_f[1][0:sk], float(windows - 1), tl_f[3][0:sk],
                                             ALU.min, ALU.add))
                for j in range(sj):
                    link(v_.tensor_scalar(sp_[0:sk, j, 0:1], pidx[0:sk], float(sj), float(j), ALU.mult, ALU.add))
                    link(v_.tensor_scalar(tl_f[4][0:sk], tl_f[1][0:sk], sp_[0:sk, j, 0:1], None, ALU.is_lt))
                    link(v_.tensor_reduce(sp_[0:sk, j, 1:2], tl_f[4][0:sk], AX.X, ALU.add))
                link(v_.tensor_tensor(sp_[0:sk, :, 2], sp_[0:sk, :, 0], sp_[0:sk, :, 1], ALU.subtract))
                link(v_.tensor_scalar_mul(sp_[0:sk, :, 3], sp_[0:sk, :, 2], -float(size)))
                link(v_.tensor_copy(spi[0:sk, 0, :], sp_[0:sk, :, 1]))
                v_.tensor_copy(spi[0:sk, 1, :], sp_[0:sk, :, 2]).then_inc(sig("windows_made"), 1)

            dve.wait_ge(sig("tiles_in"), 32 * SJ)
            part = lambda v, n: v[0:SK, :, n * EDGES:(n + 1) * EDGES]
            f = [v[0:SK] for v in st_f]
            link(v_.tensor_copy(f[0], part(st_i, 1)))
            link(v_.tensor_copy(f[3], part(st_i, 0)))
            link(v_.tensor_tensor(f[0], f[0], stp[0:SK, :, 3].unsqueeze(2).to_broadcast([SK, SJ, EDGES]), ALU.add))
            link(v_.tensor_tensor(f[1], part(st_i, 1), part(st_i, 3), ALU.not_equal))
            link(v_.scalar_tensor_tensor(f[1], f[0], 1.0, f[1], ALU.add, ALU.mult))
            link(v_.tensor_scalar_add(f[1], f[1], -1.0))
            link(v_.tensor_tensor(f[2], part(st_i, 1), part(st_i, 2), ALU.is_equal))
            v_.tensor_scalar(f[2], f[2], -1.0, BIG, ALU.add, ALU.mult).then_inc(sig("step_rows"), 1)

            dve.wait_ge(sig("ctiles_in"), 16 * CJ)
            f = [v[0:CK] for v in ct_f]
            link(v_.tensor_copy(f[0], ct_i[0:CK, :, EDGES:]))
            link(v_.tensor_copy(f[1], ct_i[0:CK, :, 0:EDGES]))
            link(v_.tensor_tensor(f[0], f[0], ctp[0:CK, :, 3].unsqueeze(2).to_broadcast([CK, CJ, EDGES]), ALU.add))
            quotient(f[2], f[1], P, f[4], ct_q[0:CK])
            link(v_.scalar_tensor_tensor(f[3], f[2], -float(P), f[1], ALU.mult, ALU.add))
            link(v_.scalar_tensor_tensor(f[1], f[2], float(Q), f[0], ALU.mult, ALU.add))
            link(v_.tensor_single_scalar(f[2], f[0], 0.0, ALU.is_ge))
            link(v_.scalar_tensor_tensor(f[2], f[0], float(Q), f[2], ALU.is_lt, ALU.mult))
            link(v_.scalar_tensor_tensor(f[1], f[1], 1.0, f[2], ALU.add, ALU.mult))
            v_.tensor_scalar_add(f[1], f[1], -1.0).then_inc(sig("cstep_rows"), 1)

            dve.wait_ge(sig("dense_copied"), after("counts"))
            dve.wait_ge(sig("rows_out"), 64)
            dve.wait_ge(sig("windows_out"), 32)
            v_.memset(KA, 0.0).then_inc(sig("zeros"), 1)
            dve.wait_ge(sig("zeros"), 1)
            dve.wait_ge(sig("k_zero"), 1)
            dve.wait_ge(sig("windows_in"), 32)

            def windows_of(row, at, n, last):
                return nc.values_load_multi_w_load_instructions(
                    row[0:1, bass.ds(at, n)], engines=[mybir.EngineType.DVE], min_val=0, max_val=last,
                    skip_runtime_bounds_check_because="steps' windows lie in this range by their construction")[1]

            with dve.Fori(0, GCN_ROUNDS) as r:
                dve.wait_ge(sig("tables_zero"), 16 * 3 * TABLES)
                def destinations(half):
                    dve.wait_ge(sig(f"edges_in{half}"), r * 32 + 32)
                    v_.tensor_scalar(dst_hot[half][0:P], dst_hot[half][0:P], pidx[0:P], None, ALU.is_equal)\
                        .then_inc(sig("dst_hot_ready"), 1)

                def sources(half):
                    same = src_row[half].rearrange("p (t e) -> p t e", t=TABLES)
                    v_.tensor_tensor(same, same, SRCF[:, bass.ds(r * GCN_STEPS + half * TABLES, TABLES)].unsqueeze(2)
                                     .to_broadcast([128, TABLES, EDGES]), ALU.is_equal).then_inc(sig("same_ready"), 1)
                    dve.wait_ge(sig("same_ready"), r * 2 + (half + 1))

                def earlier_ones(s):
                    half, t = divmod(s, TABLES)
                    if t == 0:
                        dve.wait_ge(sig("index_ready"), r * 2 + (half + 1))
                    v_.scalar_tensor_tensor(bias[:, 1 + t, :], src_row[half][:, t * EDGES:(t + 1) * EDGES], 1.0, earlier,
                                            ALU.mult, ALU.mult, accum_out=again[:, t:t + 1]).then_inc(sig("again_made"), 1)

                def indices(half):
                    dve.wait_ge(sig("again_made"), r * GCN_STEPS + (half + 1) * TABLES)
                    v_.tensor_scalar(again, again, 0.0, spare, ALU.is_gt, ALU.mult).then_inc(sig("spare_made"), 1)
                    dve.wait_ge(sig("spare_made"), r * 2 + (half + 1))
                    for t in range(TABLES):
                        dve.wait_ge(tabled[t], r * 32 + 16 * (half + 1))
                    v_.tensor_tensor(index[:, half * TABLES:(half + 1) * TABLES], again,
                                     SRCF[:, bass.ds(r * GCN_STEPS + half * TABLES, TABLES)],
                                     ALU.max).then_inc(sig("index_ready"), 1)

                def count_hots(j):
                    m = r * CNT_PER_ROUND + j
                    dve.wait_ge(sig("csum_ready"), m + (1 if j else 2))
                    v_.tensor_scalar(khot[:, j % 2, :], keys[:, :], KEY[:, bass.ds(m, 1)], None, ALU.is_equal)
                    v_.tensor_scalar(slohot[:, j % 2, 0:P], keys[:, 0:P], SLO[:, bass.ds(m, 1)], None, ALU.is_equal)\
                        .then_inc(sig("chot_ready"), 1)

                def add_counts(j):
                    m = r * CNT_PER_ROUND + j
                    dve.wait_ge(sig("cnt_copied"), m + 3)
                    dve.wait_ge(sig("cnt_added"), m + 2)
                    part = K[0:P, :, bass.ds(cwindow[j] * Q, Q)]
                    v_.tensor_tensor(part, part, cnt[0:P, j % 3, :].rearrange("p (b d) -> p b d", b=W), ALU.add)\
                        .then_inc(sig("cnt_added"), 1)

                for j in range(CNT_PER_ROUND):
                    count_hots(j)
                    half, i = divmod(j, TABLES)
                    if half < 2 and i == 0:
                        destinations(half)
                        sources(half)
                    if half < 2 and i < 3:
                        for t in range(2 * i, min(2 * i + 2, TABLES)):
                            earlier_ones(half * TABLES + t)
                    if half < 2 and i == 2:
                        indices(half)
                    if j == 0:
                        cwindow = windows_of(CIK, r * CNT_PER_ROUND, CNT_PER_ROUND, QW - 1)
                    if j > 1:
                        add_counts(j - 2)
                add_counts(CNT_PER_ROUND - 2)
                add_counts(CNT_PER_ROUND - 1)

            X_, H_, Y_, T_ = wide(X), wide(H), wide(Y), wide(T)
            dve.wait_ge(sig("nb0_in"), 16)
            for t in range(1, TABLES):
                dve.wait_ge(sig(f"nb{t}_in"), 16)
                v_.tensor_tensor(Y_, Y_, wide((H, T)[t % 2]), ALU.add).then_inc(sig("nb_added"), 1)
                dve.wait_ge(sig("nb_added"), t)
            dve.wait_ge(sig("x_in"), 32)
            dve.wait_ge(sig("wts_in"), 16 * 19)
            group = lambda v, g: v[:, g * GROUP:(g + 1) * GROUP]
            over_group = lambda v: v.unsqueeze(1).to_broadcast([P, GROUP, D])
            for g in range(GROUPS):
                dve.wait_ge(sig("dense_copied"), before("gcn_out") + g + 1)
                y, t = group(Y_, g), group(H_, g)
                link(v_.tensor_tensor(y, y, over_group(bias[0:P, 0, :]), ALU.add))
                link(v_.tensor_tensor(t, y, y, ALU.mult))
                ins = v_.tensor_reduce(rowv[:, 1, g * GROUP:(g + 1) * GROUP], t, AX.X, ALU.add)
            ins.then_inc(sig("root_in"), 1)
            root(2, 1e-12)
            link(v_.tensor_tensor(Y_, Y_, over_features(rowv[:, 1, :]), ALU.mult))
            link(v_.tensor_tensor(X_, X_, Y_, ALU.add))
            normalise(X_, H_, T_, 3)

            dve.wait_ge(sig("dense_copied"), after("msg_Q"))
            v_.memset(macc[0:P], 0.0)
            v_.memset(carry[:, :], -BIG)
            v_.memset(back[:, :, D:D + 1], 1.0).then_inc(sig("macc_zero"), 1)

            def destination_hots(r, half):
                dve.wait_ge(sig(f"rows_in{half}"), r * 32 + 32)
                v_.tensor_scalar(mrhs[half][0:P], dlb[half][0:P], pidx[0:P], None, ALU.is_equal)\
                    .then_inc(sig("mrhs_ready"), 1)

            def last_hots(r, half):
                for s in range(HALF):
                    n = half * HALF + s
                    v_.tensor_scalar(lasthot[:, n, :], ramp[:, 0:P], LAST[:, bass.ds(r * MSG_SLOTS + n, 1)], None,
                                     ALU.is_equal).then_inc(sig("last_ready"), 1)

            def running_max(r, half):
                q = r * 2 + half
                dve.wait_ge(sig(f"pen_in{half}"), r * 16 + 16)
                dve.wait_ge(sig("msg_ready"), q + 2)
                dve.wait_ge(sig("back_ready"), q + 1)
                dve.wait_ge(sig("carried"), q + 1)
                v_.tensor_tensor_scan(scan, penb[half], PS[:, 5, :], carry[:, 0:1], ALU.add, ALU.max)\
                    .then_inc(sig("scan_ready"), 1)
                dve.wait_ge(sig("scan_ready"), q + 2)
                v_.tensor_copy(carry[:, :], scan[:, HALF * EDGES - 1:HALF * EDGES]).then_inc(sig("carried"), 1)

            def add_maxima(r, half, window):
                for s in range(HALF):
                    n = half * HALF + s
                    dve.wait_ge(sig("sums_ready"), r * MSG_SLOTS + (n + 2))
                    dve.wait_ge(sig("sums_added"), r * MSG_SLOTS + (n + HALF))
                    part = macc[0:P, bass.ds(window[n], 1), :].rearrange("p a d -> p (a d)")
                    v_.tensor_tensor(part, part, PS[0:P, SUM_BANKS[s], 0:D + 1], ALU.add).then_inc(sig("sums_added"), 1)

            destination_hots(0, 0)
            destination_hots(0, 1)
            last_hots(0, 0)
            running_max(0, 0)
            with dve.Fori(0, MSG_ROUNDS - 1) as r:
                window = windows_of(IK, r * MSG_SLOTS, MSG_SLOTS, W - 1)
                for half, after_ in ((0, (r, 1)), (1, (r + 1, 0))):
                    destination_hots(r + 1, half)
                    last_hots(*after_)
                    running_max(*after_)
                    add_maxima(r, half, window)
            r = MSG_ROUNDS - 1
            window = windows_of(IK, r * MSG_SLOTS, MSG_SLOTS, W - 1)
            last_hots(r, 1)
            running_max(r, 1)
            add_maxima(r, 0, window)
            add_maxima(r, 1, window)
            dve.wait_ge(sig("sums_added"), STEPS + HALF)
            link(v_.tensor_tensor(H_, over_features(macc[0:P, :, D]), over_windows(bias[0:P, 1, :]), ALU.mult))
            v_.tensor_tensor(H_, H_, macc[0:P, :, 0:D], ALU.add).then_inc(sig("agg_made"), 1)
            for g in range(GROUPS):
                dve.wait_ge(sig("dense_copied"), before("msg_out") + g + 1)
                x, y = group(X_, g), group(Y_, g)
                link(v_.tensor_tensor(y, y, over_group(bias[0:P, 2, :]), ALU.add))
                link(v_.tensor_tensor(x, x, y, ALU.add))
            v_.engine_nop().then_inc(sig("x2_made"), 1)
            normalise(X_, H_, T_, 4)
            for g in range(GROUPS):
                dve.wait_ge(sig("dense_copied"), before("gat_emb") + g + 1)
                v_.tensor_tensor(group(Y_, g), group(Y_, g), over_group(bias[0:P, 3, :]), ALU.add)\
                    .then_inc(sig("emb_made"), 1)

            c = lambda n: cols[0:P, n, :]

            def scores_in(u, g):
                each = (GROUPS + 1 - g % 2) // 2
                return sig(f"ab_in{g % 2}"), 16 * (u * each + g // 2 + 1)

            def scores(u, src, to):
                dve.wait_ge(sig(f"att{u}_in"), 32)
                for n in range(2):
                    link(v_.tensor_tensor(wide(ATT_T), src, over_windows(atts[u % 2][0:P, n, :]), ALU.mult))
                    link(v_.tensor_reduce(c(to + n), wide(ATT_T), AX.X, ALU.add))

            for u in range(3):
                if u == 1:
                    for n in range(2):
                        link(v_.tensor_copy(c(n), c(11 + n)))
                else:
                    dve.wait_ge(sig("dense_copied"), after(("gat_x0", None, "gat_x2")[u]))
                    link(v_.memset(xw[0:P, :, D:D + 1], 1.0))
                    scores(u, xw[0:P, :, 0:D], 0)
                if u == 0:
                    dve.wait_ge(sig("dense_copied"), after("gat_x1"))
                    scores(1, H_, 11)
                    v_.engine_nop().then_inc(sig("second_scored"), 1)
                link(v_.tensor_reduce(scal[0:P, 0:1], c(0), AX.X, ALU.max))
                link(v_.tensor_reduce(scal[0:P, 1:2], c(0), AX.X, ALU.min))
                v_.tensor_scalar_mul(scal[0:P, 1:2], scal[0:P, 1:2], -1.0).then_inc(sig("range_in"), 1)
                dve.wait_ge(sig("range_out"), u + 1)
                link(v_.tensor_tensor(scal[0:P, 4:5], scal[0:P, 2:3], scal[0:P, 3:4], ALU.add))
                link(v_.tensor_scalar_max(scal[0:P, 5:6], scal[0:P, 4:5], 1e-30))
                link(v_.reciprocal(scal[0:P, 5:6], scal[0:P, 5:6]))
                link(v_.tensor_scalar(c(2), c(0), scal[0:P, 3:4], scal[0:P, 5:6], ALU.add, ALU.mult))
                link(v_.tensor_scalar_min(c(2), c(2), 1.0))
                if u == 0:
                    dve.wait_ge(sig("k_in"), 16 * 6)
                    for b in range(W):
                        part = K[0:P, b, b * P:(b + 1) * P]
                        ins = v_.tensor_tensor(part, part, ident[0:P, 0:P], ALU.add)
                    link(ins)
                for d0, d1 in MAX_PARTS:
                    v_.memset(macc_att[0:P, d0:d1], 0.0).then_inc(sig("max_step"), 1)
                with dve.Fori(0, W) as b:
                    for i, (d0, d1) in enumerate(MAX_PARTS):
                        dve.wait_ge(sig("max_step"), b * 2 + (u * 2 * (W + 1) + i + 1))
                        v_.scalar_tensor_tensor(macc_att[0:P, d0:d1], K[0:P, bass.ds(b, 1), d0:d1].rearrange("p a d -> p (a d)"),
                                                cols[0:P, 2, bass.ds(b, 1)], macc_att[0:P, d0:d1], ALU.min, ALU.max)\
                            .then_inc(sig("max_step"), 1)
                for g in range(GROUPS):
                    dve.wait_ge(sig("max_turned"), u * GROUPS + g + 1)
                    v_.tensor_reduce(cols[0:P, 3, g * GROUP:(g + 1) * GROUP], pairs_of_banks[0][0:P, 0:GROUP, 0:P],
                                     AX.X, ALU.max)\
                        .then_inc(sig("max_reduced"), 1)
                dve.wait_ge(sig("max_reduced"), (u + 1) * GROUPS)
                link(v_.tensor_scalar(c(4), c(3), scal[0:P, 4:5], scal[0:P, 3:4], ALU.mult, ALU.subtract))
                link(v_.tensor_tensor(c(5), c(4), c(1), ALU.add))
                link(v_.scalar_tensor_tensor(c(6), c(5), SLOPE, c(5), ALU.mult, ALU.max))
                v_.tensor_tensor(c(7), c(6), c(1), ALU.subtract)
                v_.tensor_scalar_mul(c(9), c(0), SLOPE - 1.0)
                link(v_.tensor_scalar_mul(c(10), c(0), -SLOPE))
                v_.scalar_tensor_tensor(c(8), c(1), -SLOPE, c(6), ALU.mult, ALU.add).then_inc(sig("ab_made"), 1)

                def minimum(g, q, i):
                    dve.wait_ge(sig("z_used"), q * GROUP + (u * W * GROUPS + g * W + i + 1))
                    v_.scalar_tensor_tensor(zs[0:P, i, :], AB[g % 2][0:P, 0, :], cols[0:P, 9, bass.ds(q * GROUP + i, 1)],
                                            AB[g % 2][0:P, 1, :], ALU.add, ALU.min).then_inc(sig("min_ready"), 1)

                def counted(g, q, i):
                    if i not in POOL_SLOTS:
                        dve.wait_ge(sig("exp_ready"), q * GROUP + (u * W * GROUPS + g * W + i + 1))
                        v_.tensor_tensor(zs[0:P, i, :], zs[0:P, i, :],
                                         K[0:P, bass.ds(q * GROUP + i, 1), g * GC:(g + 1) * GC].rearrange("p a d -> p (a d)"),
                                         ALU.mult).then_inc(sig("z_ready"), 1)

                def divide(g):
                    dve.wait_ge(sig("outs_ready"), u * GROUPS + g + 1)
                    dve.wait_ge(sig("rowsAB_out"), 16 * (u + 1))
                    dve.wait_ge(sig("o_out"), 16 * (u * GROUPS + g))
                    link(v_.tensor_scalar_add(scal[0:P, 8:13], PS[0:P, 3:8, D], 1e-16))
                    link(v_.reciprocal(scal[0:P, 8:13], scal[0:P, 8:13]))
                    for w in range(GROUP):
                        ins = v_.scalar_tensor_tensor(yg[0:P, w, :], PS[0:P, 3 + w, 0:D], scal[0:P, 8 + w:9 + w],
                                                      bias[0:P, 4 + u, :], ALU.mult, ALU.add)
                    ins.then_inc(sig("outs_free"), 1)

                def minimum_and_counted(g, q, i):
                    minimum(g, *((q, i + 2) if i < GROUP - 2 else (q + 1, i + 2 - GROUP)))
                    counted(g, q, i)

                dve.wait_ge(*scores_in(u, 0))
                minimum(0, 0, 0)
                minimum(0, 0, 1)
                for g in range(GROUPS):
                    if g:
                        for i in range(GROUP):
                            minimum_and_counted(g, 0, i)
                            if i == 0:
                                divide(g - 1)
                    with dve.Fori(1 if g else 0, GROUPS - 1) as q:
                        for i in range(GROUP):
                            minimum_and_counted(g, q, i)
                    for i in range(GROUP):
                        if i < GROUP - 2:
                            minimum(g, GROUPS - 1, i + 2)
                        elif g < GROUPS - 1:
                            if i == GROUP - 2:
                                dve.wait_ge(*scores_in(u, g + 1))
                            minimum(g + 1, 0, i + 2 - GROUP)
                        counted(g, GROUPS - 1, i)
                divide(GROUPS - 1)
                if u == 1:
                    for n in range(2):
                        dve.wait_ge(sig(f"o{n}_in"), 16)
                        if n:
                            dve.wait_ge(sig("dense_copied"), after("gat_o0T"))
                        va, vb = elus[n][0][0:P, 0:W * D], elus[n][1][0:P]
                        v_.tensor_scalar_min(vb, va, 0.0).then_inc(sig("elu_in"), 1)
                        dve.wait_ge(sig("elu_in"), n + 1)
                        link(v_.tensor_scalar_max(va, va, 0.0))
                        dve.wait_ge(sig("elu_out"), n + 1)
                        v_.scalar_tensor_tensor(va, vb, -1.0, va, ALU.add, ALU.add).then_inc(sig("elu_made"), 1)

            for b in range(W):
                part = K[0:P, b, b * P:(b + 1) * P]
                ins = v_.tensor_tensor(part, part, ident[0:P, 0:P], ALU.subtract)
            link(ins)
            dve.wait_ge(sig("x3_in"), 32)
            v_.tensor_tensor(wide(S1), wide(S1), wide(H3), ALU.add).then_inc(sig("x3_made"), 1)
            dve.wait_ge(sig("x3_made"), 1)
            normalise(wide(S1), wide(H3), wide(S2), 5)
            dve.wait_ge(sig("x3_out"), 16)
            h_, t_ = wide(H3), wide(S2)
            dve.wait_ge(sig("h_made"), 4)
            link(v_.tensor_scalar_mul(t_, h_, FIXED))
            link(v_.tensor_copy(hs1[0:P, :, 0:D], t_))
            link(v_.tensor_tensor(t_, t_, hs1[0:P, :, 0:D], ALU.subtract))
            v_.memset(hs1[0:P, :, 2 * D:2 * D + 2], 1.0)
            v_.tensor_copy(hs1[0:P, :, D:2 * D], t_).then_inc(sig("parts_made"), 1)

            def split(src):
                v_.memset(hs2[0:P, :, 3 * D:3 * D + 2], 1.0)
                for w0, w1 in ((0, 13), (13, W)):
                    parts, left = hs2[0:P, w0:w1], rest[0:P, 0:w1 - w0]
                    link(v_.tensor_copy(parts[:, :, 0:D], src[:, w0:w1]))
                    link(v_.tensor_tensor(left, src[:, w0:w1], parts[:, :, 0:D], ALU.subtract))
                    link(v_.tensor_copy(parts[:, :, D:2 * D], left))
                    link(v_.tensor_tensor(left, left, parts[:, :, D:2 * D], ALU.subtract))
                    ins = v_.tensor_copy(parts[:, :, 2 * D:3 * D], left)
                    if w0 == 0:
                        link(ins)
                ins.then_inc(sig("parts_made"), 1)

            for v in range(2):
                with dve.Fori(0, GROUPS) as g:
                    n = 0
                    base = done[0]
                    for w in range(GROUP):
                        i = g * GROUP + (v * W + w)
                        dst, bank = mean_of(v, g, w), PS[0:P, 3 + w, :]

                        def chained(ins):
                            nonlocal n
                            n += 1
                            ins.then_inc(step, 1)
                            dve.wait_ge(step, g * (4 * GROUP) + (base + n))
                        dve.wait_ge(sig("last_copied"), i + 1)
                        chained(v_.tensor_scalar_max(scal[0:P, 13:14], bank[:, PARTS[v] * D:PARTS[v] * D + 1], 1.0))
                        chained(v_.reciprocal(scal[0:P, 14:15], scal[0:P, 13:14]))
                        if v == 0:
                            chained(v_.tensor_scalar_mul(scal[0:P, 14:15], scal[0:P, 14:15], 1.0 / FIXED))
                        chained(v_.tensor_scalar(dst, dst, scal[0:P, 14:15], None, ALU.mult))
                        if v == 1:
                            chained(v_.scalar_tensor_tensor(dst, bank[:, D:2 * D], scal[0:P, 14:15], dst, ALU.mult, ALU.add))
                        v_.scalar_tensor_tensor(dst, bank[:, 0:D], scal[0:P, 14:15], dst, ALU.mult, ALU.add)\
                            .then_inc(sig("sg_ready"), 1)
                        dve.wait_ge(sig("sg_ready"), i + (GROUP + 1))
                done[0] += 4 * GROUP * GROUPS
                if v == 0:
                    dve.wait_ge(sig("dense_copied"), after("sage1_out"))
                    link(v_.tensor_tensor(wide(H3), wide(H3), over_windows(bias[0:P, 7, :]), ALU.add))
                    link(v_.tensor_scalar_max(wide(H3), wide(H3), 0.0))
                    split(wide(H3))
            dve.wait_ge(sig("x4_in"), 16)
            for g in range(GROUPS):
                dve.wait_ge(sig("dense_copied"), before("sage2_out") + g + 1)
                h_, x_ = (wide(v)[:, g * GROUP:(g + 1) * GROUP] for v in (H3, X))
                link(v_.tensor_tensor(h_, h_, bias[0:P, 8, :].unsqueeze(1).to_broadcast([P, GROUP, D]), ALU.add))
                v_.scalar_tensor_tensor(h_, h_, 0.0, x_, ALU.max, ALU.add).then_inc(sig("x4_made"), 1)

        @block.tensor
        def _(pe):
            mmul = nc.tensor.matmul

            def rounds(stage, ins, *ready):
                for name, value in ready:
                    pe.wait_ge(sig(name), value)
                if before(stage):
                    pe.wait_ge(sig("dense_copied"), before(stage))
                for g in range(dict(STAGES)[stage]):
                    n = before(stage) + g
                    if n > 1:
                        pe.wait_ge(sig("dense_copied"), n - 1)
                    for last in ins(g, mm_of(n)):
                        pass
                    last.then_inc(sig("dense_ready"), 1)

            def turn(src):
                def ins(g, mm):
                    for w in range(GROUP):
                        yield nc.tensor.transpose(mm[:, w, 0:P], src[0:P, g * GROUP + w, 0:D], ident[0:P, 0:P])
                return ins

            def project(*pairs):
                def ins(g, mm):
                    for w in range(GROUP):
                        at = (g * GROUP + w) * P
                        for i, (nodes_T, block_) in enumerate(pairs):
                            yield mmul(mm[0:P, w, :], nodes_T[:, at:at + P], wts[:, block_, :],
                                       start=i == 0, stop=i == len(pairs) - 1)
                return ins

            def columns(views, size):
                def ins(j, mm):
                    for i, v in enumerate(views):
                        yield nc.tensor.transpose(mm[:, i, 0:size], v[0:size, j, :], ident[0:size, 0:size])
                return ins

            pe.wait_ge(sig("consts_in"), 96)
            rounds("steps", columns((st_f[3], st_f[3], st_f[1], st_w), SK), ("step_rows", 1), ("tiles_in", 32 * SJ))
            rounds("counts", columns((ct_f[1], ct_f[3]), CK), ("cstep_rows", 1))

            pe.wait_ge(sig("h_made"), 1)
            pe.wait_ge(sig("windows_in"), 32)
            with pe.Fori(0, GCN_ROUNDS) as r:
                def pick(s):
                    k = r * GCN_STEPS + s
                    half, t = divmod(s, TABLES)
                    pe.wait_ge(sig("dst_hot_ready"), r * 2 + (half + 1))
                    pe.wait_ge(sig("picked_copied"), k + 1)
                    mmul(PS[:, 2 + s % 2, 0:D], dst_hot[half][0:P, t * EDGES:(t + 1) * EDGES],
                         HN[0:P, bass.ds(window[s], 1), :].rearrange("p a d -> p (a d)"), start=True, stop=True)\
                        .then_inc(sig("picked_ready"), 1)

                def add_up(s):
                    k = r * GCN_STEPS + s
                    half, t = divmod(s, TABLES)
                    pe.wait_ge(sig("same_ready"), r * 2 + (half + 1))
                    pe.wait_ge(sig("picked_copied"), k + 3)
                    pe.wait_ge(sig("rows_ready"), k + 1)
                    mmul(PS[:, 6 + s % 2, 0:D], src_row[half][:, t * EDGES:(t + 1) * EDGES], picked[:, s % 2, :],
                         start=True, stop=True).then_inc(sig("summed"), 1)

                for j in range(CNT_PER_ROUND):
                    m = r * CNT_PER_ROUND + j
                    pe.wait_ge(sig("chot_ready"), m + 1)
                    pe.wait_ge(sig("cnt_copied"), m + (1 if j else 2))
                    mmul(PS[0:P, 4 + j % 2, 0:W * Q], slohot[:, j % 2, 0:P], khot[:, j % 2, :], start=True, stop=True)\
                        .then_inc(sig("csum_ready"), 1)
                    if j == 0:
                        _, window = nc.values_load_multi_w_load_instructions(
                            IK[0:1, bass.ds(r * GCN_STEPS, GCN_STEPS)], engines=[mybir.EngineType.PE], min_val=0, max_val=W - 1,
                            skip_runtime_bounds_check_because="steps' windows lie in this range by their construction")
                    if 2 <= j < 2 + GCN_STEPS:
                        pick(j - 2)
                    if 3 <= j < 3 + GCN_STEPS:
                        add_up(j - 3)

            rounds("gcn_hT", turn(wide(H0)), ("rows_ready", STEPS + 2), ("k_out4", 16))
            rounds("gcn_aT", turn(wide(Y)), ("nb_added", TABLES - 1))
            rounds("gcn_out", project((HT, 0), (T, 1)), ("wts_in", 16 * 19))
            rounds("msg_hT", turn(wide(H)), ("h_made", 2))
            rounds("msg_P", project((HT, 2)))
            rounds("msg_Q", project((HT, 3)), ("p_out", 16))

            def first_layer(r, half):
                q = r * 2 + half
                pe.wait_ge(sig("mrhs_ready"), q + 1)
                pe.wait_ge(sig("relu_done"), q + 1)
                for s in range(HALF):
                    n = half * HALF + s
                    part = PS[:, 4, s * EDGES:(s + 1) * EDGES]
                    pe.wait_ge(gathered[n], r * 16 + 16)
                    pe.wait_ge(sig("q_copied"), r * MSG_SLOTS + (n + 1))
                    mmul(part, MG[:, n, :], ident[:, :], start=True, stop=False).then_inc(sig("msg_used"), 1)
                    last = mmul(part, Qc[0:P + 1, n, :], mrhs[half][0:P + 1, s * EDGES:(s + 1) * EDGES],
                                start=False, stop=True)
                last.then_inc(sig("pre_ready"), 1)

            def second_layer(r, half):
                pe.wait_ge(sig("relu_done"), r * 2 + (half + 2))
                pe.wait_ge(sig("scan_ready"), r * 2 + (half + 1))
                mmul(PS[:, 5, :], wts[:, 4, :], relu, start=True, stop=True).then_inc(sig("msg_ready"), 1)

            def turn_back(r, half):
                pe.wait_ge(sig("scan_ready"), r * 2 + (half + 2))
                pe.wait_ge(sig("back_copied"), r * 2 + (half + 1))
                for s in range(HALF):
                    last = nc.tensor.transpose(PS[:, 0, s * EDGES:(s + 1) * EDGES], scan[:, s * EDGES:(s + 1) * EDGES],
                                               ident[:, :])
                last.then_inc(sig("back_ready"), 1)

            def pick_last(r, half):
                pe.wait_ge(sig("back_copied"), r * 2 + (half + 2))
                for s in range(HALF):
                    n = half * HALF + s
                    pe.wait_ge(sig("last_ready"), r * MSG_SLOTS + (n + 1))
                    pe.wait_ge(sig("sums_added"), r * MSG_SLOTS + (n + 1))
                    mmul(PS[0:P, SUM_BANKS[s], 0:D + 1], lasthot[:, n, :], back[:, s, :], start=True, stop=True)\
                        .then_inc(sig("sums_ready"), 1)

            first_layer(0, 0)
            second_layer(0, 0)
            with pe.Fori(0, MSG_ROUNDS - 1) as r:
                for half, after_ in ((0, (r, 1)), (1, (r + 1, 0))):
                    first_layer(*after_)
                    turn_back(r, half)
                    second_layer(*after_)
                    pick_last(r, half)
            r = MSG_ROUNDS - 1
            first_layer(r, 1)
            turn_back(r, 0)
            second_layer(r, 1)
            pick_last(r, 0)
            turn_back(r, 1)
            pick_last(r, 1)

            def hidden(g, mm):
                for w in range(GROUP):
                    at = (g * GROUP + w) * P
                    mmul(mm[:, w, 0:P], wts[:, 5, :], HT[:, at:at + P], start=True, stop=False)
                    yield mmul(mm[:, w, 0:P], wts[:, 6, :], T[:, at:at + P], start=False, stop=True)

            rounds("msg_aT", turn(wide(H)), ("agg_made", 1))
            rounds("msg_u", hidden)
            rounds("msg_out", project((QU, 7)))
            rounds("gat_hT", turn(wide(H)), ("h_made", 3))
            rounds("gat_emb", project((HT, 0)), ("wts2_in", 16 * 5))
            rounds("gat_eT", turn(wide(Y)), ("emb_made", GROUPS))
            rounds("gat_x0", project((T, 1)))
            rounds("gat_x1", project((T, 2)))

            for u in range(3):
                pe.wait_ge(sig("max_step"), (u + 1) * 2 * (W + 1))
                for g in range(GROUPS):
                    pe.wait_ge(sig("max_reduced"), u * GROUPS + g)
                    for w in range(GROUP):
                        at = (g * GROUP + w) * P
                        last = nc.tensor.transpose(pairs_of_banks[0][0:P, w, 0:P], macc_att[0:P, at:at + P], ident[0:P, 0:P])
                    last.then_inc(sig("max_turned"), 1)
                rounds(f"rows{u}", lambda g, mm: [nc.tensor.transpose(
                    mm[0:2 * W, 0, 0:P], cols[0:P, 7:9, :].rearrange("p a w -> p (a w)"), ident[0:P, 0:P])],
                    ("ab_made", u + 1), ("max_reduced", (u + 1) * GROUPS))

                def chunk(g, b, i, first, b_round=0):
                    by_pool = i in POOL_SLOTS
                    slots = [x for x in range(GROUP) if (x in POOL_SLOTS) == by_pool]
                    q = 0 if isinstance(b, int) else b_round
                    pe.wait_ge(sig("pool_z_ready" if by_pool else "z_ready"),
                               q * len(slots) + ((u * GROUPS + g) * GROUPS * len(slots) + slots.index(i) + 1))
                    rows = xw[0:P, b, :] if isinstance(b, int) else xw[0:P, bass.ds(b, 1), :].rearrange("p a d -> p (a d)")
                    for w in range(GROUP):
                        last = mmul(PS[0:P, 3 + w, 0:D + 1], zs[0:P, i, w * P:(w + 1) * P], rows,
                                    start=first, stop=False, skip_group_check=True)
                    last.then_inc(sig("z_used"), 1)
                    return last

                if u == 1:
                    pe.wait_ge(sig("xw_in"), 16)
                for g in range(GROUPS):
                    at = u * W * GROUPS + g * W
                    pe.wait_ge(sig("outs_free"), u * GROUPS + g)
                    for i in range(GROUP):
                        chunk(g, i, i, i == 0)
                    with pe.Fori(1, GROUPS) as q:
                        for i in range(GROUP):
                            chunk(g, q * GROUP + i, i, False, q)
                    pe.wait_ge(sig("z_used"), at + W + GROUP)
                    pe.sem_inc(sig("outs_ready"), 1)
                if u == 1:
                    for n in range(2):
                        rounds(f"gat_o{n}T", turn(wide(elus[n][0])), ("elu_made", n + 1))
                    rounds("gat_x2", project((V3, 3), (V2, 4)))

            for v in range(2):
                pe.wait_ge(sig("parts_made"), v + 1)
                hs, size = (hs1, hs2)[v], PARTS[v] * D + 1
                with pe.Fori(0, GROUPS) as g:
                    for w in range(GROUP):
                        pe.wait_ge(sig("sg_ready"), g * GROUP + (v * W + w + 1))
                        for b in range(W):
                            last = mmul(PS[0:P, 3 + w, 0:size], K[0:P, b, bass.ds(g * GC + w * P, P)],
                                        hs[0:P, b, 0:size], start=b == 0, stop=b == W - 1)
                        last.then_inc(sig("sage_ready"), 1)
                name = f"sage{v + 1}"

                def means_turned(g, mm, v=v):
                    for w in range(GROUP):
                        yield nc.tensor.transpose(mm[:, w, 0:P], mean_of(v, g, w), ident[0:P, 0:P])

                rounds(f"{name}_aT", means_turned, ("sg_ready", (v + 1) * W + GROUP))
                rounds(f"{name}_hT", turn(wide(H3)))
                rounds(f"{name}_out", project((S1, 5 if v == 0 else 7), (S2, 6 if v == 0 else 0)),
                       ("wts3_in", 48), ("wts4_in", 16))


def kernel(**inputs):
    import concourse.bacc as bacc
    from concourse.bass_utils import run_bass_kernel_spmd

    g = {k: np.asarray(v) for k, v in inputs.items()}
    pad = TILES * EDGES - E
    src, dst, w = (g[k] for k in ("src", "dst", "edge_weight"))
    s_ = np.concatenate([src, np.zeros(pad, src.dtype)]).reshape(TILES, EDGES)
    d_ = np.concatenate([dst, np.full(pad, N, dst.dtype)])
    w_ = np.concatenate([w, np.zeros(pad, w.dtype)]).reshape(TILES, EDGES)
    prev = np.concatenate([np.full(1, N + 1, dst.dtype), d_[:-1]]).reshape(TILES, EDGES)
    next_ = np.concatenate([d_[1:], np.full(1, N + 1, dst.dtype)]).reshape(TILES, EDGES)
    d_ = d_.reshape(TILES, EDGES)
    block = lambda m, i, j: m[i * D:(i + 1) * D, j * D:(j + 1) * D]
    arrays = {
        "x": g["x"], "edges": np.concatenate([s_, d_, prev, next_], 1), "ends": np.concatenate([s_, d_], 1),
        "weights": w_, "last": d_[:, -1], "tiles": np.arange(TILES, dtype=np.float32),
        "pidx": np.arange(128, dtype=np.float32).reshape(128, 1), "ident": np.eye(128, dtype=np.float32),
        "earlier": np.tril(np.ones((EDGES, EDGES), np.float32), -1), "spare": N + np.arange(128, dtype=np.float32).reshape(128, 1),
        "ramp": np.tile(np.arange(128, dtype=np.float32), (128, 1)),
        "keys": np.tile(np.arange(W * Q, dtype=np.float16), (128, 1)),
        "L0_a": block(g["L0_gnn_W"], 0, 0).T, "L0_b_w": block(g["L0_gnn_W"], 0, 1).T, "L0_b": g["L0_gnn_b"],
        "L1_src": block(g["L1_gnn_W1"], 0, 0), "L1_dst": block(g["L1_gnn_W1"], 1, 0), "L1_wrow": g["L1_gnn_W1"][2 * D:],
        "L1_W2": g["L1_gnn_W2"], "L1_U1a": block(g["L1_gnn_U1"], 0, 0), "L1_U1b": block(g["L1_gnn_U1"], 1, 0),
        "L1_U2": g["L1_gnn_U2"], "L1_b1": g["L1_gnn_b1"].reshape(D, 1), "L1_c1": g["L1_gnn_c1"].reshape(D, 1),
        "L1_b2": g["L1_gnn_b2"], "L1_c2": g["L1_gnn_c2"],
        "L2_emb": g["L2_gnn_W_emb"], "L2_W1a": block(g["L2_gnn_W1"], 0, 0), "L2_W1b": block(g["L2_gnn_W1"], 0, 1),
        "L2_W2a": block(g["L2_gnn_W2"], 0, 0), "L2_W2b": block(g["L2_gnn_W2"], 1, 0), "L2_b_emb": g["L2_gnn_b_emb"],
        "L2_b1a": g["L2_gnn_b1"][:D], "L2_b1b": g["L2_gnn_b1"][D:], "L2_b2": g["L2_gnn_b2"],
        "L2_src0": g["L2_gnn_att_src1"][0], "L2_dst0": g["L2_gnn_att_dst1"][0],
        "L2_src1": g["L2_gnn_att_src1"][1], "L2_dst1": g["L2_gnn_att_dst1"][1],
        "L2_src2": g["L2_gnn_att_src2"][0], "L2_dst2": g["L2_gnn_att_dst2"][0],
        "L3_Wl1": g["L3_gnn_Wl1"], "L3_Wr1": g["L3_gnn_Wr1"], "L3_Wl2": g["L3_gnn_Wl2"], "L3_Wr2": g["L3_gnn_Wr2"],
        "L3_bl1": g["L3_gnn_bl1"], "L3_bl2": g["L3_gnn_bl2"],
    }
    arrays = {f"in_{k}": np.ascontiguousarray(v) for k, v in arrays.items()}
    nc = bacc.Bacc("TRN2", target_bir_lowering=False, num_devices=1)
    a = {k[3:]: nc.dram_tensor(k, v.shape, mybir.dt.from_np(v.dtype), kind="ExternalInput").ap() for k, v in arrays.items()}
    out = nc.dram_tensor("out", (N, D), f32, kind="ExternalOutput").ap()
    gnn(nc, a, out)
    r = run_bass_kernel_spmd(nc, [arrays], core_ids=[0])
    return r.results[0]["out"]
```
